# Optimizing a Trainium2 kernel written in Bass

```python
import numpy as np
import jax
import jax.numpy as jnp

def _softmax(x, axis=-1):
    return jax.nn.softmax(x, axis=axis)

def _gelu(x):
    return jax.nn.gelu(x, approximate=True)

def _silu(x):
    return jax.nn.silu(x)

def _sigmoid(x):
    return jax.nn.sigmoid(x)

def _layernorm(x, axis=-1, eps=1e-05):
    m = jnp.mean(x, axis=axis, keepdims=True)
    v = jnp.var(x, axis=axis, keepdims=True)
    return (x - m) / jnp.sqrt(v + eps)

def _scatter_add(tgt, idx, src, axis=0):
    return tgt.at[idx].add(src)

def _segment_sum(src, seg, n):
    return jax.ops.segment_sum(src, seg, n)
kernel_name = 'mk_audio_tower_d2_tok_audfeat256_r4_5ba2db'

def setup_inputs(seed: int=0):
    np.random.seed(seed)
    _w = jnp.asarray

    def _rec_inputs():
        import jax
        import jax.numpy as jnp
        _rk = jax.random.key(seed)
        x = jax.random.uniform(jax.random.fold_in(_rk, 1), (16, 4, 750), jnp.float32, 0.0, 0.999986)
        return x
    x = _rec_inputs()

    def _L0_tok_setup():
        import jax, jax.numpy as jnp
        import numpy as np
        T = 8
        key = jax.random.key(seed)
        ks = jax.random.split(key, 9)
        bs, dims, L, d = (16, 4, 512, 64)
        x = jax.random.uniform(ks[0], (bs, dims, L), dtype=jnp.float32)
        s_in = 1.0 / np.sqrt(dims)
        s_d = 1.0 / np.sqrt(d)
        W1 = jax.random.uniform(ks[1], (d, dims), minval=-s_in, maxval=s_in, dtype=jnp.float32)
        b1 = jax.random.uniform(ks[2], (d,), minval=-s_in, maxval=s_in, dtype=jnp.float32)
        W2 = jax.random.uniform(ks[3], (d, d), minval=-s_d, maxval=s_d, dtype=jnp.float32)
        b2 = jax.random.uniform(ks[4], (d,), minval=-s_d, maxval=s_d, dtype=jnp.float32)
        W3 = jax.random.uniform(ks[5], (d, dims), minval=-s_in, maxval=s_in, dtype=jnp.float32)
        b3 = jax.random.uniform(ks[6], (d,), minval=-s_in, maxval=s_in, dtype=jnp.float32)
        W4 = jax.random.uniform(ks[7], (d, d), minval=-s_d, maxval=s_d, dtype=jnp.float32)
        b4 = jax.random.uniform(ks[8], (d,), minval=-s_d, maxval=s_d, dtype=jnp.float32)
        return dict(x=x, W1=W1, b1=b1, W2=W2, b2=b2, W3=W3, b3=b3, W4=W4, b4=b4)
    _L0_tok_all = _L0_tok_setup()
    _L0_tok_in = {k: v for k, v in _L0_tok_all.items() if k in ('W1', 'b1', 'W2', 'b2', 'W3', 'b3', 'W4', 'b4')}
    del _L0_tok_all

    def _L0_attn_setup():
        import jax, jax.numpy as jnp
        import numpy as np
        B, N, D = (8, 512, 64)
        key = jax.random.key(seed)
        k1, k2, k3, k4 = jax.random.split(key, 4)
        s = D ** (-0.5)
        return {'x': jax.random.normal(k1, (B, N, D), dtype=jnp.float32), 'Wq': jax.random.normal(k2, (D, D), dtype=jnp.float32) * s, 'Wk': jax.random.normal(k3, (D, D), dtype=jnp.float32) * s, 'Wv': jax.random.normal(k4, (D, D), dtype=jnp.float32) * s}
    _L0_attn_all = _L0_attn_setup()
    _L0_attn_in = {k: v for k, v in _L0_attn_all.items() if k in ('Wq', 'Wk', 'Wv')}
    del _L0_attn_all

    def _L0_ffn_setup():
        import jax, jax.numpy as jnp
        import numpy as np
        B, S, H, NH, NE = (4, 256, 64, 4, 4)
        D = H // NH
        EPS = 1e-08

        def layernorm(x, g, b):
            m = jnp.mean(x, axis=-1, keepdims=True)
            v = jnp.mean((x - m) ** 2, axis=-1, keepdims=True)
            return (x - m) / jnp.sqrt(v + EPS) * g + b
        key = jax.random.key(seed)
        ks = jax.random.split(key, 18)
        sc = 0.05
        return {'x': jax.random.normal(ks[0], (B, S, H), jnp.float32), 'hl_w': jax.random.normal(ks[1], (NH, D, H), jnp.float32) * sc, 'hl_b': jax.random.normal(ks[2], (NH, D), jnp.float32) * sc, 'wq': jax.random.normal(ks[3], (NH, NE, D, D), jnp.float32) * sc, 'wk': jax.random.normal(ks[4], (NH, D, D), jnp.float32) * sc, 'wv': jax.random.normal(ks[5], (NH, D, D), jnp.float32) * sc, 'gate_w': jax.random.normal(ks[6], (NH, NE, NE * D), jnp.float32) * sc, 'gate_b': jax.random.normal(ks[7], (NH, NE), jnp.float32) * sc, 'ln_g': jnp.ones((D,), jnp.float32), 'ln_b': jnp.zeros((D,), jnp.float32), 'fc1_w': jax.random.normal(ks[8], (D, D), jnp.float32) * sc, 'fc1_b': jax.random.normal(ks[9], (D,), jnp.float32) * sc, 'fc2_w': jax.random.normal(ks[10], (D, D), jnp.float32) * sc, 'fc2_b': jax.random.normal(ks[11], (D,), jnp.float32) * sc, 'fnorm_g': jnp.ones((D,), jnp.float32), 'fnorm_b': jnp.zeros((D,), jnp.float32), 'fgate_w': jax.random.normal(ks[12], (NH, H), jnp.float32) * sc}
    _L0_ffn_all = _L0_ffn_setup()
    _L0_ffn_in = {k: v for k, v in _L0_ffn_all.items() if k in ('hl_w', 'hl_b', 'wq', 'wk', 'wv', 'gate_w', 'gate_b', 'ln_g', 'ln_b', 'fc1_w', 'fc1_b', 'fc2_w', 'fc2_b', 'fnorm_g', 'fnorm_b', 'fgate_w')}
    del _L0_ffn_all

    def _L1_attn_setup():
        import jax, jax.numpy as jnp
        import numpy as np
        D = 64
        L = 2
        B, S = (8, 1024)
        LR = 0.001
        WD = 0.01
        MAX_ALR = 0.1
        EPS = 1e-08

        def _lmm(Ws, bs, x):
            for i in range(L):
                x = x + jax.nn.silu(x @ Ws[i] + bs[i])
            return x

        def _reference_tuple_inner(x, Wk, Wq, Wv, Wlr, blr, Ws, bs):
            keys = x @ Wk
            queries = x @ Wq
            values = x @ Wv
            alr = (jax.nn.sigmoid(x @ Wlr + blr) * MAX_ALR).reshape(-1)

            def loss_fn(params):
                Ws_, bs_ = params
                preds = _lmm(Ws_, bs_, keys).reshape(-1, D)
                tgt = values.reshape(-1, D)
                per_tok = jnp.mean((preds - tgt) ** 2, axis=-1)
                return jnp.sum(per_tok * alr)
            gWs, gbs = jax.grad(loss_fn)((Ws, bs))

            def adamw_step(p, g):
                return p * (1.0 - LR * WD) - LR * g / (jnp.sqrt(g * g) + EPS)
            nWs = adamw_step(Ws, gWs)
            nbs = adamw_step(bs, gbs)
            retrieved = _lmm(nWs, nbs, queries)
            return (retrieved, -gWs, -gbs)
        key = jax.random.key(seed)
        ks = jax.random.split(key, 9)
        scale = 0.05
        return {'x': jax.random.normal(ks[0], (B, S, D), dtype=jnp.float32), 'Wk': jax.random.normal(ks[1], (D, D), dtype=jnp.float32) * scale, 'Wq': jax.random.normal(ks[2], (D, D), dtype=jnp.float32) * scale, 'Wv': jax.random.normal(ks[3], (D, D), dtype=jnp.float32) * scale, 'Wlr': jax.random.normal(ks[4], (D, 1), dtype=jnp.float32) * scale, 'blr': jnp.zeros((1,), dtype=jnp.float32), 'Ws': jax.random.normal(ks[5], (L, D, D), dtype=jnp.float32) * scale, 'bs': jnp.zeros((L, D), dtype=jnp.float32)}
    _L1_attn_all = _L1_attn_setup()
    _L1_attn_in = {k: v for k, v in _L1_attn_all.items() if k in ('Wk', 'Wq', 'Wv', 'Wlr', 'blr', 'Ws', 'bs')}
    del _L1_attn_all

    def _L1_ffn_setup():
        import jax, jax.numpy as jnp
        import numpy as np
        DIM = 64
        HEADS = 8
        NUM_KEYS = 64
        NUM_KV = NUM_KEYS ** 2
        PK_TOPK = 16
        FINAL_TOPK = 16
        DIM_KEY = DIM // 2
        P = 2

        def _pk(x, Wq_pk, pk_keys):
            b, n, _ = x.shape
            q = (x @ Wq_pk).reshape(b, n, P, HEADS, DIM_KEY).transpose(2, 0, 1, 3, 4)
            sim = jnp.einsum('pbnhd,pkhd->pbnhk', q, pk_keys)
            scores, idx = jax.lax.top_k(sim, PK_TOPK)
            idx0 = idx[0]
            idx1 = idx[1] * NUM_KEYS
            index = (idx0[..., :, None] + idx1[..., None, :]).reshape(b, n, HEADS, PK_TOPK * PK_TOPK)
            score = (scores[0][..., :, None] + scores[1][..., None, :]).reshape(b, n, HEADS, PK_TOPK * PK_TOPK)
            final_scores, pk_idx = jax.lax.top_k(score, FINAL_TOPK)
            final_indices = jnp.take_along_axis(index, pk_idx, axis=-1)
            final_scores = jax.nn.softmax(final_scores, axis=-1)
            return (final_scores, final_indices)
        key = jax.random.key(seed)
        ks = jax.random.split(key, 7)
        b, n = (2, 256)
        std = 0.02
        x = jax.random.normal(ks[0], (b, n, DIM), dtype=jnp.float32)
        Wq_pk = jax.random.normal(ks[1], (DIM, P * HEADS * DIM_KEY), dtype=jnp.float32) * std
        pk_keys = jax.random.normal(ks[2], (P, NUM_KEYS, HEADS, DIM_KEY), dtype=jnp.float32) * std
        Wq = jax.random.normal(ks[3], (DIM, HEADS * DIM), dtype=jnp.float32) * std
        keys_table = jax.random.normal(ks[4], (NUM_KV * HEADS, DIM), dtype=jnp.float32) * std
        values_table = jax.random.normal(ks[5], (NUM_KV * HEADS, DIM), dtype=jnp.float32) * std
        Wo = jax.random.normal(ks[6], (DIM * HEADS, DIM), dtype=jnp.float32) * std
        return {'x': x, 'Wq_pk': Wq_pk, 'pk_keys': pk_keys, 'Wq': Wq, 'keys_table': keys_table, 'values_table': values_table, 'Wo': Wo}
    _L1_ffn_all = _L1_ffn_setup()
    _L1_ffn_in = {k: v for k, v in _L1_ffn_all.items() if k in ('Wq_pk', 'pk_keys', 'Wq', 'keys_table', 'values_table', 'Wo')}
    del _L1_ffn_all
    return {'x': x, 'L0_tok_W1': _L0_tok_in['W1'], 'L0_tok_b1': _L0_tok_in['b1'], 'L0_tok_W2': _L0_tok_in['W2'], 'L0_tok_b2': _L0_tok_in['b2'], 'L0_tok_W3': _L0_tok_in['W3'], 'L0_tok_b3': _L0_tok_in['b3'], 'L0_tok_W4': _L0_tok_in['W4'], 'L0_tok_b4': _L0_tok_in['b4'], 'L0_attn_Wq': _L0_attn_in['Wq'], 'L0_attn_Wk': _L0_attn_in['Wk'], 'L0_attn_Wv': _L0_attn_in['Wv'], 'L0_ffn_hl_w': _L0_ffn_in['hl_w'], 'L0_ffn_hl_b': _L0_ffn_in['hl_b'], 'L0_ffn_wq': _L0_ffn_in['wq'], 'L0_ffn_wk': _L0_ffn_in['wk'], 'L0_ffn_wv': _L0_ffn_in['wv'], 'L0_ffn_gate_w': _L0_ffn_in['gate_w'], 'L0_ffn_gate_b': _L0_ffn_in['gate_b'], 'L0_ffn_ln_g': _L0_ffn_in['ln_g'], 'L0_ffn_ln_b': _L0_ffn_in['ln_b'], 'L0_ffn_fc1_w': _L0_ffn_in['fc1_w'], 'L0_ffn_fc1_b': _L0_ffn_in['fc1_b'], 'L0_ffn_fc2_w': _L0_ffn_in['fc2_w'], 'L0_ffn_fc2_b': _L0_ffn_in['fc2_b'], 'L0_ffn_fnorm_g': _L0_ffn_in['fnorm_g'], 'L0_ffn_fnorm_b': _L0_ffn_in['fnorm_b'], 'L0_ffn_fgate_w': _L0_ffn_in['fgate_w'], 'L1_attn_Wk': _L1_attn_in['Wk'], 'L1_attn_Wq': _L1_attn_in['Wq'], 'L1_attn_Wv': _L1_attn_in['Wv'], 'L1_attn_Wlr': _L1_attn_in['Wlr'], 'L1_attn_blr': _L1_attn_in['blr'], 'L1_attn_Ws': _L1_attn_in['Ws'], 'L1_attn_bs': _L1_attn_in['bs'], 'L1_ffn_Wq_pk': _L1_ffn_in['Wq_pk'], 'L1_ffn_pk_keys': _L1_ffn_in['pk_keys'], 'L1_ffn_Wq': _L1_ffn_in['Wq'], 'L1_ffn_keys_table': _L1_ffn_in['keys_table'], 'L1_ffn_values_table': _L1_ffn_in['values_table'], 'L1_ffn_Wo': _L1_ffn_in['Wo']}

def reference(x, L0_tok_W1, L0_tok_b1, L0_tok_W2, L0_tok_b2, L0_tok_W3, L0_tok_b3, L0_tok_W4, L0_tok_b4, L0_attn_Wq, L0_attn_Wk, L0_attn_Wv, L0_ffn_hl_w, L0_ffn_hl_b, L0_ffn_wq, L0_ffn_wk, L0_ffn_wv, L0_ffn_gate_w, L0_ffn_gate_b, L0_ffn_ln_g, L0_ffn_ln_b, L0_ffn_fc1_w, L0_ffn_fc1_b, L0_ffn_fc2_w, L0_ffn_fc2_b, L0_ffn_fnorm_g, L0_ffn_fnorm_b, L0_ffn_fgate_w, L1_attn_Wk, L1_attn_Wq, L1_attn_Wv, L1_attn_Wlr, L1_attn_blr, L1_attn_Ws, L1_attn_bs, L1_ffn_Wq_pk, L1_ffn_pk_keys, L1_ffn_Wq, L1_ffn_keys_table, L1_ffn_values_table, L1_ffn_Wo):
    import jax
    import jax.numpy as jnp

    def _L0_tok_ref(x, W1, b1, W2, b2, W3, b3, W4, b4):
        import jax, jax.numpy as jnp
        import numpy as np
        T = 8
        a = jnp.einsum('bdl,od->blo', x, W1) + b1
        bs, L, d = a.shape
        zcol = jnp.zeros((bs, 1, d), a.dtype)
        shift_r = lambda v: jnp.concatenate([zcol, v[:, :-1]], axis=1)
        shift_l = lambda v: jnp.concatenate([v[:, 1:], zcol], axis=1)
        up = jnp.zeros_like(a)
        down = jnp.zeros_like(a)
        for _ in range(T):
            up = jax.nn.relu(a + shift_r(up) @ W2.T + b2)
            down = jax.nn.relu(a + shift_l(down) @ W2.T + b2)
        c = jnp.einsum('bdl,od->blo', x, W3) + b3
        miu = jax.nn.relu(c + (shift_r(up) @ W4.T + b4) + (shift_l(down) @ W4.T + b4))
        return miu

    def _L0_attn_ref(x, Wq, Wk, Wv):
        import jax, jax.numpy as jnp
        import numpy as np
        B, N, D = (8, 512, 64)
        q = jnp.einsum('bnd,ed->bne', x, Wq)
        k = jnp.einsum('bnd,ed->bne', x, Wk)
        v = jnp.einsum('bnd,ed->bne', x, Wv)
        energy = jnp.einsum('bqd,bkd->bqk', q, k)
        scaling = jnp.asarray(x.shape[-1] ** (-0.5), x.dtype)
        att = jax.nn.softmax(energy, axis=-1) * scaling
        out = jnp.einsum('bqk,bkv->bqv', att, v)
        return out

    def _L0_ffn_ref(x, hl_w, hl_b, wq, wk, wv, gate_w, gate_b, ln_g, ln_b, fc1_w, fc1_b, fc2_w, fc2_b, fnorm_g, fnorm_b, fgate_w):
        import jax, jax.numpy as jnp
        import numpy as np
        B, S, H, NH, NE = (4, 256, 64, 4, 4)
        D = H // NH
        EPS = 1e-08

        def layernorm(x, g, b):
            m = jnp.mean(x, axis=-1, keepdims=True)
            v = jnp.mean((x - m) ** 2, axis=-1, keepdims=True)
            return (x - m) / jnp.sqrt(v + EPS) * g + b
        b, s, h = x.shape
        nh, d, _ = wk.shape
        ne = wq.shape[1]
        sx = jnp.einsum('bsh,ndh->bnsd', x, hl_w) + hl_b[None, :, None, :]
        pad = sx == 0
        q = jnp.einsum('bnsd,neod->bneso', sx, wq)
        k = jnp.einsum('bnsd,nod->bnso', sx, wk)
        v = jnp.einsum('bnsd,nod->bnso', sx, wv)
        causal = jnp.where(jnp.tril(jnp.ones((s, s), bool)), 0.0, -jnp.inf).astype(x.dtype)
        scores = jnp.einsum('bnesd,bntd->bnest', q, k) * d ** 0.5 + causal
        att = jax.nn.softmax(scores, axis=-1)
        qkv = jnp.einsum('bnest,bntd->bnesd', att, v)
        qkv = jnp.where(pad[:, :, None], 0.0, qkv)
        out = jnp.transpose(qkv, (0, 1, 3, 2, 4)).reshape(b, nh, s, ne * d)
        gs = jax.nn.softmax(jnp.einsum('bnsf,nef->bnse', out, gate_w) + gate_b[None, :, None, :], axis=-1)
        mixed = jnp.einsum('bnsed,bnse->bnsd', out.reshape(b, nh, s, ne, d), gs)
        resid = sx[jnp.arange(nh), jnp.arange(nh)]
        hn = layernorm(mixed + resid, ln_g, ln_b)
        f_n = jnp.transpose(hn, (0, 2, 1, 3)).reshape(b, s, h)
        fx = f_n.reshape(b, s, nh, d)
        pm = fx == 0
        hx = jnp.where(pm, 0.0, fx @ fc1_w.T + fc1_b)
        hx = jax.nn.relu(hx)
        hx = jnp.where(pm, 0.0, hx @ fc2_w.T + fc2_b)
        hx = layernorm(hx + fx, fnorm_g, fnorm_b)
        fout = hx.reshape(b, s, h)
        fg = jax.nn.softmax(fout @ fgate_w.T, axis=-1)
        return (fout.reshape(b, s, nh, d) * fg[..., None]).reshape(b, s, h)

    def _L1_attn_ref(x, Wk, Wq, Wv, Wlr, blr, Ws, bs):
        import jax, jax.numpy as jnp
        import numpy as np
        D = 64
        L = 2
        B, S = (8, 1024)
        LR = 0.001
        WD = 0.01
        MAX_ALR = 0.1
        EPS = 1e-08

        def _lmm(Ws, bs, x):
            for i in range(L):
                x = x + jax.nn.silu(x @ Ws[i] + bs[i])
            return x

        def _reference_tuple_inner(x, Wk, Wq, Wv, Wlr, blr, Ws, bs):
            keys = x @ Wk
            queries = x @ Wq
            values = x @ Wv
            alr = (jax.nn.sigmoid(x @ Wlr + blr) * MAX_ALR).reshape(-1)

            def loss_fn(params):
                Ws_, bs_ = params
                preds = _lmm(Ws_, bs_, keys).reshape(-1, D)
                tgt = values.reshape(-1, D)
                per_tok = jnp.mean((preds - tgt) ** 2, axis=-1)
                return jnp.sum(per_tok * alr)
            gWs, gbs = jax.grad(loss_fn)((Ws, bs))

            def adamw_step(p, g):
                return p * (1.0 - LR * WD) - LR * g / (jnp.sqrt(g * g) + EPS)
            nWs = adamw_step(Ws, gWs)
            nbs = adamw_step(bs, gbs)
            retrieved = _lmm(nWs, nbs, queries)
            return (retrieved, -gWs, -gbs)
        return _reference_tuple_inner(x, Wk, Wq, Wv, Wlr, blr, Ws, bs)[0]

    def _L1_ffn_ref(x, Wq_pk, pk_keys, Wq, keys_table, values_table, Wo):
        import jax, jax.numpy as jnp
        import numpy as np
        DIM = 64
        HEADS = 8
        NUM_KEYS = 64
        NUM_KV = NUM_KEYS ** 2
        PK_TOPK = 16
        FINAL_TOPK = 16
        DIM_KEY = DIM // 2
        P = 2

        def _pk(x, Wq_pk, pk_keys):
            b, n, _ = x.shape
            q = (x @ Wq_pk).reshape(b, n, P, HEADS, DIM_KEY).transpose(2, 0, 1, 3, 4)
            sim = jnp.einsum('pbnhd,pkhd->pbnhk', q, pk_keys)
            scores, idx = jax.lax.top_k(sim, PK_TOPK)
            idx0 = idx[0]
            idx1 = idx[1] * NUM_KEYS
            index = (idx0[..., :, None] + idx1[..., None, :]).reshape(b, n, HEADS, PK_TOPK * PK_TOPK)
            score = (scores[0][..., :, None] + scores[1][..., None, :]).reshape(b, n, HEADS, PK_TOPK * PK_TOPK)
            final_scores, pk_idx = jax.lax.top_k(score, FINAL_TOPK)
            final_indices = jnp.take_along_axis(index, pk_idx, axis=-1)
            final_scores = jax.nn.softmax(final_scores, axis=-1)
            return (final_scores, final_indices)
        b, n, d = x.shape
        q = (x @ Wq).reshape(b, n, HEADS, DIM) * DIM ** (-0.5)
        kv_scores, indices = _pk(x, Wq_pk, pk_keys)
        offsets = jnp.arange(HEADS, dtype=indices.dtype) * NUM_KV
        ind = indices + offsets[None, None, :, None]
        k = jnp.einsum('bnhk,bnhkd->bnhd', kv_scores, keys_table[ind])
        v = jnp.einsum('bnhk,bnhkd->bnhd', kv_scores, values_table[ind])
        sim = jnp.einsum('bihd,bjhd->bhij', q, k)
        neg = -jnp.finfo(sim.dtype).max
        causal = jnp.tril(jnp.ones((n, n), dtype=bool))
        sim = jnp.where(causal, sim, neg)
        attn = jax.nn.softmax(sim, axis=-1)
        out = jnp.einsum('bhij,bjhd->bhid', attn, v)
        out = out.transpose(0, 2, 1, 3).reshape(b, n, HEADS * DIM)
        return out @ Wo
    h = _L0_tok_ref(x, L0_tok_W1, L0_tok_b1, L0_tok_W2, L0_tok_b2, L0_tok_W3, L0_tok_b3, L0_tok_W4, L0_tok_b4)
    h = h + _L0_attn_ref(_layernorm(h, axis=-1), L0_attn_Wq, L0_attn_Wk, L0_attn_Wv)
    h = h + _L0_ffn_ref(_layernorm(h, axis=-1), L0_ffn_hl_w, L0_ffn_hl_b, L0_ffn_wq, L0_ffn_wk, L0_ffn_wv, L0_ffn_gate_w, L0_ffn_gate_b, L0_ffn_ln_g, L0_ffn_ln_b, L0_ffn_fc1_w, L0_ffn_fc1_b, L0_ffn_fc2_w, L0_ffn_fc2_b, L0_ffn_fnorm_g, L0_ffn_fnorm_b, L0_ffn_fgate_w)
    h = h + _L1_attn_ref(_layernorm(h, axis=-1), L1_attn_Wk, L1_attn_Wq, L1_attn_Wv, L1_attn_Wlr, L1_attn_blr, L1_attn_Ws, L1_attn_bs)
    h = h + _L1_ffn_ref(_layernorm(h, axis=-1), L1_ffn_Wq_pk, L1_ffn_pk_keys, L1_ffn_Wq, L1_ffn_keys_table, L1_ffn_values_table, L1_ffn_Wo)
    return h

_drawn_inputs = setup_inputs


def setup_inputs(seed=0):
    import zlib

    import numpy as np

    out = dict(_drawn_inputs(seed))
    spreads = {'L0_ffn_ln_g': (1.0, 0.2),
     'L0_ffn_ln_b': (0.0, 0.1),
     'L0_ffn_fnorm_g': (1.0, 0.2),
     'L0_ffn_fnorm_b': (0.0, 0.1),
     'L1_attn_bs': (0.0, 0.1)}
    factors = {'L0_ffn_wq': 8.0,
     'L0_ffn_wk': 24.741,
     'L0_ffn_gate_w': 64.0,
     'L0_ffn_gate_b': 64.0,
     'L0_ffn_fc1_w': 5.219,
     'L0_ffn_fc1_b': 8.0,
     'L0_ffn_fc2_w': 3.597,
     'L1_attn_Wk': 64.0,
     'L1_attn_Wv': 64.0,
     'L1_attn_Wlr': 64.0,
     'L1_ffn_Wq_pk': 8.0,
     'L1_ffn_pk_keys': 8.0,
     'L1_ffn_Wq': 64.0,
     'L1_ffn_keys_table': 64.0,
     'L1_ffn_values_table': 8.0,
     'L1_ffn_Wo': 8.0}
    for name, (base, spread) in spreads.items():
        noise = np.random.default_rng([zlib.crc32(name.encode()), seed]).standard_normal(out[name].shape)
        drawn = base * np.exp(spread * noise) if base else spread * noise
        out[name] = jnp.asarray(drawn.astype(out[name].dtype))
    for name, factor in factors.items():
        out[name] = (out[name] * factor).astype(out[name].dtype)
    return out
```

```python
import concourse.bass as bass
from concourse import mybir
from contextlib import ExitStack

FP = mybir.dt.float32
BF = mybir.dt.bfloat16
U32 = mybir.dt.uint32
ALU = mybir.AluOpType
ACT = mybir.ActivationFunctionType
AXX = mybir.AxisListType.X

B, CH, L, D = 16, 4, 750, 64
TP, NT = 125, 6
HALF = L // 2
STEPS = 8
NH, NE, HD = 4, 4, 16
PH, PKEYS, PDK, TOPK = 8, 64, 32, 16
ROWS = PH * PKEYS * PKEYS
NEG = -3.0e38
RUNS = [(0, 1, 16), (1, 1, 8), (2, 1, 5), (3, 1, 4), (4, 1, 3), (5, 3, 2), (8, 8, 1)]
NC_ = sum(n * m for _, n, m in RUNS)


PASSED = {}


def wait_apart(eng, semaphore, value):
    eng.wait_ge(semaphore, value)
    eng.sem_inc(PASSED[eng.engine], 1)


def bcast(ap, n):
    return ap.unsqueeze(2).to_broadcast([ap.shape[0], ap.shape[1], n])


def row(ap, i):
    return ap[bass.ds(i, 1), :, :].rearrange("a p n -> (a p) n")


def tokens(ap, b):
    return ap.rearrange("b (t p) d -> b p t d", p=TP)[bass.ds(b, 1), :, :, :].rearrange("a p t d -> (a p) t d")



def layernorm(nc, dve, k, src, dst, groups, width, eps, wait_rstd, done, scale=None, shift=None):
    dev, sq = k.ln_dev[0:TP, 0:groups * width].rearrange("p (g w) -> p g w", w=width), \
        k.ln_sq[0:TP, 0:groups * width].rearrange("p (g w) -> p g w", w=width)
    mean, var, rstd = k.ln_mean[0:TP, 0:groups], k.ln_var[0:TP, 0:groups], k.ln_rstd[0:TP, 0:groups]
    nc.vector.reduce_sum(mean, src, AXX)
    dve.drain()
    nc.vector.tensor_scalar_mul(mean, mean, 1.0 / width)
    dve.drain()
    nc.vector.tensor_tensor(dev, src, bcast(mean, width), ALU.subtract)
    dve.drain()
    nc.vector.tensor_tensor(sq, dev, dev, ALU.mult)
    dve.drain()
    nc.vector.reduce_sum(var, sq, AXX)
    dve.drain()
    nc.vector.tensor_scalar(var, var, 1.0 / width, eps, ALU.mult, ALU.add).then_inc(k.var_ready, 1)
    wait_rstd()
    if scale is None:
        nc.vector.tensor_tensor(dst, dev, bcast(rstd, width), ALU.mult).then_inc(done, 1)
    else:
        nc.vector.tensor_tensor(dev, dev, bcast(rstd, width), ALU.mult)
        dve.drain()
        nc.vector.tensor_tensor(dev, dev, scale[0:TP, :].unsqueeze(1).to_broadcast([TP, groups, width]), ALU.mult)
        dve.drain()
        nc.vector.tensor_tensor(dst, dev, shift[0:TP, :].unsqueeze(1).to_broadcast([TP, groups, width]), ALU.add)\
            .then_inc(done, 1)
    dve.drain()


def rsqrt(nc, pool, k, groups, n):
    pool.wait_ge(k.var_ready, n)
    nc.gpsimd.tensor_tensor(k.ln_rstd[0:TP, 0:groups], k.ln_var[0:TP, 0:groups],
                            k.minus_half[0:TP, 0:1].to_broadcast([TP, groups]), ALU.pow).then_inc(k.rstd_ready, 1)



class Attention:

    def __init__(self, nc, k, sem, name, units):
        self.nc, self.k, self.units = nc, k, units
        self.n = len(units)
        self.nb_second = [sum(u.nb > 3 for u in units[:m]) for m in range(len(units) + 1)]
        self.scores_ready = sem(name + "_scores_ready")
        self.max_ready = sem(name + "_max_ready")
        self.probs_ready = sem(name + "_probs_ready")
        self.first_turned = sem(name + "_first_turned")
        self.second_turned = sem(name + "_second_turned")
        self.first_copied = sem(name + "_first_copied")
        self.second_copied = sem(name + "_second_copied")
        self.out_ready = sem(name + "_out_ready")

    def tensor(self, pe, it, m):
        nc, k, N, units = self.nc, self.k, self.n, self.units
        base = it * N
        if m < N:
            u = units[m]
            if m >= 2:
                pe.wait_ge(self.probs_ready, base + m - 1)
            w = u.nb * TP
            parts = [(0, min(w, 375))] + ([(375, w)] if w > 375 else [])
            for h, (lo, hi) in enumerate(parts):
                diag = u.masked and hi == w
                last = nc.tensor.matmul(k.S[m % 2][0:TP, h, 0:hi - lo], u.q, u.keys[:, lo:hi],
                                        start=True, stop=not diag)
                if diag:
                    last = nc.tensor.matmul(k.S[m % 2][0:TP, h, hi - lo - TP:hi - lo], k.ident_bf[0:TP, 0:TP],
                                            k.causal[0:TP, :], start=False, stop=True)
            last.then_inc(self.scores_ready, 1)
        if 1 <= m <= N:
            n = m - 1
            u = units[n]
            pe.wait_ge(self.probs_ready, base + n + 1)
            if n >= 1:
                pe.wait_ge(self.first_copied, base + n)
            for b in range(min(3, u.nb)):
                last = nc.tensor.transpose(k.T[0:TP, 0, b * TP:(b + 1) * TP], k.P[n % 2][:, b * TP:(b + 1) * TP],
                                           k.ident[0:TP, 0:TP])
            last.then_inc(self.first_turned, 1)
            if u.nb > 3:
                if n >= 1:
                    pe.wait_ge(self.second_copied, it * self.nb_second[N] + self.nb_second[n])
                for b in range(3, u.nb):
                    last = nc.tensor.transpose(k.T[0:TP, 1, (b - 3) * TP:(b - 2) * TP],
                                               k.P[n % 2][:, b * TP:(b + 1) * TP], k.ident[0:TP, 0:TP])
                last.then_inc(self.second_turned, 1)
        if 2 <= m:
            n = m - 2
            u = units[n]
            pe.wait_ge(self.first_copied, base + n + 1)
            if u.nb > 3:
                pe.wait_ge(self.second_copied, it * self.nb_second[N] + self.nb_second[n + 1])
            for b in range(u.nb):
                last = nc.tensor.matmul(u.out, k.PT[n % 2][:, b * TP:(b + 1) * TP], u.value(b),
                                        start=b == 0, stop=b == u.nb - 1)
            last.then_inc(self.out_ready, 1)

    def vector(self, dve, it, m):
        nc, k, N = self.nc, self.k, self.n
        if m < N:
            u = self.units[m]
            dve.wait_ge(self.scores_ready, it * N + m + 1)
            w = u.nb * TP
            src = k.S[m % 2][0:TP, 0, 0:w] if w <= 375 else \
                (k.S[m % 2][0:TP, :, 0:w // 2] if w == 750 else None)
            if src is not None:
                nc.vector.tensor_reduce(k.nmax[:, m:m + 1], src, AXX if w <= 375 else mybir.AxisListType.XY,
                                        ALU.max, negate=True).then_inc(self.max_ready, 1)
            else:
                nc.vector.reduce_max(k.mtmp[:, 2 * m:2 * m + 1], k.S[m % 2][0:TP, 0, 0:375], AXX)
                nc.vector.reduce_max(k.mtmp[:, 2 * m + 1:2 * m + 2], k.S[m % 2][0:TP, 1, 0:w - 375], AXX)
                dve.drain()
                nc.vector.tensor_reduce(k.nmax[:, m:m + 1], k.mtmp[:, 2 * m:2 * m + 2], AXX, ALU.max,
                                        negate=True).then_inc(self.max_ready, 1)
        if 1 <= m <= N and self.units[m - 1].nb > 3:
            n = m - 1
            u = self.units[n]
            if n >= 2:
                dve.wait_ge(self.out_ready, it * N + n - 1)
            dve.wait_ge(self.second_turned, it * self.nb_second[N] + self.nb_second[m])
            w = (u.nb - 3) * TP
            nc.vector.tensor_copy(k.PT[n % 2][:, 375:375 + w], k.T[0:TP, 1, 0:w]).then_inc(self.second_copied, 1)

    def scalar(self, act, it, m):
        nc, k, N = self.nc, self.k, self.n
        if m < N:
            u = self.units[m]
            act.wait_ge(self.max_ready, it * N + m + 1)
            if m >= 2:
                act.wait_ge(self.first_turned, it * N + m - 1)
                if self.units[m - 2].nb > 3:
                    act.wait_ge(self.second_turned, it * self.nb_second[N] + self.nb_second[m - 1])
            w = u.nb * TP
            if w <= 375:
                nc.scalar.activation(k.P[m % 2][:, 0:w], k.S[m % 2][0:TP, 0, 0:w], ACT.Exp, bias=k.nmax[:, m:m + 1],
                                     accum_out=k.rsum[:, m:m + 1]).then_inc(self.probs_ready, 1)
            elif w == 750:
                nc.scalar.activation(k.P[m % 2][:, :].rearrange("p (h w) -> p h w", h=2), k.S[m % 2][0:TP, :, 0:375],
                                     ACT.Exp, bias=k.nmax[:, m:m + 1],
                                     accum_out=k.rsum[:, m:m + 1]).then_inc(self.probs_ready, 1)
            else:
                nc.scalar.activation(k.P[m % 2][:, 0:375], k.S[m % 2][0:TP, 0, 0:375], ACT.Exp,
                                     bias=k.nmax[:, m:m + 1], accum_out=k.rsum[:, m:m + 1])
                nc.scalar.activation(k.P[m % 2][:, 375:w], k.S[m % 2][0:TP, 1, 0:w - 375], ACT.Exp,
                                     bias=k.nmax[:, m:m + 1],
                                     accum_out=k.rsum2[:, m:m + 1]).then_inc(self.probs_ready, 1)
        if 1 <= m <= N:
            n = m - 1
            u = self.units[n]
            if n >= 2:
                act.wait_ge(self.out_ready, it * N + n - 1)
            act.wait_ge(self.first_turned, it * N + m)
            w = min(3, u.nb) * TP
            nc.scalar.activation(k.PT[n % 2][:, 0:w], k.T[0:TP, 0, 0:w], ACT.Copy).then_inc(self.first_copied, 1)


class unit:

    def __init__(self, nb, q, keys, value, out, masked):
        self.nb, self.q, self.keys, self.value, self.out, self.masked = nb, q, keys, value, out, masked


def inverse_sums(nc, dve, k, lo, hi, split):
    if split:
        nc.vector.tensor_tensor(k.rinv[:, lo:hi], k.rsum[:, lo:hi], k.rsum2[:, lo:hi], ALU.add)
        dve.drain()
        nc.vector.reciprocal(k.rinv[:, lo:hi], k.rinv[:, lo:hi])
    else:
        nc.vector.reciprocal(k.rinv[:, lo:hi], k.rsum[:, lo:hi])
    dve.drain()



def clear(nc, k):
    with nc.Block() as block:
        @block.gpsimd
        def _(pool):
            nc.gpsimd.memset(k.minus_half[:, :], -0.5)
            nc.gpsimd.memset(k.plus_half[:, :], 0.5)
            nc.gpsimd.memset(k.ident[:, :], 0.0)
            nc.gpsimd.memset(k.ident_bf[:, :], 0.0)
            nc.gpsimd.memset(k.causal[:, :], 0.0)
            pool.drain()
            for m in (k.ident, k.ident_bf):
                nc.gpsimd.affine_select(out=m[:, :], in_=m[:, :], compare_op=ALU.not_equal, fill=1.0,
                                        base=0, pattern=[[-1, 128]], channel_multiplier=1)
            nc.gpsimd.affine_select(out=k.causal[:, :], in_=k.causal[:, :], compare_op=ALU.is_ge, fill=NEG,
                                    base=0, pattern=[[-1, TP]], channel_multiplier=1)
            nc.gpsimd.iota(k.place_i[:, :], pattern=[[1, NC_]], base=0, channel_multiplier=0)
            nc.gpsimd.memset(k.xs[:, :], 1.0)

        @block.vector
        def _(dve):
            for t in (k.W2BD, k.WX, k.R3, k.HLP, k.WVB, k.GW, k.FC1, k.FC2, k.R2, k.WB, k.rsum2, k.wqb, k.wkb, k.BD,
                      k.U[0], k.U[1], k.UR, k.grads):
                nc.vector.memset(t[:], 0.0)
            nc.vector.memset(k.ones[:, :], 1.0)
            nc.vector.memset(k.xT[64:65, :], 1.0)
            nc.vector.memset(k.xT2[64:65, :], 1.0)
            nc.vector.memset(k.xT3[64:65, :], 1.0)
            nc.vector.memset(k.x1[:, :, 64:65], 1.0)
            dve.drain()
            nc.vector.memset(k.R2[64:65, 64:65], 1.0)


def load_weights(nc, k, A, sem):
    done = sem("weights_loaded")
    qkv = [
        (k.WX[0:4, 0:64], A["W1T"]), (k.WX[4:8, 64:128], A["W1T"]),
        (k.R3[0:4, :], A["W3T"]), (k.R3[8:9, :], A["b3"]), (k.R3[9:10, :], A["b4"]), (k.R3[10:11, :], A["b4"]),
        (k.W2BD[0:64, 0:64], A["W2T"]), (k.W2BD[64:128, 64:128], A["W2T"]),
        (k.W4[0:64, :], A["W4T"]), (k.W4[64:128, :], A["W4T"]),
        (k.WqN[:, :], A["attn_Wq"]), (k.WkN[:, :], A["attn_Wk"]), (k.WvT[:, :], A["attn_WvT"]),
        (k.HLT[0:64, :], A["hlT"]), (k.HLT[64:65, :], A["hl_b"]),
        (k.GW[0:64, 0, 0:4], A["gwT"][0]), (k.GW[64:128, 0, 4:8], A["gwT"][1]),
        (k.GW[0:64, 1, 8:12], A["gwT"][2]), (k.GW[64:128, 1, 12:16], A["gwT"][3]),
        (k.GB[:, :], A["gb"]), (k.FG[:, :], A["fgT"]),
        (k.R2[0:64, 0:64], A["Wk1"]), (k.R2[0:64, 129:193], A["Wv1"]), (k.R2[0:64, 193:194], A["Wlr"]),
        (k.R2[64:65, 193:194], A["blr"]),
        (k.WB[0:64, 0:64], A["Ws"][0]), (k.WB[0:64, 64:128], A["Ws"][1]),
        (k.WB[64:65, :], A["bs"]), (k.W1Tr[:, :], A["Ws1T"]), (k.WkT1[:, :], A["WkT1"]), (k.WqT1[:, :], A["WqT1"]),
        (k.R4[0:64, 0:64], A["Wq1"]), (k.WPK[:, :], A["wpk"]), (k.KPK[:, :], A["kpk"]),
    ]
    for j in range(2):
        for r, n in ((8, "b1"), (9, "b2")):
            qkv.append((k.WX[r:r + 1, 64 * j:64 * j + 64], A[n]))
    for n in range(NH):
        s = slice(16 * n, 16 * n + 16)
        p = slice(32 * n, 32 * n + 16)
        qkv += [(k.HLP[0:64, p], A["hlT"][:, s]), (k.HLP[64:65, p], A["hl_b"][:, s]),
                (k.WVB[p, s], A["wvT"][n]), (k.wkb[p, p], A["wk"][n]),
                (k.FC1[s, s], A["fc1T"]), (k.FC1[64:65, s], A["fc1_b"]),
                (k.FC2[s, s], A["fc2T"]), (k.FC2[64:65, s], A["fc2_b"])]
        qkv += [(k.wqb[p, e, p], A["wq"][n, e]) for e in range(NE)]
    for t, n in ((k.LNG, "ln_g"), (k.LNB, "ln_b"), (k.FNG, "fn_g"), (k.FNB, "fn_b")):
        qkv.append((t[:, :], A[n].to_broadcast([TP, 16])))
    for h in range(PH):
        qkv += [(k.BD[0:64, h, 0:64], A["WqpT"][64 * h:64 * h + 64, :]),
                (k.BD[64:128, h, 64:128], A["Wo"][64 * h:64 * h + 64, :])]
    with nc.Block() as block:
        @block.sync
        def _(sp):
            for dst, src in qkv[0::2]:
                sp.dma_start(dst, src).then_inc(done, 16)
            sp.wait_ge(done, 16 * len(qkv))

        @block.scalar
        def _(act):
            for dst, src in qkv[1::2]:
                act.dma_start(dst, src).then_inc(done, 16)


def weight_products(nc, k, sem):
    made, kept = sem("weight_products_made"), sem("weight_products_kept")
    with nc.Block() as block:
        @block.tensor
        def _(pe):
            nc.tensor.matmul(k.PV[0:64, 0:64], k.WkN[:, :], k.WqN[:, :], start=True, stop=True)
            nc.tensor.matmul(k.PV[0:64, 64:128], k.WkT1[:, :], k.WB[0:64, 0:64], start=True, stop=True).then_inc(made, 1)
            for e in range(NE):
                last = nc.tensor.matmul(k.MI[:, e * 128:(e + 1) * 128], k.wqb[:, e, :], k.wkb[:, :],
                                        start=True, stop=True)
            last.then_inc(made, 1)
            for h in range(PH):
                for p in range(2):
                    c = (h * 2 + p) * 64
                    last = nc.tensor.matmul(k.S[0][0:64, c // 512, c % 512:c % 512 + 64],
                                            k.WPK[:, (p * PH + h) * 64:(p * PH + h + 1) * 64],
                                            k.KPK[:, (p * PH + h) * 64:(p * PH + h + 1) * 64], start=True, stop=True)
            last.then_inc(made, 1)

        @block.vector
        def _(dve):
            dve.wait_ge(made, 1)
            nc.vector.tensor_copy(k.ATT0[:, :], k.PV[0:64, 0:64])
            nc.vector.tensor_copy(k.R2[0:64, 65:129], k.PV[0:64, 64:128])
            nc.vector.tensor_copy(k.R2[64:65, 65:129], k.WB[64:65, 0:64])
            dve.wait_ge(made, 2)
            nc.vector.tensor_scalar_mul(k.LB[:, :, :], k.MI[:, :].rearrange("p (e c) -> p e c", e=NE), HD ** 0.5)
            dve.wait_ge(made, 3)
            nc.vector.tensor_copy(k.Mk[:, :].rearrange("p (a c) -> p a c", a=2), k.S[0][0:64, :, :])
            nc.vector.tensor_copy(k.place[:, :], k.place_i[:, :])
            nc.vector.tensor_scalar_mul(k.BD[0:64, :, :], k.BD[0:64, :, :], D ** -0.5)


def build_table(nc, k, A, sem):
    loaded, stored = sem("rows_loaded"), sem("rows_stored")
    turned, turned_kept = sem("rows_turned"), sem("turned_rows_kept")
    mapped, mapped_kept = sem("rows_mapped"), sem("mapped_rows_kept")
    N = ROWS // 1024
    with nc.Block() as block:
        @block.sync
        def _(sp):
            with sp.Fori(0, N) as i:
                sp.wait_ge(turned, i)
                for c, n in ((0, "keys"), (64, "values")):
                    src = A[n].rearrange("(i p j) d -> i p j d", p=128, j=8)[bass.ds(i, 1), :, :, :]
                    sp.dma_start(k.rows_in[:, :, c:c + 64], src.rearrange("a p j d -> (a p) j d")).then_inc(loaded, 16)
                sp.wait_ge(mapped_kept, 2 * i + 2)
                dst = k.table.rearrange("(i p j) d -> i p (j d)", p=128, j=8)
                sp.dma_start(row(dst, i), k.rows_out[:, :]).then_inc(stored, 16)
            sp.wait_ge(stored, 16 * N)

        @block.tensor
        def _(pe):
            with pe.Fori(0, N) as i:
                pe.wait_ge(loaded, 32 * i + 32)
                pe.wait_ge(turned_kept, 2 * i)
                for j in range(8):
                    last = nc.tensor.transpose(k.S[0][:, j // 4, (j % 4) * 128:(j % 4 + 1) * 128],
                                               k.rows_in[:, j, :], k.ident[:, :])
                last.then_inc(turned, 1)
                pe.wait_ge(turned_kept, 2 * i + 2)
                pe.wait_ge(mapped_kept, 2 * i)
                for j in range(8):
                    last = nc.tensor.matmul(k.S[1][:, j // 4, (j % 4) * 128:(j % 4 + 1) * 128],
                                            k.rows_turned[:, j * 128:(j + 1) * 128],
                                            k.BD[:, :, :].rearrange("p h c -> p (h c)")[:, bass.ds(((i >> 2) & (PH - 1)) * 128, 128)],
                                            start=True, stop=True)
                last.then_inc(mapped, 1)

        @block.scalar
        def _(act):
            with act.Fori(0, N) as i:
                act.wait_ge(turned, i + 1)
                act.wait_ge(mapped, i)
                nc.scalar.activation(k.rows_turned[:, 0:512], k.S[0][:, 0, :], ACT.Copy).then_inc(turned_kept, 1)
                act.wait_ge(mapped, i + 1)
                act.wait_ge(stored, 16 * i)
                nc.scalar.activation(k.rows_out[:, 0:512], k.S[1][:, 0, :], ACT.Copy).then_inc(mapped_kept, 1)

        @block.vector
        def _(dve):
            with dve.Fori(0, N) as i:
                dve.wait_ge(turned, i + 1)
                dve.wait_ge(mapped, i)
                nc.vector.tensor_copy(k.rows_turned[:, 512:1024], k.S[0][:, 1, :]).then_inc(turned_kept, 1)
                dve.wait_ge(mapped, i + 1)
                dve.wait_ge(stored, 16 * i)
                nc.vector.tensor_copy(k.rows_out[:, 512:1024], k.S[1][:, 1, :]).then_inc(mapped_kept, 1)



def tok_and_attention(nc, k, A, sem):
    xs_loaded, tok_products, tok_done = sem("xs_loaded"), sem("tok_products"), sem("tok_steps_done")
    tok_out, h1_ready, xn_ready = sem("tok_out"), sem("h1_ready"), sem("xn1_ready")
    xn_turned, xT_ready, kT_made, kT_ready = sem("xn1_turned"), sem("xT1_ready"), sem("kT1_made"), sem("kT1_ready")
    v_made, v_ready, h2_ready = sem("v1_made"), sem("v1_ready"), sem("h2_ready")
    xn2_ready, xn2_turned, xT2_ready = sem("xn2_ready"), sem("xn2_turned"), sem("xT2_ready")
    h2_stored, xT2_stored = sem("h2_stored"), sem("xT2_stored")
    k.var_ready, k.rstd_ready = sem("p1_var_ready"), sem("p1_rstd_ready")
    INCS = 2 * (STEPS - 1) + 4
    units = [unit(NT, k.xT[0:64, t * TP:(t + 1) * TP], k.kT[0:64, :],
                  lambda b: k.V[:, b * 64:(b + 1) * 64], k.PV[0:TP, t * 64:(t + 1) * 64], False) for t in range(NT)]
    att = Attention(nc, k, sem, "a1", units)
    with nc.Block() as block:
        @block.sync
        def _(sp):
            with sp.Fori(0, B) as b:
                sp.wait_ge(tok_out, b)
                sp.dma_start(k.xs[0:4, :], row(A["x"], b)).then_inc(xs_loaded, 16)
                sp.dma_start(k.xs[4:8, :], row(A["xr"], b)).then_inc(xs_loaded, 16)
                sp.wait_ge(h2_ready, b + 1)
                sp.dma_start(row(k.d_h2, b), k.h2[:, :]).then_inc(h2_stored, 16)
                sp.wait_ge(xT2_ready, b + 1)
                sp.dma_start(row(k.d_xT2, b), k.xT2[0:64, :]).then_inc(xT2_stored, 16)
            sp.wait_ge(h2_stored, 16 * B)
            sp.wait_ge(xT2_stored, 16 * B)

        @block.tensor
        def _(pe):
            with pe.Fori(0, B) as b:
                pe.wait_ge(xs_loaded, 32 * b + 32)
                for s in range(STEPS):
                    for h in range(2):
                        out = k.S[s % 2][:, h, 0:HALF]
                        last = nc.tensor.matmul(out, k.WX[:, :], k.xs[:, h * HALF:(h + 1) * HALF],
                                                start=True, stop=s == 0)
                        if s:
                            pe.wait_ge(tok_done, b * INCS + 2 * s - 1 + h)
                            last = nc.tensor.matmul(out, k.W2BD[:, :], k.U[(s - 1) % 2][:, h * HALF:(h + 1) * HALF],
                                                    start=False, stop=True)
                        last.then_inc(tok_products, 1)
                pe.wait_ge(tok_done, b * INCS + INCS)
                for t in range(NT):
                    out, cols = k.PV[0:TP, t * 64:(t + 1) * 64], slice(t * TP, (t + 1) * TP)
                    nc.tensor.matmul(out, k.xs[:, cols], k.R3[:, :], start=True, stop=False)
                    last = nc.tensor.matmul(out, k.UR[:, cols], k.W4[:, :], start=False, stop=True)
                last.then_inc(tok_out, 1)
                wait_apart(pe, xn_ready, b + 1)
                turn(nc, k, k.xn)
                k.turned_last.then_inc(xn_turned, 1)
                wait_apart(pe, xT_ready, b + 1)
                for h in range(2):
                    last = nc.tensor.matmul(k.S[1][0:64, h, 0:HALF], k.ATT0[:, :], k.xT[0:64, h * HALF:(h + 1) * HALF],
                                            start=True, stop=True)
                last.then_inc(kT_made, 1)
                for t in range(NT):
                    last = nc.tensor.matmul(k.MI[0:TP, t * 64:(t + 1) * 64], k.xT[0:64, t * TP:(t + 1) * TP],
                                            k.WvT[:, :], start=True, stop=True)
                last.then_inc(v_made, 1)
                pe.wait_ge(kT_ready, b + 1)
                pe.wait_ge(v_ready, b + 1)
                for m in range(NT + 2):
                    att.tensor(pe, b, m)
                wait_apart(pe, xn2_ready, b + 1)
                turn(nc, k, k.xn)
                k.turned_last.then_inc(xn2_turned, 1)

        @block.scalar
        def _(act):
            with act.Fori(0, B) as b:
                for s in range(STEPS - 1):
                    for h in range(2):
                        act.wait_ge(tok_products, b * 2 * STEPS + 2 * s + h + 1)
                        nc.scalar.activation(k.U[s % 2][:, 1 + h * HALF:1 + (h + 1) * HALF],
                                             k.S[s % 2][:, h, 0:HALF], ACT.Relu).then_inc(tok_done, 1)
                s = STEPS - 1
                act.wait_ge(tok_products, b * 2 * STEPS + 2 * s + 2)
                for h in range(2):
                    nc.scalar.activation(k.UR[0:64, 1 + h * HALF:1 + (h + 1) * HALF],
                                         k.S[1][0:64, h, 0:HALF], ACT.Relu).then_inc(tok_done, 1)
                nc.scalar.activation(k.UR[64:128, 0:HALF - 1], k.S[1][64:128, 1, HALF - 2::-1], ACT.Relu)\
                    .then_inc(tok_done, 1)
                nc.scalar.activation(k.UR[64:128, HALF - 1:L - 1], k.S[1][64:128, 0, HALF - 1::-1], ACT.Relu)\
                    .then_inc(tok_done, 1)
                act.wait_ge(tok_out, b + 1)
                nc.scalar.activation(k.h1[:, :], k.PV[0:TP, 0:384], ACT.Relu).then_inc(h1_ready, 1)
                act.wait_ge(xn_turned, b + 1)
                nc.scalar.activation(halves(k.xT[0:64, :]), k.T[0:64, :, 0:HALF], ACT.Copy).then_inc(xT_ready, 1)
                act.wait_ge(kT_made, b + 1)
                nc.scalar.activation(halves(k.kT[0:64, :]), k.S[1][0:64, :, 0:HALF], ACT.Copy).then_inc(kT_ready, 1)
                for m in range(NT + 2):
                    att.scalar(act, b, m)
                act.wait_ge(xn2_turned, b + 1)
                act.wait_ge(xT2_stored, 16 * b)
                nc.scalar.activation(halves(k.xT2[0:64, :]), k.T[0:64, :, 0:HALF], ACT.Copy).then_inc(xT2_ready, 1)

        @block.gpsimd
        def _(pool):
            with pool.Fori(0, B) as b:
                for n in range(2):
                    rsqrt(nc, pool, k, NT, b * 2 + n + 1)

        @block.vector
        def _(dve):
            with dve.Fori(0, B) as b:
                dve.wait_ge(h1_ready, b + 1)
                layernorm(nc, dve, k, tiles(k.h1), tiles(k.xn), NT, D, 1e-5,
                          lambda: dve.wait_ge(k.rstd_ready, 2 * b + 1), xn_ready)
                dve.wait_ge(v_made, b + 1)
                nc.vector.tensor_copy(k.V[:, :], k.MI[0:TP, 0:384]).then_inc(v_ready, 1)
                for m in range(NT + 2):
                    att.vector(dve, b, m)
                inverse_sums(nc, dve, k, 0, NT, False)
                dve.wait_ge(att.out_ready, NT * b + NT)
                nc.vector.tensor_tensor(tiles(k.tmp), tiles(k.PV[0:TP, 0:384]), bcast(k.rinv[:, 0:NT], D), ALU.mult)
                dve.drain()
                dve.wait_ge(h2_stored, 16 * b)
                nc.vector.scalar_tensor_tensor(k.h2[:, :], k.tmp[:, :], D ** -0.5, k.h1[:, :], ALU.mult, ALU.add)\
                    .then_inc(h2_ready, 1)
                dve.drain()
                layernorm(nc, dve, k, tiles(k.h2), tiles(k.xn), NT, D, 1e-5,
                          lambda: dve.wait_ge(k.rstd_ready, 2 * b + 2), xn2_ready)


def tiles(ap, w=D):
    ap = ap if isinstance(ap, bass.AP) else ap[:, :]
    return ap.rearrange("p (t w) -> p t w", w=w)


def halves(ap):
    return ap.rearrange("p (h w) -> p h w", h=2)


def turn(nc, k, src):
    for t in range(NT):
        k.turned_last = nc.tensor.transpose(k.T[0:64, t // 3, (t % 3) * TP:(t % 3 + 1) * TP],
                                            src[:, t * 64:(t + 1) * 64], k.ident[0:TP, 0:TP])



def residuals(nc, k, A, sem):
    loaded, made, kept = sem("resid_x_loaded"), sem("resid_made"), sem("resid_kept")
    with nc.Block() as block:
        @block.sync
        def _(sp):
            for n in range(NH):
                sp.wait_ge(made, n)
                sp.dma_start(k.xT2[0:64, :], k.d_xT2[n]).then_inc(loaded, 16)

        @block.tensor
        def _(pe):
            for n in range(NH):
                pe.wait_ge(loaded, 16 * n + 16)
                pe.wait_ge(kept, n)
                for t in range(NT):
                    last = nc.tensor.matmul(k.MI[0:TP, t * 16:(t + 1) * 16], k.xT2[:, t * TP:(t + 1) * TP],
                                            k.HLT[:, n * 16:(n + 1) * 16], start=True, stop=True)
                last.then_inc(made, 1)

        @block.vector
        def _(dve):
            for n in range(NH):
                dve.wait_ge(made, n + 1)
                nc.vector.tensor_copy(tiles(k.resid)[:, :, n * 16:(n + 1) * 16], tiles(k.MI[0:TP, 0:96], 16))\
                    .then_inc(kept, 1)


def softmax4(nc, dve, k, logits, groups, exp_in, exp_done, n):
    g, e = k.soft[:, 0:groups * 4].rearrange("p (g e) -> p g e", e=4), \
        k.soft_exp[:, 0:groups * 4].rearrange("p (g e) -> p g e", e=4)
    nc.vector.reduce_max(k.soft_m[:, 0:groups], logits, AXX)
    dve.drain()
    nc.vector.tensor_tensor(g, logits, bcast(k.soft_m[:, 0:groups], 4), ALU.subtract).then_inc(exp_in, 1)
    dve.wait_ge(exp_done, n)
    nc.vector.reduce_sum(k.soft_m[:, 0:groups], e, AXX)
    dve.drain()
    nc.vector.reciprocal(k.soft_m[:, 0:groups], k.soft_m[:, 0:groups])
    dve.drain()
    nc.vector.tensor_tensor(g, e, bcast(k.soft_m[:, 0:groups], 4), ALU.mult)
    dve.drain()


def sigmoid_of_exp(nc, dve, dst, e):
    nc.vector.tensor_scalar_add(dst, e, 1.0)
    dve.drain()
    nc.vector.reciprocal(dst, dst)
    dve.drain()


def r2_place(k, t):
    bank = (k.S[0][:, 0, :], k.S[0][:, 1, :], k.S[1][:, 0, :])[t // 2]
    return bank[0:TP, (t % 2) * 194:(t % 2 + 1) * 194]


def ffn_and_gradients(nc, k, A, sem):
    h2_loaded, x_loaded, sxT_made, sxT_ready = sem("h2_loaded"), sem("xT2_loaded"), sem("sxT_made"), sem("sxT_ready")
    sx_made, sx_ready, u_made, u_ready = sem("sx_made"), sem("sx_ready"), sem("u_made"), sem("u_ready")
    v_made, v_ready, att_kept = sem("v2_made"), sem("v2_ready"), sem("att_kept")
    att_turned, attT_ready, gate_made = sem("att_turned"), sem("attT_ready"), sem("gate_made")
    soft_in, soft_exp = sem("soft_in"), sem("soft_exp")
    src_ready, turned, turned_kept = sem("p2_turn_source"), sem("p2_turned"), sem("p2_turned_kept")
    fc1_made, fc2_made, fg_made, r2_made = sem("fc1_made"), sem("fc2_made"), sem("fgate_made"), sem("r2_made")
    g_ready, z1_made, e1_ready, dx_made = sem("x0_ready"), sem("z1_made"), sem("e1_ready"), sem("dx_made")
    dz0_ready, grads_made, grads_kept = sem("dz0_ready"), sem("grads_made"), sem("grads_kept")
    h3_ready, h3_stored, xT3_stored = sem("h3_ready"), sem("h3_stored"), sem("xT3_stored")
    k.var_ready, k.rstd_ready = sem("p2_var_ready"), sem("p2_rstd_ready")
    units = []
    for i in range(NT):
        for n in range(NH):
            for e in range(NE):
                p = slice(32 * n, 32 * n + 16)
                c = (n * NE + e) * 16
                units.append(unit(i + 1, k.UT[p, e, i * TP:(i + 1) * TP], k.sxT[p, :],
                                  (lambda n: lambda b: k.V[:, b * 64 + n * 16:b * 64 + n * 16 + 16])(n),
                                  (k.PV, k.MI)[i % 2][0:TP, c:c + 16], True))
    att = Attention(nc, k, sem, "a2", units)
    TURNS = 6
    with nc.Block() as block:
        @block.sync
        def _(sp):
            with sp.Fori(0, B) as b:
                sp.wait_ge(u_ready, 4 * b)
                sp.dma_start(k.xT2[0:64, :], row(k.d_xT2, b)).then_inc(x_loaded, 16)
                sp.wait_ge(h3_ready, b)
                sp.dma_start(k.h2[:, :], row(k.d_h2, b)).then_inc(h2_loaded, 16)
                sp.wait_ge(h3_ready, b + 1)
                sp.dma_start(row(k.d_h3, b), k.h3[:, :]).then_inc(h3_stored, 16)
                sp.wait_ge(turned_kept, TURNS * b + 4)
                sp.dma_start(row(k.d_xT3, b), k.xT3[0:64, :]).then_inc(xT3_stored, 16)
            sp.wait_ge(h3_stored, 16 * B)
            sp.wait_ge(xT3_stored, 16 * B)

        @block.tensor
        def _(pe):
            def turned_of(b, n, src):
                wait_apart(pe, src_ready, TURNS * b + n)
                turn(nc, k, src)
                k.turned_last.then_inc(turned, 1)
                pe.wait_ge(turned_kept, TURNS * b + n)

            def per_tile(weights, width, rows, x, done, col=0):
                for t in range(NT):
                    last = nc.tensor.matmul(k.MI[0:TP, t * width:(t + 1) * width], x[0:rows, t * TP:(t + 1) * TP],
                                            weights, start=True, stop=True)
                last.then_inc(done, 1)

            with pe.Fori(0, B) as b:
                pe.wait_ge(x_loaded, 16 * b + 16)
                for h in range(2):
                    last = nc.tensor.matmul(k.S[0][:, h, 0:HALF], k.HLP[:, :], k.xT2[:, h * HALF:(h + 1) * HALF],
                                            start=True, stop=True)
                last.then_inc(sxT_made, 1)
                per_tile(k.HLT[:, :], 64, 65, k.xT2, sx_made)
                pe.wait_ge(sxT_ready, b + 1)
                for e in range(NE):
                    if e >= 2:
                        pe.wait_ge(u_ready, 4 * b + e - 1)
                    for h in range(2):
                        last = nc.tensor.matmul(k.S[(e + 1) % 2][:, h, 0:HALF], k.LB[:, e, :],
                                                k.sxT[:, h * HALF:(h + 1) * HALF], start=True, stop=True)
                    last.then_inc(u_made, 1)
                pe.wait_ge(sx_ready, b + 1)
                per_tile(k.WVB[:, :], 64, 128, k.sxT, v_made)
                pe.wait_ge(u_ready, 4 * b + 4)
                pe.wait_ge(v_ready, b + 1)
                for m in range(len(units) + 2):
                    n = m - 2
                    if n >= 32 and n % 16 == 0:
                        pe.wait_ge(att_kept, NT * b + n // 16 - 1)
                    att.tensor(pe, b, m)
                pe.wait_ge(att_kept, NT * b + NT)
                for c in range(2):
                    for t in range(NT):
                        last = nc.tensor.transpose(k.S[c][:, t // 3, (t % 3) * TP:(t % 3 + 1) * TP],
                                                   k.att[:, t, c * 128:(c + 1) * 128], k.ident[0:TP, 0:TP])
                last.then_inc(att_turned, 1)
                pe.wait_ge(attT_ready, b + 1)
                for t in range(NT):
                    out, cols = k.MI[0:TP, t * 16:(t + 1) * 16], slice(t * TP, (t + 1) * TP)
                    nc.tensor.matmul(out, k.ones[0:1, 0:TP], k.GB[:, :], start=True, stop=False)
                    nc.tensor.matmul(out, k.UT[:, 0, cols], k.GW[:, 0, :], start=False, stop=False)
                    last = nc.tensor.matmul(out, k.UT[:, 1, cols], k.GW[:, 1, :], start=False, stop=True)
                last.then_inc(gate_made, 1)
                turned_of(b, 1, k.fx)
                per_tile(k.FC1[:, :], 64, 65, k.xT, fc1_made)
                turned_of(b, 2, k.hx)
                per_tile(k.FC2[:, :], 64, 65, k.xT, fc2_made)
                turned_of(b, 3, k.fout)
                per_tile(k.FG[:, :], 4, 64, k.xT, fg_made)
                turned_of(b, 4, k.xn)
                for t in range(NT):
                    last = nc.tensor.matmul(r2_place(k, t), k.xT3[:, t * TP:(t + 1) * TP], k.R2[:, :],
                                            start=True, stop=True)
                last.then_inc(r2_made, 1)
                wait_apart(pe, src_ready, TURNS * b + 5)
                for t in range(NT):
                    last = nc.tensor.transpose(k.T[0:64, t // 3, (t % 3) * TP:(t % 3 + 1) * TP],
                                               k.x1[:, t, 0:64], k.ident[0:TP, 0:TP])
                last.then_inc(turned, 1)
                pe.wait_ge(turned_kept, TURNS * b + 5)
                per_tile(k.WB[:, 64:128], 64, 65, k.xT, z1_made)
                turned_of(b, 6, k.dz1)
                per_tile(k.W1Tr[:, :], 64, 64, k.xT, dx_made)
                pe.wait_ge(dz0_ready, b + 1)
                for t in range(NT):
                    nc.tensor.matmul(k.PV[0:65, 0:64], k.G[:, t, 0:65], k.dz0[:, t * 64:(t + 1) * 64],
                                     start=t == 0, stop=t == NT - 1)
                for t in range(NT):
                    last = nc.tensor.matmul(k.PV[0:65, 64:128], k.x1[:, t, :], k.dz1[:, t * 64:(t + 1) * 64],
                                            start=t == 0, stop=t == NT - 1)
                last.then_inc(grads_made, 1)
                pe.wait_ge(grads_kept, b + 1)

        @block.scalar
        def _(act):
            def keep_turned(b, n, dst):
                act.wait_ge(turned, TURNS * b + n)
                nc.scalar.activation(halves(dst[0:64, :]), k.T[0:64, :, 0:HALF], ACT.Copy).then_inc(turned_kept, 1)

            with act.Fori(0, B) as b:
                act.wait_ge(sxT_made, b + 1)
                nc.scalar.activation(halves(k.sxT[:, :]), k.S[0][:, :, 0:HALF], ACT.Copy).then_inc(sxT_ready, 1)
                for e in range(NE):
                    act.wait_ge(u_made, 4 * b + e + 1)
                    nc.scalar.activation(halves(k.UT[:, e, :]), k.S[(e + 1) % 2][:, :, 0:HALF], ACT.Copy)\
                        .then_inc(u_ready, 1)
                for m in range(len(units) + 2):
                    att.scalar(act, b, m)
                act.wait_ge(att_turned, b + 1)
                nc.scalar.activation(halves(k.UT[:, 0, :]), k.S[0][:, :, 0:HALF], ACT.Copy)
                nc.scalar.activation(halves(k.UT[:, 1, :]), k.S[1][:, :, 0:HALF], ACT.Copy).then_inc(attT_ready, 1)
                act.wait_ge(soft_in, 2 * b + 1)
                nc.scalar.activation(k.soft_exp[:, 0:96], k.soft[:, 0:96], ACT.Exp).then_inc(soft_exp, 1)
                for n in (1, 2, 3):
                    keep_turned(b, n, k.xT)
                act.wait_ge(soft_in, 2 * b + 2)
                nc.scalar.activation(k.soft_exp[:, 0:24], k.soft[:, 0:24], ACT.Exp).then_inc(soft_exp, 1)
                act.wait_ge(xT3_stored, 16 * b)
                keep_turned(b, 4, k.xT3)
                act.wait_ge(r2_made, b + 1)
                for c in range(3):
                    src = (k.S[0][0:TP, 0, :], k.S[0][0:TP, 1, :], k.S[1][0:TP, 0, :])[c][:, 0:388]\
                        .rearrange("p (a w) -> p a w", a=2)
                    nc.scalar.activation(k.G[:, 2 * c:2 * c + 2, :], src, ACT.Copy)
                    last = nc.scalar.activation(k.E0[:, 2 * c:2 * c + 2, 0:64], src[:, :, 65:129], ACT.Exp, scale=-1.0)
                    last = nc.scalar.activation(k.E0[:, 2 * c:2 * c + 2, 64:65], src[:, :, 193:194], ACT.Exp, scale=-1.0)
                last.then_inc(g_ready, 1)
                keep_turned(b, 5, k.xT)
                act.wait_ge(z1_made, b + 1)
                nc.scalar.activation(k.E1[:, :], k.MI[0:TP, 0:384], ACT.Exp, scale=-1.0).then_inc(e1_ready, 1)
                keep_turned(b, 6, k.xT)

        @block.gpsimd
        def _(pool):
            with pool.Fori(0, B) as b:
                rsqrt(nc, pool, k, NT * NH, 3 * b + 1)
                rsqrt(nc, pool, k, NT * NH, 3 * b + 2)
                rsqrt(nc, pool, k, NT, 3 * b + 3)

        @block.vector
        def _(dve):
            def normalise(b, i):
                dve.wait_ge(att.out_ready, 96 * b + 16 * (i + 1))
                inverse_sums(nc, dve, k, 16 * i, 16 * i + 16, i in (3, 4))
                nc.vector.tensor_tensor(k.att[:, i, :].rearrange("p (a d) -> p a d", d=16),
                                        (k.PV, k.MI)[i % 2][0:TP, 0:256].rearrange("p (a d) -> p a d", d=16),
                                        bcast(k.rinv[:, 16 * i:16 * i + 16], 16), ALU.mult)
                dve.drain()
                a4 = k.att[:, i, :].rearrange("p (n e d) -> p n e d", n=NH, e=NE)
                m4 = k.live[:, i * 64:(i + 1) * 64].rearrange("p (n d) -> p n d", n=NH).unsqueeze(2)\
                    .to_broadcast([TP, NH, NE, HD])
                nc.vector.tensor_tensor(a4, a4, m4, ALU.mult).then_inc(att_kept, 1)

            with dve.Fori(0, B) as b:
                dve.wait_ge(sx_made, b + 1)
                nc.vector.tensor_scalar(k.live[:, :], k.MI[0:TP, 0:384], 0.0, None, ALU.not_equal).then_inc(sx_ready, 1)
                dve.wait_ge(v_made, b + 1)
                nc.vector.tensor_copy(k.V[:, :], k.MI[0:TP, 0:384]).then_inc(v_ready, 1)
                for m in range(len(units) + 2):
                    att.vector(dve, b, m)
                    if m >= 20 and m % 16 == 4:
                        normalise(b, m // 16 - 1)
                normalise(b, NT - 1)
                dve.wait_ge(gate_made, b + 1)
                softmax4(nc, dve, k, k.MI[0:TP, 0:96].rearrange("p (g e) -> p g e", e=4), 24, soft_in, soft_exp, 2 * b + 1)
                nc.vector.tensor_tensor(k.big[:, :].rearrange("p (a d) -> p a d", d=16),
                                        k.att[:, :, :].rearrange("p t (a d) -> p (t a) d", d=16),
                                        bcast(k.soft[:, 0:96], 16), ALU.mult)
                dve.drain()
                nc.vector.reduce_sum(tiles(k.mix, 16), k.big[:, :].rearrange("p (g e d) -> p g d e", e=NE, d=HD), AXX)
                dve.drain()
                nc.vector.tensor_tensor(k.mix[:, :], k.mix[:, :], k.resid[:, :], ALU.add)
                dve.drain()
                layernorm(nc, dve, k, tiles(k.mix, 16), tiles(k.fx, 16), 24, 16, 1e-8,
                          lambda: dve.wait_ge(k.rstd_ready, 3 * b + 1), src_ready, k.LNG, k.LNB)
                nc.vector.tensor_scalar(k.live[:, :], k.fx[:, :], 0.0, None, ALU.not_equal)
                dve.drain()
                dve.wait_ge(fc1_made, b + 1)
                nc.vector.scalar_tensor_tensor(k.hx[:, :], k.MI[0:TP, 0:384], 0.0, k.live[:, :], ALU.max, ALU.mult)\
                    .then_inc(src_ready, 1)
                dve.wait_ge(fc2_made, b + 1)
                nc.vector.tensor_tensor(k.mix[:, :], k.MI[0:TP, 0:384], k.live[:, :], ALU.mult)
                dve.drain()
                nc.vector.tensor_tensor(k.mix[:, :], k.mix[:, :], k.fx[:, :], ALU.add)
                dve.drain()
                layernorm(nc, dve, k, tiles(k.mix, 16), tiles(k.fout, 16), 24, 16, 1e-8,
                          lambda: dve.wait_ge(k.rstd_ready, 3 * b + 2), src_ready, k.FNG, k.FNB)
                dve.wait_ge(fg_made, b + 1)
                softmax4(nc, dve, k, k.MI[0:TP, 0:24].rearrange("p (g e) -> p g e", e=4), NT, soft_in, soft_exp, 2 * b + 2)
                nc.vector.tensor_tensor(tiles(k.mix, 16), tiles(k.fout, 16), bcast(k.soft[:, 0:24], 16), ALU.mult)
                dve.drain()
                dve.wait_ge(h3_stored, 16 * b)
                dve.wait_ge(h2_loaded, 16 * b + 16)
                nc.vector.tensor_tensor(k.h3[:, :], k.mix[:, :], k.h2[:, :], ALU.add).then_inc(h3_ready, 1)
                dve.drain()
                layernorm(nc, dve, k, tiles(k.h3), tiles(k.xn), NT, D, 1e-5,
                          lambda: dve.wait_ge(k.rstd_ready, 3 * b + 3), src_ready)
                dve.wait_ge(g_ready, b + 1)
                x0, z0, tgt = k.G[:, :, 0:64], k.G[:, :, 65:129], k.G[:, :, 129:193]
                sigmoid_of_exp(nc, dve, k.E0[:, :, :], k.E0[:, :, :])
                s0 = k.E0[:, :, 0:64]
                nc.vector.tensor_scalar_mul(k.alr[:, :].unsqueeze(2), k.E0[:, :, 64:65], 0.1 * 2.0 / D)
                nc.vector.tensor_tensor(tiles(k.silu), z0, s0, ALU.mult)
                dve.drain()
                nc.vector.tensor_tensor(k.x1[:, :, 0:64], x0, tiles(k.silu), ALU.add).then_inc(src_ready, 1)
                slope(nc, dve, tiles(k.d0), s0, tiles(k.silu), tiles(k.tmp))
                dve.wait_ge(e1_ready, b + 1)
                sigmoid_of_exp(nc, dve, k.E1[:, :], k.E1[:, :])
                nc.vector.tensor_tensor(k.silu[:, :], k.MI[0:TP, 0:384], k.E1[:, :], ALU.mult)
                dve.drain()
                nc.vector.tensor_tensor(tiles(k.dx), k.x1[:, :, 0:64], tiles(k.silu), ALU.add)
                dve.drain()
                nc.vector.tensor_tensor(tiles(k.dx), tiles(k.dx), tgt, ALU.subtract)
                dve.drain()
                nc.vector.tensor_tensor(tiles(k.dx), tiles(k.dx), bcast(k.alr[:, :], D), ALU.mult)
                slope(nc, dve, k.dz1[:, :], k.E1[:, :], k.silu[:, :], k.tmp[:, :])
                nc.vector.tensor_tensor(k.dz1[:, :], k.dz1[:, :], k.dx[:, :], ALU.mult).then_inc(src_ready, 1)
                dve.wait_ge(dx_made, b + 1)
                nc.vector.tensor_tensor(k.dx[:, :], k.MI[0:TP, 0:384], k.dx[:, :], ALU.add)
                dve.drain()
                nc.vector.tensor_tensor(k.dz0[:, :], k.dx[:, :], k.d0[:, :], ALU.mult).then_inc(dz0_ready, 1)
                dve.wait_ge(grads_made, b + 1)
                nc.vector.tensor_tensor(k.grads[:, :], k.grads[:, :], k.PV[0:65, 0:128], ALU.add).then_inc(grads_kept, 1)
                dve.drain()


def slope(nc, dve, dst, s, silu, tmp):
    nc.vector.tensor_tensor(tmp, silu, s, ALU.mult)
    nc.vector.tensor_tensor(dst, silu, s, ALU.add)
    dve.drain()
    nc.vector.tensor_tensor(dst, dst, tmp, ALU.subtract)
    dve.drain()


def adamw(nc, k, sem):
    squared, rooted, stepped, made = sem("grads_squared"), sem("grads_rooted"), sem("stepped"), sem("wq_w0_made")
    with nc.Block() as block:
        @block.gpsimd
        def _(pool):
            pool.wait_ge(squared, 1)
            nc.gpsimd.tensor_tensor(k.gabs[:, :], k.gsq[:, :], k.plus_half[0:65, 0:1].to_broadcast([65, 128]), ALU.pow)\
                .then_inc(rooted, 1)

        @block.vector
        def _(dve):
            nc.vector.tensor_tensor(k.gsq[:, :], k.grads[:, :], k.grads[:, :], ALU.mult).then_inc(squared, 1)
            dve.wait_ge(rooted, 1)
            nc.vector.tensor_scalar_add(k.gabs[:, :], k.gabs[:, :], 1e-8)
            dve.drain()
            nc.vector.reciprocal(k.gabs[:, :], k.gabs[:, :])
            dve.drain()
            nc.vector.tensor_tensor(k.gabs[:, :], k.gabs[:, :], k.grads[:, :], ALU.mult)
            nc.vector.tensor_scalar_mul(k.NW[:, :], k.WB[:, :], 1.0 - 0.001 * 0.01)
            dve.drain()
            nc.vector.scalar_tensor_tensor(k.NW[:, :], k.gabs[:, :], -0.001, k.NW[:, :], ALU.mult, ALU.add)\
                .then_inc(stepped, 1)
            dve.drain()
            dve.wait_ge(made, 1)
            nc.vector.memset(k.R4[64:65, 0:64], 0.0)
            nc.vector.tensor_copy(k.R4[0:64, 64:128], k.MI[0:64, 0:64])
            nc.vector.tensor_copy(k.R4[64:65, 64:128], k.NW[64:65, 0:64])

        @block.tensor
        def _(pe):
            pe.wait_ge(stepped, 1)
            nc.tensor.matmul(k.MI[0:64, 0:64], k.WqT1[:, :], k.NW[0:64, 0:64], start=True, stop=True).then_inc(made, 1)



def retrieve(nc, k, A, out, sem):
    loaded, made, g_ready = sem("h3_loaded"), sem("q_made"), sem("q_ready")
    src_ready, turned, turned_kept = sem("p3_turn_source"), sem("p3_turned"), sem("p3_turned_kept")
    z1_made, e1_ready, h4_ready = sem("rz1_made"), sem("re1_ready"), sem("h4_ready")
    h4_stored, xT4_stored = sem("h4_stored"), sem("xT4_stored")
    k.var_ready, k.rstd_ready = sem("p3_var_ready"), sem("p3_rstd_ready")
    with nc.Block() as block:
        @block.sync
        def _(sp):
            with sp.Fori(0, B) as b:
                sp.wait_ge(h4_ready, b)
                sp.dma_start(k.h3[:, :], row(k.d_h3, b)).then_inc(loaded, 16)
                sp.dma_start(k.xT3[0:64, :], row(k.d_xT3, b)).then_inc(loaded, 16)
                sp.wait_ge(h4_ready, b + 1)
                sp.dma_start(tokens(out, b), tiles(k.h4)).then_inc(h4_stored, 16)
                sp.wait_ge(turned_kept, 2 * b + 2)
                sp.dma_start(row(k.d_xT4, b), k.xT2[0:64, :]).then_inc(xT4_stored, 16)
            sp.wait_ge(h4_stored, 16 * B)
            sp.wait_ge(xT4_stored, 16 * B)

        @block.tensor
        def _(pe):
            with pe.Fori(0, B) as b:
                pe.wait_ge(loaded, 32 * b + 32)
                for t in range(NT):
                    last = nc.tensor.matmul(k.S[0][0:TP, t // 3, (t % 3) * 128:(t % 3 + 1) * 128],
                                            k.xT3[:, t * TP:(t + 1) * TP], k.R4[:, :], start=True, stop=True)
                last.then_inc(made, 1)
                wait_apart(pe, src_ready, 2 * b + 1)
                turn(nc, k, k.q1)
                k.turned_last.then_inc(turned, 1)
                pe.wait_ge(turned_kept, 2 * b + 1)
                for t in range(NT):
                    last = nc.tensor.matmul(k.MI[0:TP, t * 64:(t + 1) * 64], k.xT[:, t * TP:(t + 1) * TP],
                                            k.NW[:, 64:128], start=True, stop=True)
                last.then_inc(z1_made, 1)
                wait_apart(pe, src_ready, 2 * b + 2)
                turn(nc, k, k.xn)
                k.turned_last.then_inc(turned, 1)

        @block.scalar
        def _(act):
            with act.Fori(0, B) as b:
                act.wait_ge(made, b + 1)
                for c in range(2):
                    src = k.S[0][0:TP, c, 0:384].rearrange("p (a w) -> p a w", a=3)
                    nc.scalar.activation(k.G[:, 3 * c:3 * c + 3, 0:128], src, ACT.Copy)
                    last = nc.scalar.activation(k.E0[:, 3 * c:3 * c + 3, 0:64], src[:, :, 64:128], ACT.Exp, scale=-1.0)
                last.then_inc(g_ready, 1)
                act.wait_ge(turned, 2 * b + 1)
                nc.scalar.activation(halves(k.xT[0:64, :]), k.T[0:64, :, 0:HALF], ACT.Copy).then_inc(turned_kept, 1)
                act.wait_ge(z1_made, b + 1)
                nc.scalar.activation(k.E1[:, :], k.MI[0:TP, 0:384], ACT.Exp, scale=-1.0).then_inc(e1_ready, 1)
                act.wait_ge(turned, 2 * b + 2)
                act.wait_ge(xT4_stored, 16 * b)
                nc.scalar.activation(halves(k.xT2[0:64, :]), k.T[0:64, :, 0:HALF], ACT.Copy).then_inc(turned_kept, 1)

        @block.gpsimd
        def _(pool):
            with pool.Fori(0, B) as b:
                rsqrt(nc, pool, k, NT, b + 1)

        @block.vector
        def _(dve):
            with dve.Fori(0, B) as b:
                dve.wait_ge(g_ready, b + 1)
                s0 = k.E0[:, :, 0:64]
                sigmoid_of_exp(nc, dve, s0, s0)
                nc.vector.tensor_tensor(tiles(k.silu), k.G[:, :, 64:128], s0, ALU.mult)
                dve.drain()
                nc.vector.tensor_tensor(tiles(k.q1), k.G[:, :, 0:64], tiles(k.silu), ALU.add).then_inc(src_ready, 1)
                dve.wait_ge(e1_ready, b + 1)
                nc.vector.tensor_tensor(k.q1[:, :], k.q1[:, :], k.h3[:, :], ALU.add)
                sigmoid_of_exp(nc, dve, k.E1[:, :], k.E1[:, :])
                nc.vector.tensor_tensor(k.silu[:, :], k.MI[0:TP, 0:384], k.E1[:, :], ALU.mult)
                dve.drain()
                dve.wait_ge(h4_stored, 16 * b)
                nc.vector.tensor_tensor(k.h4[:, :], k.q1[:, :], k.silu[:, :], ALU.add).then_inc(h4_ready, 1)
                dve.drain()
                layernorm(nc, dve, k, tiles(k.h4), tiles(k.xn), NT, D, 1e-5,
                          lambda: dve.wait_ge(k.rstd_ready, b + 1), src_ready)



def product_key_attention(nc, k, out, sem):
    xk_loaded, sims_made, sims_ready = sem("xk_loaded"), sem("sims_made"), sem("sims_ready")
    top_exp_in, top_exp, chosen = sem("top_exp_in"), sem("top_exp"), sem("indices_chosen")
    xa_loaded, acc_loaded, acc_ready, acc_stored = sem("xa_loaded"), sem("acc_loaded"), sem("acc_ready"), sem("acc_stored")
    gathered = [sem(f"gathered_{t}") for t in range(NT)]
    taken = sem("gathered_rows_taken")
    kv_turned, kv_ready = sem("kv_turned"), sem("kT4_ready")
    G = B * PH
    units = [unit(t + 1, k.xT[0:64, t * TP:(t + 1) * TP], k.kT[0:64, :],
                  lambda b: k.kv[:, b * 128 + 64:(b + 1) * 128], k.PV[0:TP, t * 64:(t + 1) * 64], True)
             for t in range(NT)]
    att = Attention(nc, k, sem, "a4", units)

    with nc.Block() as block:
        @block.sync
        def _(sp):
            def load_xk(g, b):
                wait_apart(sp, sims_made, g)
                sp.dma_start(k.xT3[0:64, :], row(k.d_xT4, b)).then_inc(xk_loaded, 16)

            def attention_io(g, b, b_last):
                wait_apart(sp, att.out_ready, NT * g)
                sp.dma_start(k.xT[0:64, :], row(k.d_xT4, b)).then_inc(xa_loaded, 16)
                wait_apart(sp, acc_stored, 16 * g)
                sp.dma_start(tiles(k.h4), tokens(out, b)).then_inc(acc_loaded, 16)
                wait_apart(sp, acc_ready, g + 1)
                sp.dma_start(tokens(out, b), tiles(k.h4)).then_inc(acc_stored, 16)

            load_xk(0, 0)
            with sp.Fori(0, G - 1) as g:
                b_next, b_now = ((g + 1) >> 3) & (B - 1), (g >> 3) & (B - 1)
                load_xk(g + 1, b_next)
                attention_io(g, b_now, 0)
            attention_io(G - 1, B - 1, 0)
            sp.wait_ge(acc_stored, 16 * G)

        @block.gpsimd
        def _(pool):
            with pool.Fori(0, G) as g:
                for t in range(NT):
                    wait_apart(pool, chosen, NT * g + t + 1)
                    for j in range(TOPK):
                        pool.indirect_dma_start(
                            out=k.rows[t][:, j * 128:(j + 1) * 128], out_offset=None, in_=k.table,
                            in_offset=bass.IndirectOffsetOnAxis(ap=k.idx[:, t * TOPK + j:t * TOPK + j + 1], axis=0))\
                            .then_inc(gathered[t], 16)

        @block.tensor
        def _(pe):
            def scores_of(g, h):
                pe.wait_ge(xk_loaded, 16 * g + 16)
                pe.wait_ge(sims_ready, 2 * g)
                for t in range(NT):
                    last = nc.tensor.matmul(k.S2[0:TP, t // 3, (t % 3) * 128:(t % 3 + 1) * 128],
                                            k.xT3[0:64, t * TP:(t + 1) * TP], k.Mk[:, bass.ds(h * 128, 128)],
                                            start=True, stop=True)
                last.then_inc(sims_made, 1)

            def attention(g):
                pe.wait_ge(xa_loaded, 16 * g + 16)
                for m in range(NT + 2):
                    if m < NT:
                        pe.wait_ge(kv_ready, NT * g + m)
                        wait_apart(pe, taken, NT * g + m + 1)
                        nc.tensor.transpose(k.MI[0:64, 0:TP], k.kv[:, m * 128:m * 128 + 64], k.ident[0:TP, 0:TP])\
                            .then_inc(kv_turned, 1)
                        pe.wait_ge(kv_ready, NT * g + m + 1)
                    if m == 2:
                        pe.wait_ge(acc_ready, g)
                    att.tensor(pe, g, m)

            scores_of(0, 0)
            with pe.Fori(0, G - 1) as g:
                h_next = (g + 1) & 7
                scores_of(g + 1, h_next)
                attention(g)
            attention(G - 1)

        @block.scalar
        def _(act):
            def choose(g):
                act.wait_ge(sims_made, g + 1)
                act.wait_ge(top_exp_in, g)
                for c in range(2):
                    nc.scalar.activation(k.sims[:, 3 * c:3 * c + 3, :],
                                         k.S2[0:TP, c, 0:384].rearrange("p (a w) -> p a w", a=3), ACT.Copy)\
                        .then_inc(sims_ready, 1)
                act.wait_ge(top_exp_in, g + 1)
                nc.scalar.activation(k.top_e[:, :], k.top_v[:, :], ACT.Exp).then_inc(top_exp, 1)

            def attention(g):
                for m in range(NT + 2):
                    if m < NT:
                        act.wait_ge(kv_turned, NT * g + m + 1)
                        nc.scalar.activation(k.kT[0:64, m * TP:(m + 1) * TP], k.MI[0:64, 0:TP], ACT.Copy)\
                            .then_inc(kv_ready, 1)
                    att.scalar(act, g, m)

            choose(0)
            with act.Fori(0, G - 1) as g:
                choose(g + 1)
                attention(g)
            attention(G - 1)

        @block.vector
        def _(dve):
            sc = k.sc[:, :].rearrange("p (t a n) -> p t a n", t=NT, a=2)
            ix = k.ix[:, :].rearrange("p (t a n) -> p t a n", t=NT, a=2)
            ixf = k.ixf[:, :].rearrange("p (t a n) -> p t a n", t=NT, a=2)
            cand = k.cand[:, :].rearrange("p (t n) -> p t n", t=NT)
            cidx = k.cidx[:, :].rearrange("p (t n) -> p t n", t=NT)

            def pairs(dst, src):
                at = 0
                for i0, ni, nj in RUNS:
                    for t0 in range(0, NT, 1 if ni > 1 and nj > 1 else NT):
                        ts = slice(t0, t0 + 1) if ni > 1 and nj > 1 else slice(0, NT)
                        d = dst[:, ts, at:at + ni * nj]
                        a, b = src[:, ts, 0, i0:i0 + ni], src[:, ts, 1, 0:nj]
                        if ni > 1 and nj > 1:
                            d = dst[:, t0, at:at + ni * nj].rearrange("p (i j) -> p i j", j=nj)
                            a = src[:, t0, 0, i0:i0 + ni].unsqueeze(2).to_broadcast([TP, ni, nj])
                            b = src[:, t0, 1, 0:nj].unsqueeze(1).to_broadcast([TP, ni, nj])
                        elif ni == 1:
                            a = a.to_broadcast([TP, NT, nj])
                        else:
                            b = b.to_broadcast([TP, NT, ni])
                        nc.vector.tensor_tensor(d, a, b, ALU.add)
                    at += ni * nj

            def choose(g, h):
                nc.vector.tensor_copy(k.head[:, :], k.heads[:, bass.ds(h, 1)])
                dve.wait_ge(sims_ready, 2 * g + 2)
                nc.vector.tensor_copy(k.gate[:, :], k.ones[0:TP, 0:1])
                both = [(t, a) for t in range(NT) for a in range(2)]
                for t, a in both:
                    nc.vector.max(sc[:, t, a, 0:8], k.sims[:, t, a * 64:(a + 1) * 64])
                dve.drain()
                for t, a in both:
                    s = k.sims[:, t, a * 64:(a + 1) * 64]
                    nc.vector.max_index(ix[:, t, a, 0:8], sc[:, t, a, 0:8], s)
                    nc.vector.match_replace(k.sims2[:, t, a * 64:(a + 1) * 64], sc[:, t, a, 0:8], s, NEG)
                dve.drain()
                for t, a in both:
                    nc.vector.max(sc[:, t, a, 8:16], k.sims2[:, t, a * 64:(a + 1) * 64])
                dve.drain()
                for t, a in both:
                    nc.vector.max_index(ix[:, t, a, 8:16], sc[:, t, a, 8:16], k.sims2[:, t, a * 64:(a + 1) * 64])
                dve.drain()
                nc.vector.tensor_copy(k.ixf[:, :], k.ix[:, :])
                dve.drain()
                nc.vector.tensor_scalar(ixf[:, :, 1, :], ixf[:, :, 1, :], float(PKEYS), None, ALU.mult)
                nc.vector.tensor_scalar(ixf[:, :, 0, :], ixf[:, :, 0, :], k.head[:, 0:1], None, ALU.add)
                pairs(cand, sc)
                dve.drain()
                pairs(cidx, ixf)
                for t in range(NT):
                    nc.vector.max(k.top[:, t, 0:8], cand[:, t, :])
                dve.drain()
                for t in range(NT):
                    nc.vector.max_index(k.pos[:, t, 0:8], k.top[:, t, 0:8], cand[:, t, :])
                    nc.vector.match_replace(k.cand2[:, t, :], k.top[:, t, 0:8], cand[:, t, :], NEG)
                dve.drain()
                for t in range(NT):
                    nc.vector.max(k.top[:, t, 8:16], k.cand2[:, t, :])
                dve.drain()
                for t in range(NT):
                    nc.vector.max_index(k.pos[:, t, 8:16], k.top[:, t, 8:16], k.cand2[:, t, :])
                nc.vector.tensor_tensor(tiles(k.top_v, TOPK), k.top[:, :, :], k.top[:, :, 0:1].to_broadcast([TP, NT, TOPK]),
                                        ALU.subtract).then_inc(top_exp_in, 1)
                dve.drain()
                nc.vector.tensor_copy(k.posf[:, :], k.pos[:, :, :].rearrange("p t n -> p (t n)"))
                dve.drain()
                for t in range(NT):
                    hot = k.hot[:, t * TOPK * NC_:(t + 1) * TOPK * NC_].rearrange("p (j c) -> p j c", c=NC_)
                    nc.vector.tensor_tensor(hot, bcast(k.posf[:, t * TOPK:(t + 1) * TOPK], NC_),
                                            k.place[:, :].unsqueeze(1).to_broadcast([TP, TOPK, NC_]), ALU.is_equal)
                dve.drain()
                for t in range(NT):
                    hot = k.hot[:, t * TOPK * NC_:(t + 1) * TOPK * NC_].rearrange("p (j c) -> p j c", c=NC_)
                    nc.vector.tensor_tensor(hot, hot, cidx[:, t:t + 1, :].to_broadcast([TP, TOPK, NC_]), ALU.mult)
                dve.drain()
                nc.vector.reduce_sum(k.idxf[:, :], k.hot[:, :].rearrange("p (j c) -> p j c", c=NC_), AXX)
                dve.drain()
                dve.wait_ge(top_exp, g + 1)
                nc.vector.reduce_sum(k.wsum[:, :], tiles(k.top_e, TOPK), AXX)
                dve.drain()
                nc.vector.reciprocal(k.wsum[:, :], k.wsum[:, :])
                dve.drain()
                nc.vector.tensor_tensor(tiles(k.w_next, TOPK), tiles(k.top_e, TOPK), bcast(k.wsum[:, :], TOPK), ALU.mult)
                dve.drain()

            def take_over(t):
                s = slice(t * TOPK, (t + 1) * TOPK)
                nc.vector.tensor_copy(k.w[:, s], k.w_next[:, s])
                nc.vector.tensor_copy(k.idx[:, s], k.idxf[:, s]).then_inc(chosen, 1)

            def attention(g, more):
                for m in range(NT + 2):
                    if m < NT:
                        dve.wait_ge(gathered[m], 16 * TOPK * (g + 1))
                        prod = k.prod[:, :].rearrange("p (j c) -> p j c", c=128)
                        nc.vector.tensor_tensor(prod, k.rows[m][:, :].rearrange("p (j c) -> p j c", c=128),
                                                bcast(k.w[:, m * TOPK:(m + 1) * TOPK], 128), ALU.mult)
                        dve.drain()
                        if more:
                            take_over(m)
                        nc.vector.reduce_sum(k.kv[:, m * 128:(m + 1) * 128], prod.rearrange("p j c -> p c j"), AXX)\
                            .then_inc(taken, 1)
                        dve.drain()
                    att.vector(dve, g, m)
                inverse_sums(nc, dve, k, 0, NT, True)
                dve.wait_ge(att.out_ready, NT * g + NT)
                nc.vector.tensor_tensor(tiles(k.tmp), tiles(k.PV[0:TP, 0:384]), bcast(k.rinv[:, 0:NT], D), ALU.mult)
                dve.drain()
                dve.wait_ge(acc_loaded, 16 * g + 16)
                nc.vector.tensor_tensor(k.h4[:, :], k.h4[:, :], k.tmp[:, :], ALU.add).then_inc(acc_ready, 1)
                dve.drain()

            for h in range(PH):
                nc.vector.memset(k.heads[:, h:h + 1], float(h * PKEYS * PKEYS))
            dve.drain()
            choose(0, 0)
            for t in range(NT):
                take_over(t)
            dve.drain()
            with dve.Fori(0, G - 1) as g:
                choose(g + 1, (g + 1) & 7)
                attention(g, True)
            attention(G - 1, False)



class Shared:
    pass


def build(nc, A, out):
    ctx = ExitStack()
    with ctx:
        def sb(name, shape, dt=FP):
            return ctx.enter_context(nc.sbuf_tensor(name, shape, dt))

        def sem(name):
            return ctx.enter_context(nc.semaphore(name))

        def eb(name, shape, dt=FP):
            return early.enter_context(nc.sbuf_tensor(name, shape, dt))

        k = Shared()
        ps = [ctx.enter_context(nc.psum_tensor(f"bank_pair_{i}", [128, 2, 512], FP)) for i in range(3)]
        k.S, k.T = ps[0:2], ps[2]
        k.S2 = ps[1]
        k.PV = ctx.enter_context(nc.psum_tensor("PV", [128, 512], FP))
        k.MI = ctx.enter_context(nc.psum_tensor("MI", [128, 512], FP))
        k.ident = sb("ident", [128, 128])
        k.ident_bf = sb("ident_bf", [128, 128], BF)
        k.causal = sb("causal", [TP, TP], BF)
        k.ones = sb("ones", [128, 128])
        k.minus_half = sb("minus_half", [128, 1])
        k.plus_half = sb("plus_half", [128, 1])
        k.place_i = sb("place_i", [TP, NC_], mybir.dt.int32)
        k.place = sb("place", [TP, NC_])
        k.WX = sb("WX", [11, 128])
        k.R3 = sb("R3", [11, 64])
        k.W2BD = sb("W2BD", [128, 128])
        k.W4 = sb("W4", [128, 64])
        k.WqN = sb("WqN", [64, 64])
        k.WkN = sb("WkN", [64, 64])
        k.WvT = sb("WvT", [64, 64])
        k.ATT0 = sb("ATT0", [64, 64])
        k.HLP = sb("HLP", [65, 128])
        k.HLT = sb("HLT", [65, 64])
        k.WVB = sb("WVB", [128, 64])
        k.wqb = sb("wqb", [128, NE, 128])
        k.wkb = sb("wkb", [128, 128])
        k.LB = sb("LB", [128, NE, 128])
        k.GW = sb("GW", [128, 2, 16])
        k.GB = sb("GB", [1, 16])
        k.FG = sb("FG", [64, 4])
        k.LNG = sb("LNG", [TP, 16])
        k.LNB = sb("LNB", [TP, 16])
        k.FNG = sb("FNG", [TP, 16])
        k.FNB = sb("FNB", [TP, 16])
        k.FC1 = sb("FC1", [65, 64])
        k.FC2 = sb("FC2", [65, 64])
        k.R2 = sb("R2", [65, 194])
        k.WB = sb("WB", [65, 128])
        k.NW = sb("NW", [65, 128])
        k.W1Tr = sb("W1Tr", [64, 64])
        k.WkT1 = sb("WkT1", [64, 64])
        k.WqT1 = sb("WqT1", [64, 64])
        k.R4 = sb("R4", [65, 128])
        k.grads = sb("grads", [65, 128])
        k.gsq = sb("gsq", [65, 128])
        k.gabs = sb("gabs", [65, 128])
        k.WPK = sb("WPK", [32, 1024])
        k.KPK = sb("KPK", [32, 1024])
        k.Mk = sb("Mk", [64, 1024])
        k.BD = sb("BD", [128, PH, 128])
        k.xT = sb("xT", [65, L])
        k.xT2 = sb("xT2", [65, L])
        k.xT3 = sb("xT3", [65, L])
        k.kT = sb("kT", [64, L])
        k.h1 = sb("h1", [TP, NT * D])
        k.h2 = sb("h2", [TP, NT * D])
        k.h3 = sb("h3", [TP, NT * D])
        k.h4 = sb("h4", [TP, NT * D])
        k.xn = sb("xn", [TP, NT * D])
        k.tmp = sb("tmp", [TP, NT * D])
        k.V = sb("V", [TP, NT * D])
        k.mix = sb("mix", [TP, NT * D])
        k.fx = sb("fx", [TP, NT * D])
        k.hx = sb("hx", [TP, NT * D])
        k.fout = sb("fout", [TP, NT * D])
        k.live = sb("live", [TP, NT * D])
        k.resid = sb("resid", [TP, NT * D])
        k.silu = sb("silu", [TP, NT * D])
        k.d0 = sb("d0", [TP, NT * D])
        k.dx = sb("dx", [TP, NT * D])
        k.dz0 = sb("dz0", [TP, NT * D])
        k.dz1 = sb("dz1", [TP, NT * D])
        k.E1 = sb("E1", [TP, NT * D])
        k.q1 = sb("q1", [TP, NT * D])
        k.ln_dev = sb("ln_dev", [TP, NT * D])
        k.ln_sq = sb("ln_sq", [TP, NT * D])
        k.ln_mean = sb("ln_mean", [TP, 24])
        k.ln_var = sb("ln_var", [TP, 24])
        k.ln_rstd = sb("ln_rstd", [TP, 24])
        k.P0 = sb("P0", [TP, L])
        k.P1 = sb("P1", [TP, L])
        k.PT0 = sb("PT0", [TP, L])
        k.PT1 = sb("PT1", [TP, L])
        k.P, k.PT = [k.P0, k.P1], [k.PT0, k.PT1]
        k.nmax = sb("nmax", [TP, 96])
        k.mtmp = sb("mtmp", [TP, 192])
        k.rsum = sb("rsum", [TP, 96])
        k.rsum2 = sb("rsum2", [TP, 96])
        k.rinv = sb("rinv", [TP, 96])
        k.table = nc.dram_tensor("table", [ROWS, 128], FP).ap()
        k.d_h2 = nc.dram_tensor("d_h2", [B, TP, NT * D], FP).ap()
        k.d_h3 = nc.dram_tensor("d_h3", [B, TP, NT * D], FP).ap()
        k.d_xT2 = nc.dram_tensor("d_xT2", [B, D, L], FP).ap()
        k.d_xT3 = nc.dram_tensor("d_xT3", [B, D, L], FP).ap()
        k.d_xT4 = nc.dram_tensor("d_xT4", [B, D, L], FP).ap()

        early = ctx.enter_context(ExitStack())
        k.xs = eb("xs", [11, L])
        k.U0 = eb("U0", [128, L + 2])
        k.U1 = eb("U1", [128, L + 2])
        k.UR = eb("UR", [128, L + 2])
        k.U = [k.U0, k.U1]
        k.sxT = eb("sxT", [128, L])
        k.UT = eb("UT", [128, NE, L])
        k.att = eb("att", [TP, NT, 256])
        k.big = eb("big", [TP, 1536])
        k.soft = eb("soft", [TP, 96])
        k.soft_exp = eb("soft_exp", [TP, 96])
        k.soft_m = eb("soft_m", [TP, 24])
        k.G = eb("G", [TP, NT, 194])
        k.E0 = eb("E0", [TP, NT, 65])
        k.x1 = eb("x1", [TP, NT, 65])
        k.alr = eb("alr", [TP, NT])
        k.rows_in = eb("rows_in", [128, 8, 128])
        k.rows_turned = eb("rows_turned", [128, 1024])
        k.rows_out = eb("rows_out", [128, 1024])

        for e in (nc.tensor, nc.gpsimd, nc.sync):
            PASSED[e.engine] = sem("waits_passed_" + str(e.engine).split(".")[-1])
        clear(nc, k)
        load_weights(nc, k, A, sem)
        weight_products(nc, k, sem)
        build_table(nc, k, A, sem)
        tok_and_attention(nc, k, A, sem)
        residuals(nc, k, A, sem)
        ffn_and_gradients(nc, k, A, sem)
        adamw(nc, k, sem)
        retrieve(nc, k, A, out, sem)
        early.close()
        k.sims = sb("sims", [TP, NT, 128])
        k.sims2 = sb("sims2", [TP, NT, 128])
        k.sc = sb("sc", [TP, NT * 32])
        k.ix = sb("ix", [TP, NT * 32], U32)
        k.ixf = sb("ixf", [TP, NT * 32])
        k.cand = sb("cand", [TP, NT * NC_])
        k.cidx = sb("cidx", [TP, NT * NC_])
        k.cand2 = sb("cand2", [TP, NT, NC_])
        k.top = sb("top", [TP, NT, TOPK])
        k.pos = sb("pos", [TP, NT, TOPK], U32)
        k.posf = sb("posf", [TP, NT * TOPK])
        k.top_v = sb("top_v", [TP, NT * TOPK])
        k.top_e = sb("top_e", [TP, NT * TOPK])
        k.hot = sb("hot", [TP, NT * TOPK * NC_])
        k.idxf = sb("idxf", [TP, NT * TOPK])
        k.wsum = sb("wsum", [TP, NT])
        k.w_next = sb("w_next", [TP, NT * TOPK])
        k.w = sb("w", [TP, NT * TOPK])
        k.idx = sb("idx", [TP, NT * TOPK], U32)
        k.gate = sb("gate", [TP, 1])
        k.heads = sb("heads", [TP, PH])
        k.head = sb("head", [TP, 1])
        k.prod = sb("prod", [TP, TOPK * 128])
        k.kv = sb("kv", [TP, NT * 128])
        k.rows = [sb(f"rows_{t}", [TP, TOPK * 128]) for t in range(NT)]
        product_key_attention(nc, k, out, sem)


def host_arrays(i):
    import numpy as np
    c = np.ascontiguousarray
    i = {n: np.asarray(v) for n, v in i.items()}
    f = {
        "x": c(i["x"]), "xr": c(i["x"][:, :, ::-1]),
        "W1T": c(i["L0_tok_W1"].T), "W2T": c(i["L0_tok_W2"].T), "W3T": c(i["L0_tok_W3"].T), "W4T": c(i["L0_tok_W4"].T),
        "b1": i["L0_tok_b1"][None], "b2": i["L0_tok_b2"][None], "b3": i["L0_tok_b3"][None], "b4": i["L0_tok_b4"][None],
        "attn_Wq": c(i["L0_attn_Wq"]), "attn_Wk": c(i["L0_attn_Wk"]), "attn_WvT": c(i["L0_attn_Wv"].T),
        "hlT": c(i["L0_ffn_hl_w"].reshape(64, 64).T), "hl_b": c(i["L0_ffn_hl_b"].reshape(1, 64)),
        "gwT": c(i["L0_ffn_gate_w"].transpose(0, 2, 1)), "gb": c(i["L0_ffn_gate_b"].reshape(1, 16)),
        "fgT": c(i["L0_ffn_fgate_w"].T), "wvT": c(i["L0_ffn_wv"].transpose(0, 2, 1)),
        "wq": c(i["L0_ffn_wq"]), "wk": c(i["L0_ffn_wk"]),
        "fc1T": c(i["L0_ffn_fc1_w"].T), "fc2T": c(i["L0_ffn_fc2_w"].T),
        "fc1_b": i["L0_ffn_fc1_b"][None], "fc2_b": i["L0_ffn_fc2_b"][None],
        "ln_g": i["L0_ffn_ln_g"][None], "ln_b": i["L0_ffn_ln_b"][None],
        "fn_g": i["L0_ffn_fnorm_g"][None], "fn_b": i["L0_ffn_fnorm_b"][None],
        "Wk1": c(i["L1_attn_Wk"]), "Wv1": c(i["L1_attn_Wv"]), "Wlr": c(i["L1_attn_Wlr"]), "Wq1": c(i["L1_attn_Wq"]),
        "blr": i["L1_attn_blr"][None], "Ws": c(i["L1_attn_Ws"]), "bs": c(i["L1_attn_bs"].reshape(1, 128)),
        "Ws1T": c(i["L1_attn_Ws"][1].T), "WkT1": c(i["L1_attn_Wk"].T), "WqT1": c(i["L1_attn_Wq"].T),
        "wpk": c(i["L1_ffn_Wq_pk"].reshape(64, 2, 8, 32).transpose(3, 1, 2, 0).reshape(32, 1024)),
        "kpk": c(i["L1_ffn_pk_keys"].transpose(3, 0, 2, 1).reshape(32, 1024)),
        "WqpT": c(i["L1_ffn_Wq"].T), "Wo": c(i["L1_ffn_Wo"]),
        "keys": c(i["L1_ffn_keys_table"]), "values": c(i["L1_ffn_values_table"]),
    }
    return {n: c(v) for n, v in f.items()}


def kernel(**inputs):
    import numpy as np
    import concourse.bacc as bacc
    from concourse.bass_utils import run_bass_kernel_spmd

    nc = bacc.Bacc("TRN2", target_bir_lowering=False, num_devices=1)
    arrays = host_arrays(inputs)
    aps = {n: nc.dram_tensor(f"in_{n}", a.shape, mybir.dt.from_np(a.dtype), kind="ExternalInput").ap()
           for n, a in arrays.items()}
    out = nc.dram_tensor("out_dram", (B, L, D), FP, kind="ExternalOutput").ap()
    build(nc, aps, out)
    r = run_bass_kernel_spmd(nc, [{f"in_{n}": a for n, a in arrays.items()}], core_ids=[0])
    return r.results[0]["out_dram"]
```

```python
import concourse.bass as bass
from concourse import mybir
from contextlib import ExitStack

FP = mybir.dt.float32
BF = mybir.dt.bfloat16
U32 = mybir.dt.uint32
ALU = mybir.AluOpType
ACT = mybir.ActivationFunctionType
AXX = mybir.AxisListType.X

B, CH, L, D = 16, 4, 750, 64
TP, NT = 125, 6
HALF = L // 2
STEPS = 8
NH, NE, HD = 4, 4, 16
PH, PKEYS, PDK, TOPK = 8, 64, 32, 16
ROWS = PH * PKEYS * PKEYS
NEG = -3.0e38
RUNS = [(0, 1, 16), (1, 1, 8), (2, 1, 5), (3, 1, 4), (4, 1, 3), (5, 3, 2), (8, 8, 1)]
NC_ = sum(n * m for _, n, m in RUNS)


PASSED = {}


def wait_apart(eng, semaphore, value):
    eng.wait_ge(semaphore, value)
    eng.sem_inc(PASSED[eng.engine], 1)


def bcast(ap, n):
    return ap.unsqueeze(2).to_broadcast([ap.shape[0], ap.shape[1], n])


def row(ap, i):
    return ap[bass.ds(i, 1), :, :].rearrange("a p n -> (a p) n")


def tokens(ap, b):
    return ap.rearrange("b (t p) d -> b p t d", p=TP)[bass.ds(b, 1), :, :, :].rearrange("a p t d -> (a p) t d")



def layernorm(nc, dve, k, src, dst, groups, width, eps, wait_rstd, done, scale=None, shift=None):
    dev, sq = k.ln_dev[0:TP, 0:groups * width].rearrange("p (g w) -> p g w", w=width), \
        k.ln_sq[0:TP, 0:groups * width].rearrange("p (g w) -> p g w", w=width)
    mean, var, rstd = k.ln_mean[0:TP, 0:groups], k.ln_var[0:TP, 0:groups], k.ln_rstd[0:TP, 0:groups]
    nc.vector.reduce_sum(mean, src, AXX)
    dve.drain()
    nc.vector.tensor_scalar_mul(mean, mean, 1.0 / width)
    dve.drain()
    nc.vector.tensor_tensor(dev, src, bcast(mean, width), ALU.subtract)
    dve.drain()
    nc.vector.tensor_tensor(sq, dev, dev, ALU.mult)
    dve.drain()
    nc.vector.reduce_sum(var, sq, AXX)
    dve.drain()
    nc.vector.tensor_scalar(var, var, 1.0 / width, eps, ALU.mult, ALU.add).then_inc(k.var_ready, 1)
    wait_rstd()
    if scale is None:
        nc.vector.tensor_tensor(dst, dev, bcast(rstd, width), ALU.mult).then_inc(done, 1)
    else:
        nc.vector.tensor_tensor(dev, dev, bcast(rstd, width), ALU.mult)
        dve.drain()
        nc.vector.tensor_tensor(dev, dev, scale[0:TP, :].unsqueeze(1).to_broadcast([TP, groups, width]), ALU.mult)
        dve.drain()
        nc.vector.tensor_tensor(dst, dev, shift[0:TP, :].unsqueeze(1).to_broadcast([TP, groups, width]), ALU.add)\
            .then_inc(done, 1)
    dve.drain()


def rsqrt(nc, pool, k, groups, n):
    pool.wait_ge(k.var_ready, n)
    nc.gpsimd.tensor_tensor(k.ln_rstd[0:TP, 0:groups], k.ln_var[0:TP, 0:groups],
                            k.minus_half[0:TP, 0:1].to_broadcast([TP, groups]), ALU.pow).then_inc(k.rstd_ready, 1)



class Attention:

    def __init__(self, nc, k, sem, name, units):
        self.nc, self.k, self.units = nc, k, units
        self.n = len(units)
        self.nb_second = [sum(u.nb > 3 for u in units[:m]) for m in range(len(units) + 1)]
        self.scores_ready = sem(name + "_scores_ready")
        self.max_ready = sem(name + "_max_ready")
        self.probs_ready = sem(name + "_probs_ready")
        self.first_turned = sem(name + "_first_turned")
        self.second_turned = sem(name + "_second_turned")
        self.first_copied = sem(name + "_first_copied")
        self.second_copied = sem(name + "_second_copied")
        self.out_ready = sem(name + "_out_ready")

    def tensor(self, pe, it, m):
        nc, k, N, units = self.nc, self.k, self.n, self.units
        base = it * N
        if m < N:
            u = units[m]
            if m >= 2:
                pe.wait_ge(self.probs_ready, base + m - 1)
            w = u.nb * TP
            parts = [(0, w)] if w <= 500 else [(0, 375), (375, w)]
            for h, (lo, hi) in enumerate(parts):
                diag = u.masked and hi == w
                last = nc.tensor.matmul(k.S[m % 2][0:TP, h, 0:hi - lo], u.q, u.keys[:, lo:hi],
                                        start=True, stop=not diag)
                if diag:
                    last = nc.tensor.matmul(k.S[m % 2][0:TP, h, hi - lo - TP:hi - lo], k.ident_bf[0:TP, 0:TP],
                                            k.causal[0:TP, :], start=False, stop=True)
            last.then_inc(self.scores_ready, 1)
        if 1 <= m <= N:
            n = m - 1
            u = units[n]
            pe.wait_ge(self.probs_ready, base + n + 1)
            if n >= 1:
                pe.wait_ge(self.first_copied, base + n)
            for b in range(min(3, u.nb)):
                last = nc.tensor.transpose(k.T[0:TP, 0, b * TP:(b + 1) * TP], k.P[n % 2][:, b * TP:(b + 1) * TP],
                                           k.ident[0:TP, 0:TP])
            last.then_inc(self.first_turned, 1)
            if u.nb > 3:
                if n >= 1:
                    pe.wait_ge(self.second_copied, it * self.nb_second[N] + self.nb_second[n])
                for b in range(3, u.nb):
                    last = nc.tensor.transpose(k.T[0:TP, 1, (b - 3) * TP:(b - 2) * TP],
                                               k.P[n % 2][:, b * TP:(b + 1) * TP], k.ident[0:TP, 0:TP])
                last.then_inc(self.second_turned, 1)
        if 2 <= m:
            n = m - 2
            u = units[n]
            pe.wait_ge(self.first_copied, base + n + 1)
            if u.nb > 3:
                pe.wait_ge(self.second_copied, it * self.nb_second[N] + self.nb_second[n + 1])
            for b in range(u.nb):
                last = nc.tensor.matmul(u.out, k.PT[n % 2][:, b * TP:(b + 1) * TP], u.value(b),
                                        start=b == 0, stop=b == u.nb - 1)
            last.then_inc(self.out_ready, 1)

    def vector(self, dve, it, m):
        nc, k, N = self.nc, self.k, self.n
        if m < N:
            u = self.units[m]
            dve.wait_ge(self.scores_ready, it * N + m + 1)
            minus_max(nc, dve, k, k.S[m % 2], m, u.nb * TP, self.max_ready)
        if 1 <= m <= N and self.units[m - 1].nb > 3:
            n = m - 1
            u = self.units[n]
            if n >= 2:
                dve.wait_ge(self.out_ready, it * N + n - 1)
            dve.wait_ge(self.second_turned, it * self.nb_second[N] + self.nb_second[m])
            w = (u.nb - 3) * TP
            nc.vector.tensor_copy(k.PT[n % 2][:, 375:375 + w], k.T[0:TP, 1, 0:w]).then_inc(self.second_copied, 1)

    def scalar(self, act, it, m):
        nc, k, N = self.nc, self.k, self.n
        if m < N:
            u = self.units[m]
            act.wait_ge(self.max_ready, it * N + m + 1)
            if m >= 2:
                act.wait_ge(self.first_turned, it * N + m - 1)
                if self.units[m - 2].nb > 3:
                    act.wait_ge(self.second_turned, it * self.nb_second[N] + self.nb_second[m - 1])
            exp_rows(nc, k, k.P[m % 2], 0, m, u.nb * TP, self.probs_ready)
        if 1 <= m <= N:
            n = m - 1
            u = self.units[n]
            if n >= 2:
                act.wait_ge(self.out_ready, it * N + n - 1)
            act.wait_ge(self.first_turned, it * N + m)
            w = min(3, u.nb) * TP
            nc.scalar.activation(k.PT[n % 2][:, 0:w], k.T[0:TP, 0, 0:w], ACT.Copy).then_inc(self.first_copied, 1)


class ExpertAttention:

    def __init__(self, nc, k, sem):
        self.nc, self.k = nc, k
        self.scores_ready, self.max_ready, self.probs_ready = \
            sem("a2_scores_ready"), sem("a2_max_ready"), sem("a2_probs_ready")
        self.turned, self.copied = sem("a2_turned"), [sem("a2_copied_by_act"), sem("a2_copied_by_dve")]
        self.used = sem("a2_probs_used")
        self.outT_ready, self.out_turned, self.kept = sem("a2_outT_ready"), sem("a2_out_turned"), sem("a2_kept")
        self.groups = [(i, n) for i in range(NT) for n in range(NH)]
        self.first_turn = [sum(i + 1 for i, _ in self.groups[:g]) for g in range(len(self.groups) + 1)]
        self.turns = self.first_turn[-1]

    def copies(self, b, t):
        return b * (self.turns // 2) + t // 2 + 1

    def scores(self, pe, b, g, e):
        nc, k = self.nc, self.k
        (i, n), u = self.groups[g], 4 * g + e
        if u >= 2:
            pe.wait_ge(self.probs_ready, 96 * b + u - 1)
        w = (i + 1) * TP
        for h, (lo, hi) in enumerate([(0, w)] if w <= 500 else [(0, 375), (375, w)]):
            last = nc.tensor.matmul(k.S[u % 2][0:TP, h, 0:hi - lo], k.UT[:, e, i * TP:(i + 1) * TP],
                                    k.sxn[:, n, lo:hi], start=True, stop=hi != w)
        last = nc.tensor.matmul(k.S[u % 2][0:TP, h, hi - lo - TP:hi - lo], k.ident_bf[0:TP, 0:TP],
                                k.causal[0:TP, :], start=False, stop=True)
        last.then_inc(self.scores_ready, 1)

    def turn(self, pe, b, g, j):
        nc, k, t = self.nc, self.k, self.first_turn[g] + j
        if t >= 2:
            pe.wait_ge(self.copied[t % 2], self.copies(b, t - 2))
        if j == 0:
            pe.wait_ge(self.probs_ready, 96 * b + 4 * g + 4)
        for e in range(NE):
            last = nc.tensor.transpose(k.T[0:TP, t % 2, e * TP:(e + 1) * TP],
                                       k.PG[g % 2][:, e * L + j * TP:e * L + (j + 1) * TP], k.ident[0:TP, 0:TP])
        last.then_inc(self.turned, 1)

    def product(self, pe, b, g, j):
        nc, k, t = self.nc, self.k, self.first_turn[g] + j
        i, n = self.groups[g]
        pe.wait_ge(self.copied[t % 2], self.copies(b, t))
        if n == 0 and j == 0 and i:
            pe.wait_ge(self.outT_ready, NT * b + i)
        nc.tensor.matmul(k.PV[:, 0:NE * TP], k.Vp[:, j, n, :], k.PTG[t % 2][:, :], start=n == 0 and j == 0,
                         stop=n == NH - 1 and j == i).then_inc(self.used, 1)

    def turn_out(self, pe, b, i):
        nc, k = self.nc, self.k
        if i:
            pe.wait_ge(self.kept, NT * b + i)
        pe.wait_ge(self.outT_ready, NT * b + i + 1)
        for e in range(NE):
            last = nc.tensor.transpose(k.MI[0:TP, e * 128:(e + 1) * 128], k.outT[:, e * TP:(e + 1) * TP],
                                       k.ident[:, :])
        last.then_inc(self.out_turned, 1)

    def tensor(self, pe, b):
        N = len(self.groups)
        for g in range(N + 1):
            nb = self.groups[g - 1][0] + 1 if g else 0
            for j in range(max(NE if g < N else 0, nb + 1)):
                if g < N and j < NE:
                    self.scores(pe, b, g, j)
                if j < nb:
                    self.turn(pe, b, g - 1, j)
                if 1 <= j <= nb:
                    self.product(pe, b, g - 1, j - 1)
                if j == 2 and g % NH == 1 and g > NH:
                    self.turn_out(pe, b, g // NH - 1)
        self.turn_out(pe, b, NT - 1)

    def scalar(self, act, b):
        nc, k, N = self.nc, self.k, len(self.groups)
        for g in range(N + 1):
            nb = self.groups[g - 1][0] + 1 if g else 0
            for j in range(max(NE if g < N else 0, nb)):
                if g < N and j < NE:
                    u, w, buf = 4 * g + j, (self.groups[g][0] + 1) * TP, k.PG[g % 2]
                    if j == 0 and g >= 2:
                        act.wait_ge(self.turned, b * self.turns + self.first_turn[g - 1])
                    act.wait_ge(self.max_ready, 96 * b + u + 1)
                    exp_rows(nc, k, buf, j * L, u, w, self.probs_ready)
                if j < nb:
                    self.copy(act, b, g - 1, j, 0)
            if g % NH == 0 and g:
                i = g // NH - 1
                if i:
                    act.wait_ge(self.out_turned, NT * b + i)
                act.wait_ge(self.used, b * self.turns + self.first_turn[g])
                nc.scalar.activation(k.outT[:, :], k.PV[:, 0:NE * TP], ACT.Copy).then_inc(self.outT_ready, 1)

    def copy(self, eng, b, g, j, mine):
        nc, k, t = self.nc, self.k, self.first_turn[g] + j
        if t % 2 != mine:
            return
        if t >= 2:
            eng.wait_ge(self.used, b * self.turns + t - 1)
        eng.wait_ge(self.turned, b * self.turns + t + 1)
        dst, src = k.PTG[t % 2][:, :], k.T[0:TP, t % 2, 0:NE * TP]
        if mine:
            nc.vector.tensor_copy(dst, src).then_inc(self.copied[1], 1)
        else:
            nc.scalar.activation(dst, src, ACT.Copy).then_inc(self.copied[0], 1)

    def vector(self, dve, b):
        nc, k, N = self.nc, self.k, len(self.groups)
        for g in range(N + 1):
            nb = self.groups[g - 1][0] + 1 if g else 0
            for j in range(max(NE if g < N else 0, nb)):
                if g < N and j < NE:
                    u, w = 4 * g + j, (self.groups[g][0] + 1) * TP
                    dve.wait_ge(self.scores_ready, 96 * b + u + 1)
                    minus_max(nc, dve, k, k.S[u % 2], u, w, self.max_ready)
                if j < nb:
                    self.copy(dve, b, g - 1, j, 1)
            if g % NH == 1 and g > NH:
                self.normalise(dve, b, g // NH - 1)
        self.normalise(dve, b, NT - 1)

    def normalise(self, dve, b, i):
        nc, k = self.nc, self.k
        dve.wait_ge(self.out_turned, NT * b + i + 1)
        inverse_sums(nc, dve, k, 16 * i, 16 * i + 16, i == 4)
        a4 = k.att[:, i, :].rearrange("p (n e d) -> p n e d", n=NH, e=NE)
        nc.vector.tensor_tensor(a4, k.MI[0:TP, :].rearrange("p (e n d) -> p n e d", e=NE, n=NH)[:, :, :, 0:HD],
                                k.rinv[:, 16 * i:16 * i + 16].rearrange("p (n e) -> p n e", n=NH).unsqueeze(3)
                                .to_broadcast([TP, NH, NE, HD]), ALU.mult)
        dve.drain()
        live = k.live[:, i * 64:(i + 1) * 64].rearrange("p (n d) -> p n d", n=NH).unsqueeze(2)\
            .to_broadcast([TP, NH, NE, HD])
        nc.vector.tensor_tensor(a4, a4, live, ALU.mult).then_inc(self.kept, 1)


def minus_max(nc, dve, k, scores, u, w, done):
    if w <= 500 or w == 750:
        src = scores[0:TP, 0, 0:w] if w <= 500 else scores[0:TP, :, 0:375]
        nc.vector.tensor_reduce(k.nmax[:, u:u + 1], src, AXX if w <= 500 else mybir.AxisListType.XY,
                                ALU.max, negate=True).then_inc(done, 1)
        return
    nc.vector.reduce_max(k.mtmp[:, 2 * u:2 * u + 1], scores[0:TP, 0, 0:375], AXX)
    nc.vector.reduce_max(k.mtmp[:, 2 * u + 1:2 * u + 2], scores[0:TP, 1, 0:w - 375], AXX)
    dve.drain()
    nc.vector.tensor_reduce(k.nmax[:, u:u + 1], k.mtmp[:, 2 * u:2 * u + 2], AXX, ALU.max, negate=True).then_inc(done, 1)


def exp_rows(nc, k, buf, at, u, w, done):
    bias, scores = k.nmax[:, u:u + 1], k.S[u % 2]
    if w <= 500 or w == 750:
        dst, src = buf[:, at:at + w], scores[0:TP, 0, 0:min(w, 500)]
        if w == 750:
            dst, src = dst.rearrange("p (h w) -> p h w", h=2), scores[0:TP, :, 0:375]
        nc.scalar.activation(dst, src, ACT.Exp, bias=bias, accum_out=k.rsum[:, u:u + 1]).then_inc(done, 1)
        return
    nc.scalar.activation(buf[:, at:at + 375], scores[0:TP, 0, 0:375], ACT.Exp, bias=bias, accum_out=k.rsum[:, u:u + 1])
    nc.scalar.activation(buf[:, at + 375:at + w], scores[0:TP, 1, 0:w - 375], ACT.Exp, bias=bias,
                         accum_out=k.rsum2[:, u:u + 1]).then_inc(done, 1)


class unit:

    def __init__(self, nb, q, keys, value, out, masked):
        self.nb, self.q, self.keys, self.value, self.out, self.masked = nb, q, keys, value, out, masked


def inverse_sums(nc, dve, k, lo, hi, split):
    if split:
        nc.vector.tensor_tensor(k.rinv[:, lo:hi], k.rsum[:, lo:hi], k.rsum2[:, lo:hi], ALU.add)
        dve.drain()
        nc.vector.reciprocal(k.rinv[:, lo:hi], k.rinv[:, lo:hi])
    else:
        nc.vector.reciprocal(k.rinv[:, lo:hi], k.rsum[:, lo:hi])
    dve.drain()



def clear(nc, k):
    with nc.Block() as block:
        @block.gpsimd
        def _(pool):
            nc.gpsimd.memset(k.minus_half[:, :], -0.5)
            nc.gpsimd.memset(k.plus_half[:, :], 0.5)
            nc.gpsimd.memset(k.ident[:, :], 0.0)
            nc.gpsimd.memset(k.ident_bf[:, :], 0.0)
            nc.gpsimd.memset(k.causal[:, :], 0.0)
            pool.drain()
            for m in (k.ident, k.ident_bf):
                nc.gpsimd.affine_select(out=m[:, :], in_=m[:, :], compare_op=ALU.not_equal, fill=1.0,
                                        base=0, pattern=[[-1, 128]], channel_multiplier=1)
            nc.gpsimd.affine_select(out=k.causal[:, :], in_=k.causal[:, :], compare_op=ALU.is_ge, fill=NEG,
                                    base=0, pattern=[[-1, TP]], channel_multiplier=1)
            nc.gpsimd.iota(k.place_i[:, :], pattern=[[1, NC_]], base=0, channel_multiplier=0)
            nc.gpsimd.memset(k.xs[:, :], 1.0)

        @block.vector
        def _(dve):
            for t in (k.W2BD, k.WX, k.R3, k.ATT0, k.WvT, k.HLP, k.HLT, k.WVB, k.GW, k.FC1, k.FC2, k.FG, k.R2, k.WB,
                      k.NW, k.W1Tr, k.R4, k.Mk, k.rsum2, k.wqb, k.wkb, k.BD, k.U[0], k.U[1], k.UR, k.grads, k.sxn,
                      k.Vp, k.kT):
                nc.vector.memset(t[:], 0.0)
            nc.vector.memset(k.ones[:, :], 1.0)
            for t in (k.xT, k.xT2, k.xT3):
                nc.vector.memset(t[64:128, :], 0.0)
            nc.vector.memset(k.x1[:, :, 64:65], 1.0)
            dve.drain()
            for t in (k.xT, k.xT2, k.xT3):
                nc.vector.memset(t[64:65, :], 1.0)
            nc.vector.memset(k.R2[64:65, 64:65], 1.0)


def load_weights(nc, k, A, sem):
    done = sem("weights_loaded")
    qkv = [
        (k.WX[0:4, 0:64], A["W1T"]), (k.WX[4:8, 64:128], A["W1T"]),
        (k.R3[0:4, :], A["W3T"]), (k.R3[8:9, :], A["b3"]), (k.R3[9:10, :], A["b4"]), (k.R3[10:11, :], A["b4"]),
        (k.W2BD[0:64, 0:64], A["W2T"]), (k.W2BD[64:128, 64:128], A["W2T"]),
        (k.W4[0:64, :], A["W4T"]), (k.W4[64:128, :], A["W4T"]),
        (k.WqN[:, :], A["attn_Wq"]), (k.WkN[:, :], A["attn_Wk"]), (k.WvT[0:64, :], A["attn_WvT"]),
        (k.HLT[0:64, :], A["hlT"]), (k.HLT[64:65, :], A["hl_b"]),
        (k.GW[0:64, 0, 0:4], A["gwT"][0]), (k.GW[64:128, 0, 4:8], A["gwT"][1]),
        (k.GW[0:64, 1, 8:12], A["gwT"][2]), (k.GW[64:128, 1, 12:16], A["gwT"][3]),
        (k.GB[:, :], A["gb"]), (k.FG[0:64, :], A["fgT"]),
        (k.R2[0:64, 0:64], A["Wk1"]), (k.R2[0:64, 129:193], A["Wv1"]), (k.R2[0:64, 193:194], A["Wlr"]),
        (k.R2[64:65, 193:194], A["blr"]),
        (k.WB[0:64, 0:64], A["Ws"][0]), (k.WB[0:64, 64:128], A["Ws"][1]),
        (k.WB[64:65, :], A["bs"]), (k.W1Tr[0:64, :], A["Ws1T"]), (k.WkT1[:, :], A["WkT1"]), (k.WqT1[:, :], A["WqT1"]),
        (k.R4[0:64, 0:64], A["Wq1"]), (k.WPK[:, :], A["wpk"]), (k.KPK[:, :], A["kpk"]),
    ]
    for j in range(2):
        for r, n in ((8, "b1"), (9, "b2")):
            qkv.append((k.WX[r:r + 1, 64 * j:64 * j + 64], A[n]))
    for n in range(NH):
        s = slice(16 * n, 16 * n + 16)
        p = slice(32 * n, 32 * n + 16)
        qkv += [(k.HLP[0:64, p], A["hlT"][:, s]), (k.HLP[64:65, p], A["hl_b"][:, s]),
                (k.WVB[p, s], A["wvT"][n]), (k.wkb[p, p], A["wk"][n]),
                (k.FC1[s, s], A["fc1T"]), (k.FC1[64:65, s], A["fc1_b"]),
                (k.FC2[s, s], A["fc2T"]), (k.FC2[64:65, s], A["fc2_b"])]
        qkv += [(k.wqb[p, e, p], A["wq"][n, e]) for e in range(NE)]
    for t, n in ((k.LNG, "ln_g"), (k.LNB, "ln_b"), (k.FNG, "fn_g"), (k.FNB, "fn_b")):
        qkv.append((t[:, :], A[n].to_broadcast([TP, 16])))
    for h in range(PH):
        qkv += [(k.BD[0:64, h, 0:64], A["WqpT"][64 * h:64 * h + 64, :]),
                (k.BD[64:128, h, 64:128], A["Wo"][64 * h:64 * h + 64, :])]
    with nc.Block() as block:
        @block.sync
        def _(sp):
            for dst, src in qkv[0::2]:
                sp.dma_start(dst, src).then_inc(done, 16)
            sp.wait_ge(done, 16 * len(qkv))

        @block.scalar
        def _(act):
            for dst, src in qkv[1::2]:
                act.dma_start(dst, src).then_inc(done, 16)


def weight_products(nc, k, sem):
    made, kept = sem("weight_products_made"), sem("weight_products_kept")
    with nc.Block() as block:
        @block.tensor
        def _(pe):
            nc.tensor.matmul(k.PV[0:64, 0:64], k.WkN[:, :], k.WqN[:, :], start=True, stop=True)
            nc.tensor.matmul(k.PV[0:64, 64:128], k.WkT1[:, :], k.WB[0:64, 0:64], start=True, stop=True).then_inc(made, 1)
            for e in range(NE):
                last = nc.tensor.matmul(k.MI[:, e * 128:(e + 1) * 128], k.wqb[:, e, :], k.wkb[:, :],
                                        start=True, stop=True)
            last.then_inc(made, 1)
            for h in range(PH):
                for p in range(2):
                    c = (h * 2 + p) * 64
                    last = nc.tensor.matmul(k.S[0][0:64, c // 512, c % 512:c % 512 + 64],
                                            k.WPK[:, (p * PH + h) * 64:(p * PH + h + 1) * 64],
                                            k.KPK[:, (p * PH + h) * 64:(p * PH + h + 1) * 64], start=True, stop=True)
            last.then_inc(made, 1)

        @block.vector
        def _(dve):
            dve.wait_ge(made, 1)
            nc.vector.tensor_copy(k.ATT0[0:64, :], k.PV[0:64, 0:64])
            nc.vector.tensor_copy(k.R2[0:64, 65:129], k.PV[0:64, 64:128])
            nc.vector.tensor_copy(k.R2[64:65, 65:129], k.WB[64:65, 0:64])
            dve.wait_ge(made, 2)
            nc.vector.tensor_scalar_mul(k.LB[:, :, :], k.MI[:, :].rearrange("p (e c) -> p e c", e=NE), HD ** 0.5)
            dve.wait_ge(made, 3)
            nc.vector.tensor_copy(k.Mk[0:64, :].rearrange("p (a c) -> p a c", a=2), k.S[0][0:64, :, :])
            nc.vector.tensor_copy(k.place[:, :], k.place_i[:, :])
            nc.vector.tensor_scalar_mul(k.BD[0:64, :, :], k.BD[0:64, :, :], D ** -0.5)


def build_table(nc, k, A, sem):
    loaded, stored = sem("rows_loaded"), sem("rows_stored")
    turned, turned_kept = sem("rows_turned"), sem("turned_rows_kept")
    mapped, mapped_kept = sem("rows_mapped"), sem("mapped_rows_kept")
    N = ROWS // 1024
    with nc.Block() as block:
        @block.sync
        def _(sp):
            with sp.Fori(0, N) as i:
                sp.wait_ge(turned, i)
                for c, n in ((0, "keys"), (64, "values")):
                    src = A[n].rearrange("(i p j) d -> i p j d", p=128, j=8)[bass.ds(i, 1), :, :, :]
                    sp.dma_start(k.rows_in[:, :, c:c + 64], src.rearrange("a p j d -> (a p) j d")).then_inc(loaded, 16)
                sp.wait_ge(mapped_kept, 2 * i + 2)
                dst = k.table.rearrange("(i p j) d -> i p (j d)", p=128, j=8)
                sp.dma_start(row(dst, i), k.rows_out[:, :]).then_inc(stored, 16)
            sp.wait_ge(stored, 16 * N)

        @block.tensor
        def _(pe):
            with pe.Fori(0, N) as i:
                pe.wait_ge(loaded, 32 * i + 32)
                pe.wait_ge(turned_kept, 2 * i)
                for j in range(8):
                    last = nc.tensor.transpose(k.S[0][:, j // 4, (j % 4) * 128:(j % 4 + 1) * 128],
                                               k.rows_in[:, j, :], k.ident[:, :])
                last.then_inc(turned, 1)
                pe.wait_ge(turned_kept, 2 * i + 2)
                pe.wait_ge(mapped_kept, 2 * i)
                for j in range(8):
                    last = nc.tensor.matmul(k.S[1][:, j // 4, (j % 4) * 128:(j % 4 + 1) * 128],
                                            k.rows_turned[:, j * 128:(j + 1) * 128],
                                            k.BD[:, :, :].rearrange("p h c -> p (h c)")[:, bass.ds(((i >> 2) & (PH - 1)) * 128, 128)],
                                            start=True, stop=True)
                last.then_inc(mapped, 1)

        @block.scalar
        def _(act):
            with act.Fori(0, N) as i:
                act.wait_ge(turned, i + 1)
                act.wait_ge(mapped, i)
                nc.scalar.activation(k.rows_turned[:, 0:512], k.S[0][:, 0, :], ACT.Copy).then_inc(turned_kept, 1)
                act.wait_ge(mapped, i + 1)
                act.wait_ge(stored, 16 * i)
                nc.scalar.activation(k.rows_out[:, 0:512], k.S[1][:, 0, :], ACT.Copy).then_inc(mapped_kept, 1)

        @block.vector
        def _(dve):
            with dve.Fori(0, N) as i:
                dve.wait_ge(turned, i + 1)
                dve.wait_ge(mapped, i)
                nc.vector.tensor_copy(k.rows_turned[:, 512:1024], k.S[0][:, 1, :]).then_inc(turned_kept, 1)
                dve.wait_ge(mapped, i + 1)
                dve.wait_ge(stored, 16 * i)
                nc.vector.tensor_copy(k.rows_out[:, 512:1024], k.S[1][:, 1, :]).then_inc(mapped_kept, 1)



def tok_and_attention(nc, k, A, sem):
    xs_loaded, tok_products, tok_done = sem("xs_loaded"), sem("tok_products"), sem("tok_steps_done")
    tok_out, h1_ready, xn_ready = sem("tok_out"), sem("h1_ready"), sem("xn1_ready")
    xn_turned, xT_ready, kT_made, kT_ready = sem("xn1_turned"), sem("xT1_ready"), sem("kT1_made"), sem("kT1_ready")
    v_made, v_ready, h2_ready = sem("v1_made"), sem("v1_ready"), sem("h2_ready")
    xn2_ready, xn2_turned, xT2_ready = sem("xn2_ready"), sem("xn2_turned"), sem("xT2_ready")
    h2_stored, xT2_stored = sem("h2_stored"), sem("xT2_stored")
    k.var_ready, k.rstd_ready = sem("p1_var_ready"), sem("p1_rstd_ready")
    INCS = 2 * (STEPS - 1) + 4
    units = [unit(NT, k.xT[:, t * TP:(t + 1) * TP], k.kT[:, :],
                  lambda b: k.V[:, b * 64:(b + 1) * 64], k.PV[0:TP, t * 64:(t + 1) * 64], False) for t in range(NT)]
    att = Attention(nc, k, sem, "a1", units)
    with nc.Block() as block:
        @block.sync
        def _(sp):
            with sp.Fori(0, B) as b:
                sp.wait_ge(tok_out, b)
                sp.dma_start(k.xs[0:4, :], row(A["x"], b)).then_inc(xs_loaded, 16)
                sp.dma_start(k.xs[4:8, :], row(A["xr"], b)).then_inc(xs_loaded, 16)
                sp.wait_ge(h2_ready, b + 1)
                sp.dma_start(row(k.d_h2, b), k.h2[:, :]).then_inc(h2_stored, 16)
                sp.wait_ge(xT2_ready, b + 1)
                sp.dma_start(row(k.d_xT2, b), k.xT2[0:64, :]).then_inc(xT2_stored, 16)
            sp.wait_ge(h2_stored, 16 * B)
            sp.wait_ge(xT2_stored, 16 * B)

        @block.tensor
        def _(pe):
            with pe.Fori(0, B) as b:
                pe.wait_ge(xs_loaded, 32 * b + 32)
                for s in range(STEPS):
                    for h in range(2):
                        out = k.S[s % 2][:, h, 0:HALF]
                        last = nc.tensor.matmul(out, k.WX[:, :], k.xs[:, h * HALF:(h + 1) * HALF],
                                                start=True, stop=s == 0)
                        if s:
                            pe.wait_ge(tok_done, b * INCS + 2 * s - 1 + h)
                            last = nc.tensor.matmul(out, k.W2BD[:, :], k.U[(s - 1) % 2][:, h * HALF:(h + 1) * HALF],
                                                    start=False, stop=True)
                        last.then_inc(tok_products, 1)
                pe.wait_ge(tok_done, b * INCS + INCS)
                for t in range(NT):
                    out, cols = k.PV[0:TP, t * 64:(t + 1) * 64], slice(t * TP, (t + 1) * TP)
                    nc.tensor.matmul(out, k.xs[:, cols], k.R3[:, :], start=True, stop=False)
                    last = nc.tensor.matmul(out, k.UR[:, cols], k.W4[:, :], start=False, stop=True)
                last.then_inc(tok_out, 1)
                wait_apart(pe, xn_ready, b + 1)
                turn(nc, k, k.xn)
                k.turned_last.then_inc(xn_turned, 1)
                wait_apart(pe, xT_ready, b + 1)
                for h in range(2):
                    last = nc.tensor.matmul(k.S[1][0:64, h, 0:HALF], k.ATT0[:, :], k.xT[:, h * HALF:(h + 1) * HALF],
                                            start=True, stop=True)
                last.then_inc(kT_made, 1)
                for t in range(NT):
                    last = nc.tensor.matmul(k.MI[0:TP, t * 64:(t + 1) * 64], k.xT[:, t * TP:(t + 1) * TP],
                                            k.WvT[:, :], start=True, stop=True)
                last.then_inc(v_made, 1)
                pe.wait_ge(kT_ready, b + 1)
                pe.wait_ge(v_ready, b + 1)
                for m in range(NT + 2):
                    att.tensor(pe, b, m)
                wait_apart(pe, xn2_ready, b + 1)
                turn(nc, k, k.xn)
                k.turned_last.then_inc(xn2_turned, 1)

        @block.scalar
        def _(act):
            with act.Fori(0, B) as b:
                for s in range(STEPS - 1):
                    for h in range(2):
                        act.wait_ge(tok_products, b * 2 * STEPS + 2 * s + h + 1)
                        nc.scalar.activation(k.U[s % 2][:, 1 + h * HALF:1 + (h + 1) * HALF],
                                             k.S[s % 2][:, h, 0:HALF], ACT.Relu).then_inc(tok_done, 1)
                s = STEPS - 1
                act.wait_ge(tok_products, b * 2 * STEPS + 2 * s + 2)
                for h in range(2):
                    nc.scalar.activation(k.UR[0:64, 1 + h * HALF:1 + (h + 1) * HALF],
                                         k.S[1][0:64, h, 0:HALF], ACT.Relu).then_inc(tok_done, 1)
                nc.scalar.activation(k.UR[64:128, 0:HALF - 1], k.S[1][64:128, 1, HALF - 2::-1], ACT.Relu)\
                    .then_inc(tok_done, 1)
                nc.scalar.activation(k.UR[64:128, HALF - 1:L - 1], k.S[1][64:128, 0, HALF - 1::-1], ACT.Relu)\
                    .then_inc(tok_done, 1)
                act.wait_ge(tok_out, b + 1)
                nc.scalar.activation(k.h1[:, :], k.PV[0:TP, 0:384], ACT.Relu).then_inc(h1_ready, 1)
                act.wait_ge(xn_turned, b + 1)
                nc.scalar.activation(halves(k.xT[0:64, :]), k.T[0:64, :, 0:HALF], ACT.Copy).then_inc(xT_ready, 1)
                act.wait_ge(kT_made, b + 1)
                nc.scalar.activation(halves(k.kT[0:64, :]), k.S[1][0:64, :, 0:HALF], ACT.Copy).then_inc(kT_ready, 1)
                for m in range(NT + 2):
                    att.scalar(act, b, m)
                act.wait_ge(xn2_turned, b + 1)
                act.wait_ge(xT2_stored, 16 * b)
                nc.scalar.activation(halves(k.xT2[0:64, :]), k.T[0:64, :, 0:HALF], ACT.Copy).then_inc(xT2_ready, 1)

        @block.gpsimd
        def _(pool):
            with pool.Fori(0, B) as b:
                for n in range(2):
                    rsqrt(nc, pool, k, NT, b * 2 + n + 1)

        @block.vector
        def _(dve):
            with dve.Fori(0, B) as b:
                dve.wait_ge(h1_ready, b + 1)
                layernorm(nc, dve, k, tiles(k.h1), tiles(k.xn), NT, D, 1e-5,
                          lambda: dve.wait_ge(k.rstd_ready, 2 * b + 1), xn_ready)
                dve.wait_ge(v_made, b + 1)
                nc.vector.tensor_copy(k.V[:, :], k.MI[0:TP, 0:384]).then_inc(v_ready, 1)
                for m in range(NT + 2):
                    att.vector(dve, b, m)
                inverse_sums(nc, dve, k, 0, NT, False)
                dve.wait_ge(att.out_ready, NT * b + NT)
                nc.vector.tensor_tensor(tiles(k.tmp), tiles(k.PV[0:TP, 0:384]), bcast(k.rinv[:, 0:NT], D), ALU.mult)
                dve.drain()
                dve.wait_ge(h2_stored, 16 * b)
                nc.vector.scalar_tensor_tensor(k.h2[:, :], k.tmp[:, :], D ** -0.5, k.h1[:, :], ALU.mult, ALU.add)\
                    .then_inc(h2_ready, 1)
                dve.drain()
                layernorm(nc, dve, k, tiles(k.h2), tiles(k.xn), NT, D, 1e-5,
                          lambda: dve.wait_ge(k.rstd_ready, 2 * b + 2), xn2_ready)


def tiles(ap, w=D):
    ap = ap if isinstance(ap, bass.AP) else ap[:, :]
    return ap.rearrange("p (t w) -> p t w", w=w)


def halves(ap):
    return ap.rearrange("p (h w) -> p h w", h=2)


def turn(nc, k, src):
    for t in range(NT):
        k.turned_last = nc.tensor.transpose(k.T[0:64, t // 3, (t % 3) * TP:(t % 3 + 1) * TP],
                                            src[:, t * 64:(t + 1) * 64], k.ident[0:TP, 0:TP])



def residuals(nc, k, A, sem):
    loaded, made, kept = sem("resid_x_loaded"), sem("resid_made"), sem("resid_kept")
    with nc.Block() as block:
        @block.sync
        def _(sp):
            for n in range(NH):
                sp.wait_ge(made, n)
                sp.dma_start(k.xT2[0:64, :], k.d_xT2[n]).then_inc(loaded, 16)

        @block.tensor
        def _(pe):
            for n in range(NH):
                pe.wait_ge(loaded, 16 * n + 16)
                pe.wait_ge(kept, n)
                for t in range(NT):
                    last = nc.tensor.matmul(k.MI[0:TP, t * 16:(t + 1) * 16], k.xT2[:, t * TP:(t + 1) * TP],
                                            k.HLT[:, n * 16:(n + 1) * 16], start=True, stop=True)
                last.then_inc(made, 1)

        @block.vector
        def _(dve):
            for n in range(NH):
                dve.wait_ge(made, n + 1)
                nc.vector.tensor_copy(tiles(k.resid)[:, :, n * 16:(n + 1) * 16], tiles(k.MI[0:TP, 0:96], 16))\
                    .then_inc(kept, 1)


def softmax4(nc, dve, k, logits, groups, exp_in, exp_done, n):
    g, e = k.soft[:, 0:groups * 4].rearrange("p (g e) -> p g e", e=4), \
        k.soft_exp[:, 0:groups * 4].rearrange("p (g e) -> p g e", e=4)
    nc.vector.reduce_max(k.soft_m[:, 0:groups], logits, AXX)
    dve.drain()
    nc.vector.tensor_tensor(g, logits, bcast(k.soft_m[:, 0:groups], 4), ALU.subtract).then_inc(exp_in, 1)
    dve.wait_ge(exp_done, n)
    nc.vector.reduce_sum(k.soft_m[:, 0:groups], e, AXX)
    dve.drain()
    nc.vector.reciprocal(k.soft_m[:, 0:groups], k.soft_m[:, 0:groups])
    dve.drain()
    nc.vector.tensor_tensor(g, e, bcast(k.soft_m[:, 0:groups], 4), ALU.mult)
    dve.drain()


def sigmoid_of_exp(nc, dve, dst, e):
    nc.vector.tensor_scalar_add(dst, e, 1.0)
    dve.drain()
    nc.vector.reciprocal(dst, dst)
    dve.drain()


def r2_place(k, t):
    bank = (k.S[0][:, 0, :], k.S[0][:, 1, :], k.S[1][:, 0, :])[t // 2]
    return bank[0:TP, (t % 2) * 194:(t % 2 + 1) * 194]


def ffn_and_gradients(nc, k, A, sem):
    h2_loaded, x_loaded, sxT_made, sxT_ready = sem("h2_loaded"), sem("xT2_loaded"), sem("sxT_made"), sem("sxT_ready")
    sx_made, sx_ready, u_made, u_ready = sem("sx_made"), sem("sx_ready"), sem("u_made"), sem("u_ready")
    v_made, v_ready, sxn_ready = sem("v2_made"), sem("v2_ready"), sem("sx_by_head_ready")
    att_turned, attT_ready, gate_made = sem("att_turned"), sem("attT_ready"), sem("gate_made")
    soft_in, soft_exp = sem("soft_in"), sem("soft_exp")
    src_ready, turned, turned_kept = sem("p2_turn_source"), sem("p2_turned"), sem("p2_turned_kept")
    fc1_made, fc2_made, fg_made, r2_made = sem("fc1_made"), sem("fc2_made"), sem("fgate_made"), sem("r2_made")
    g_ready, z1_made, e1_ready, dx_made = sem("x0_ready"), sem("z1_made"), sem("e1_ready"), sem("dx_made")
    dz0_ready, grads_made, grads_kept = sem("dz0_ready"), sem("grads_made"), sem("grads_kept")
    h3_ready, h3_stored, xT3_stored = sem("h3_ready"), sem("h3_stored"), sem("xT3_stored")
    k.var_ready, k.rstd_ready = sem("p2_var_ready"), sem("p2_rstd_ready")
    att = ExpertAttention(nc, k, sem)
    TURNS = 6
    with nc.Block() as block:
        @block.sync
        def _(sp):
            with sp.Fori(0, B) as b:
                sp.wait_ge(u_ready, 4 * b)
                sp.dma_start(k.xT2[0:64, :], row(k.d_xT2, b)).then_inc(x_loaded, 16)
                sp.wait_ge(h3_ready, b)
                sp.dma_start(k.h2[:, :], row(k.d_h2, b)).then_inc(h2_loaded, 16)
                sp.wait_ge(h3_ready, b + 1)
                sp.dma_start(row(k.d_h3, b), k.h3[:, :]).then_inc(h3_stored, 16)
                sp.wait_ge(turned_kept, TURNS * b + 4)
                sp.dma_start(row(k.d_xT3, b), k.xT3[0:64, :]).then_inc(xT3_stored, 16)
            sp.wait_ge(h3_stored, 16 * B)
            sp.wait_ge(xT3_stored, 16 * B)

        @block.tensor
        def _(pe):
            def turned_of(b, n, src):
                wait_apart(pe, src_ready, TURNS * b + n)
                turn(nc, k, src)
                k.turned_last.then_inc(turned, 1)
                pe.wait_ge(turned_kept, TURNS * b + n)

            def per_tile(weights, width, x, done):
                for t in range(NT):
                    last = nc.tensor.matmul(k.MI[0:TP, t * width:(t + 1) * width], x[:, t * TP:(t + 1) * TP],
                                            weights, start=True, stop=True)
                last.then_inc(done, 1)

            with pe.Fori(0, B) as b:
                pe.wait_ge(x_loaded, 16 * b + 16)
                for h in range(2):
                    last = nc.tensor.matmul(k.S[0][:, h, 0:HALF], k.HLP[:, :], k.xT2[:, h * HALF:(h + 1) * HALF],
                                            start=True, stop=True)
                last.then_inc(sxT_made, 1)
                per_tile(k.HLT[:, :], 64, k.xT2, sx_made)
                pe.wait_ge(sxT_ready, b + 1)
                for e in range(NE):
                    if e >= 2:
                        pe.wait_ge(u_ready, 4 * b + e - 1)
                    for h in range(2):
                        last = nc.tensor.matmul(k.S[(e + 1) % 2][:, h, 0:HALF], k.LB[:, e, :],
                                                k.sxT[:, h * HALF:(h + 1) * HALF], start=True, stop=True)
                    last.then_inc(u_made, 1)
                pe.wait_ge(sx_ready, b + 1)
                per_tile(k.WVB[:, :], 64, k.sxT, v_made)
                pe.wait_ge(u_ready, 4 * b + 4)
                pe.wait_ge(v_ready, b + 1)
                pe.wait_ge(sxn_ready, b + 1)
                att.tensor(pe, b)
                pe.wait_ge(att.kept, NT * b + NT)
                for c in range(2):
                    for t in range(NT):
                        last = nc.tensor.transpose(k.S[c][:, t // 3, (t % 3) * TP:(t % 3 + 1) * TP],
                                                   k.att[:, t, c * 128:(c + 1) * 128], k.ident[0:TP, 0:TP])
                last.then_inc(att_turned, 1)
                pe.wait_ge(attT_ready, b + 1)
                for t in range(NT):
                    out, cols = k.MI[0:TP, t * 16:(t + 1) * 16], slice(t * TP, (t + 1) * TP)
                    nc.tensor.matmul(out, k.ones[0:1, 0:TP], k.GB[:, :], start=True, stop=False)
                    nc.tensor.matmul(out, k.UT[:, 0, cols], k.GW[:, 0, :], start=False, stop=False)
                    last = nc.tensor.matmul(out, k.UT[:, 1, cols], k.GW[:, 1, :], start=False, stop=True)
                last.then_inc(gate_made, 1)
                turned_of(b, 1, k.fx)
                per_tile(k.FC1[:, :], 64, k.xT, fc1_made)
                turned_of(b, 2, k.hx)
                per_tile(k.FC2[:, :], 64, k.xT, fc2_made)
                turned_of(b, 3, k.fout)
                per_tile(k.FG[:, :], 4, k.xT, fg_made)
                turned_of(b, 4, k.xn)
                for t in range(NT):
                    last = nc.tensor.matmul(r2_place(k, t), k.xT3[:, t * TP:(t + 1) * TP], k.R2[:, :],
                                            start=True, stop=True)
                last.then_inc(r2_made, 1)
                wait_apart(pe, src_ready, TURNS * b + 5)
                for t in range(NT):
                    last = nc.tensor.transpose(k.T[0:64, t // 3, (t % 3) * TP:(t % 3 + 1) * TP],
                                               k.x1[:, t, 0:64], k.ident[0:TP, 0:TP])
                last.then_inc(turned, 1)
                pe.wait_ge(turned_kept, TURNS * b + 5)
                per_tile(k.WB[:, 64:128], 64, k.xT, z1_made)
                turned_of(b, 6, k.dz1)
                per_tile(k.W1Tr[:, :], 64, k.xT, dx_made)
                pe.wait_ge(dz0_ready, b + 1)
                for t in range(NT):
                    nc.tensor.matmul(k.PV[0:65, 0:64], k.G[:, t, 0:65], k.dz0[:, t * 64:(t + 1) * 64],
                                     start=t == 0, stop=t == NT - 1)
                for t in range(NT):
                    last = nc.tensor.matmul(k.PV[0:65, 64:128], k.x1[:, t, :], k.dz1[:, t * 64:(t + 1) * 64],
                                            start=t == 0, stop=t == NT - 1)
                last.then_inc(grads_made, 1)
                pe.wait_ge(grads_kept, b + 1)

        @block.scalar
        def _(act):
            def keep_turned(b, n, dst):
                act.wait_ge(turned, TURNS * b + n)
                nc.scalar.activation(halves(dst[0:64, :]), k.T[0:64, :, 0:HALF], ACT.Copy).then_inc(turned_kept, 1)

            with act.Fori(0, B) as b:
                act.wait_ge(sxT_made, b + 1)
                nc.scalar.activation(halves(k.sxT[:, :]), k.S[0][:, :, 0:HALF], ACT.Copy).then_inc(sxT_ready, 1)
                for e in range(NE):
                    act.wait_ge(u_made, 4 * b + e + 1)
                    nc.scalar.activation(halves(k.UT[:, e, :]), k.S[(e + 1) % 2][:, :, 0:HALF], ACT.Copy)\
                        .then_inc(u_ready, 1)
                att.scalar(act, b)
                act.wait_ge(att_turned, b + 1)
                nc.scalar.activation(halves(k.UT[:, 0, :]), k.S[0][:, :, 0:HALF], ACT.Copy)
                nc.scalar.activation(halves(k.UT[:, 1, :]), k.S[1][:, :, 0:HALF], ACT.Copy).then_inc(attT_ready, 1)
                act.wait_ge(soft_in, 2 * b + 1)
                nc.scalar.activation(k.soft_exp[:, 0:96], k.soft[:, 0:96], ACT.Exp).then_inc(soft_exp, 1)
                for n in (1, 2, 3):
                    keep_turned(b, n, k.xT)
                act.wait_ge(soft_in, 2 * b + 2)
                nc.scalar.activation(k.soft_exp[:, 0:24], k.soft[:, 0:24], ACT.Exp).then_inc(soft_exp, 1)
                act.wait_ge(xT3_stored, 16 * b)
                keep_turned(b, 4, k.xT3)
                act.wait_ge(r2_made, b + 1)
                for c in range(3):
                    src = (k.S[0][0:TP, 0, :], k.S[0][0:TP, 1, :], k.S[1][0:TP, 0, :])[c][:, 0:388]\
                        .rearrange("p (a w) -> p a w", a=2)
                    nc.scalar.activation(k.G[:, 2 * c:2 * c + 2, :], src, ACT.Copy)
                    last = nc.scalar.activation(k.E0[:, 2 * c:2 * c + 2, 0:64], src[:, :, 65:129], ACT.Exp, scale=-1.0)
                    last = nc.scalar.activation(k.E0[:, 2 * c:2 * c + 2, 64:65], src[:, :, 193:194], ACT.Exp, scale=-1.0)
                last.then_inc(g_ready, 1)
                keep_turned(b, 5, k.xT)
                act.wait_ge(z1_made, b + 1)
                nc.scalar.activation(k.E1[:, :], k.MI[0:TP, 0:384], ACT.Exp, scale=-1.0).then_inc(e1_ready, 1)
                keep_turned(b, 6, k.xT)

        @block.gpsimd
        def _(pool):
            with pool.Fori(0, B) as b:
                wait_apart(pool, sxT_ready, b + 1)
                for n in range(NH):
                    p = slice(32 * n, 32 * n + 16)
                    last = nc.gpsimd.tensor_copy(k.sxn[p, n, :], k.sxT[p, :])
                last.then_inc(sxn_ready, 1)
                rsqrt(nc, pool, k, NT * NH, 3 * b + 1)
                rsqrt(nc, pool, k, NT * NH, 3 * b + 2)
                rsqrt(nc, pool, k, NT, 3 * b + 3)

        @block.vector
        def _(dve):
            with dve.Fori(0, B) as b:
                dve.wait_ge(sx_made, b + 1)
                nc.vector.tensor_scalar(k.live[:, :], k.MI[0:TP, 0:384], 0.0, None, ALU.not_equal).then_inc(sx_ready, 1)
                dve.wait_ge(v_made, b + 1)
                for n in range(NH):
                    last = nc.vector.tensor_copy(k.Vp[:, :, n, 32 * n:32 * n + 16],
                                                 tiles(k.MI[0:TP, 0:384])[:, :, 16 * n:16 * n + 16])
                last.then_inc(v_ready, 1)
                att.vector(dve, b)
                dve.drain()
                dve.wait_ge(gate_made, b + 1)
                softmax4(nc, dve, k, k.MI[0:TP, 0:96].rearrange("p (g e) -> p g e", e=4), 24, soft_in, soft_exp, 2 * b + 1)
                nc.vector.tensor_tensor(k.big[:, :].rearrange("p (a d) -> p a d", d=16),
                                        k.att[:, :, :].rearrange("p t (a d) -> p (t a) d", d=16),
                                        bcast(k.soft[:, 0:96], 16), ALU.mult)
                dve.drain()
                nc.vector.reduce_sum(tiles(k.mix, 16), k.big[:, :].rearrange("p (g e d) -> p g d e", e=NE, d=HD), AXX)
                dve.drain()
                nc.vector.tensor_tensor(k.mix[:, :], k.mix[:, :], k.resid[:, :], ALU.add)
                dve.drain()
                layernorm(nc, dve, k, tiles(k.mix, 16), tiles(k.fx, 16), 24, 16, 1e-8,
                          lambda: dve.wait_ge(k.rstd_ready, 3 * b + 1), src_ready, k.LNG, k.LNB)
                nc.vector.tensor_scalar(k.live[:, :], k.fx[:, :], 0.0, None, ALU.not_equal)
                dve.drain()
                dve.wait_ge(fc1_made, b + 1)
                nc.vector.scalar_tensor_tensor(k.hx[:, :], k.MI[0:TP, 0:384], 0.0, k.live[:, :], ALU.max, ALU.mult)\
                    .then_inc(src_ready, 1)
                dve.wait_ge(fc2_made, b + 1)
                nc.vector.tensor_tensor(k.mix[:, :], k.MI[0:TP, 0:384], k.live[:, :], ALU.mult)
                dve.drain()
                nc.vector.tensor_tensor(k.mix[:, :], k.mix[:, :], k.fx[:, :], ALU.add)
                dve.drain()
                layernorm(nc, dve, k, tiles(k.mix, 16), tiles(k.fout, 16), 24, 16, 1e-8,
                          lambda: dve.wait_ge(k.rstd_ready, 3 * b + 2), src_ready, k.FNG, k.FNB)
                dve.wait_ge(fg_made, b + 1)
                softmax4(nc, dve, k, k.MI[0:TP, 0:24].rearrange("p (g e) -> p g e", e=4), NT, soft_in, soft_exp, 2 * b + 2)
                nc.vector.tensor_tensor(tiles(k.mix, 16), tiles(k.fout, 16), bcast(k.soft[:, 0:24], 16), ALU.mult)
                dve.drain()
                dve.wait_ge(h3_stored, 16 * b)
                dve.wait_ge(h2_loaded, 16 * b + 16)
                nc.vector.tensor_tensor(k.h3[:, :], k.mix[:, :], k.h2[:, :], ALU.add).then_inc(h3_ready, 1)
                dve.drain()
                layernorm(nc, dve, k, tiles(k.h3), tiles(k.xn), NT, D, 1e-5,
                          lambda: dve.wait_ge(k.rstd_ready, 3 * b + 3), src_ready)
                dve.wait_ge(g_ready, b + 1)
                x0, z0, tgt = k.G[:, :, 0:64], k.G[:, :, 65:129], k.G[:, :, 129:193]
                sigmoid_of_exp(nc, dve, k.E0[:, :, :], k.E0[:, :, :])
                s0 = k.E0[:, :, 0:64]
                nc.vector.tensor_scalar_mul(k.alr[:, :].unsqueeze(2), k.E0[:, :, 64:65], 0.1 * 2.0 / D)
                nc.vector.tensor_tensor(tiles(k.silu), z0, s0, ALU.mult)
                dve.drain()
                nc.vector.tensor_tensor(k.x1[:, :, 0:64], x0, tiles(k.silu), ALU.add).then_inc(src_ready, 1)
                slope(nc, dve, tiles(k.d0), s0, tiles(k.silu), tiles(k.tmp))
                dve.wait_ge(e1_ready, b + 1)
                sigmoid_of_exp(nc, dve, k.E1[:, :], k.E1[:, :])
                nc.vector.tensor_tensor(k.silu[:, :], k.MI[0:TP, 0:384], k.E1[:, :], ALU.mult)
                dve.drain()
                nc.vector.tensor_tensor(tiles(k.dx), k.x1[:, :, 0:64], tiles(k.silu), ALU.add)
                dve.drain()
                nc.vector.tensor_tensor(tiles(k.dx), tiles(k.dx), tgt, ALU.subtract)
                dve.drain()
                nc.vector.tensor_tensor(tiles(k.dx), tiles(k.dx), bcast(k.alr[:, :], D), ALU.mult)
                slope(nc, dve, k.dz1[:, :], k.E1[:, :], k.silu[:, :], k.tmp[:, :])
                nc.vector.tensor_tensor(k.dz1[:, :], k.dz1[:, :], k.dx[:, :], ALU.mult).then_inc(src_ready, 1)
                dve.wait_ge(dx_made, b + 1)
                nc.vector.tensor_tensor(k.dx[:, :], k.MI[0:TP, 0:384], k.dx[:, :], ALU.add)
                dve.drain()
                nc.vector.tensor_tensor(k.dz0[:, :], k.dx[:, :], k.d0[:, :], ALU.mult).then_inc(dz0_ready, 1)
                dve.wait_ge(grads_made, b + 1)
                nc.vector.tensor_tensor(k.grads[:, :], k.grads[:, :], k.PV[0:65, 0:128], ALU.add).then_inc(grads_kept, 1)
                dve.drain()


def slope(nc, dve, dst, s, silu, tmp):
    nc.vector.tensor_tensor(tmp, silu, s, ALU.mult)
    nc.vector.tensor_tensor(dst, silu, s, ALU.add)
    dve.drain()
    nc.vector.tensor_tensor(dst, dst, tmp, ALU.subtract)
    dve.drain()


def adamw(nc, k, sem):
    squared, rooted, stepped, made = sem("grads_squared"), sem("grads_rooted"), sem("stepped"), sem("wq_w0_made")
    with nc.Block() as block:
        @block.gpsimd
        def _(pool):
            pool.wait_ge(squared, 1)
            nc.gpsimd.tensor_tensor(k.gabs[:, :], k.gsq[:, :], k.plus_half[0:65, 0:1].to_broadcast([65, 128]), ALU.pow)\
                .then_inc(rooted, 1)

        @block.vector
        def _(dve):
            nc.vector.tensor_tensor(k.gsq[:, :], k.grads[:, :], k.grads[:, :], ALU.mult).then_inc(squared, 1)
            dve.wait_ge(rooted, 1)
            nc.vector.tensor_scalar_add(k.gabs[:, :], k.gabs[:, :], 1e-8)
            dve.drain()
            nc.vector.reciprocal(k.gabs[:, :], k.gabs[:, :])
            dve.drain()
            nc.vector.tensor_tensor(k.gabs[:, :], k.gabs[:, :], k.grads[:, :], ALU.mult)
            nc.vector.tensor_scalar_mul(k.NW[0:65, :], k.WB[0:65, :], 1.0 - 0.001 * 0.01)
            dve.drain()
            nc.vector.scalar_tensor_tensor(k.NW[0:65, :], k.gabs[:, :], -0.001, k.NW[0:65, :], ALU.mult, ALU.add)\
                .then_inc(stepped, 1)
            dve.drain()
            dve.wait_ge(made, 1)
            nc.vector.memset(k.R4[64:65, 0:64], 0.0)
            nc.vector.tensor_copy(k.R4[0:64, 64:128], k.MI[0:64, 0:64])
            nc.vector.tensor_copy(k.R4[64:65, 64:128], k.NW[64:65, 0:64])

        @block.tensor
        def _(pe):
            pe.wait_ge(stepped, 1)
            nc.tensor.matmul(k.MI[0:64, 0:64], k.WqT1[:, :], k.NW[0:64, 0:64], start=True, stop=True).then_inc(made, 1)



def retrieve(nc, k, A, out, sem):
    loaded, made, g_ready = sem("h3_loaded"), sem("q_made"), sem("q_ready")
    src_ready, turned, turned_kept = sem("p3_turn_source"), sem("p3_turned"), sem("p3_turned_kept")
    z1_made, e1_ready, h4_ready = sem("rz1_made"), sem("re1_ready"), sem("h4_ready")
    h4_stored, xT4_stored = sem("h4_stored"), sem("xT4_stored")
    k.var_ready, k.rstd_ready = sem("p3_var_ready"), sem("p3_rstd_ready")
    with nc.Block() as block:
        @block.sync
        def _(sp):
            with sp.Fori(0, B) as b:
                sp.wait_ge(h4_ready, b)
                sp.dma_start(k.h3[:, :], row(k.d_h3, b)).then_inc(loaded, 16)
                sp.dma_start(k.xT3[0:64, :], row(k.d_xT3, b)).then_inc(loaded, 16)
                sp.wait_ge(h4_ready, b + 1)
                sp.dma_start(tokens(out, b), tiles(k.h4)).then_inc(h4_stored, 16)
                sp.wait_ge(turned_kept, 2 * b + 2)
                sp.dma_start(row(k.d_xT4, b), k.xT2[0:64, :]).then_inc(xT4_stored, 16)
            sp.wait_ge(h4_stored, 16 * B)
            sp.wait_ge(xT4_stored, 16 * B)

        @block.tensor
        def _(pe):
            with pe.Fori(0, B) as b:
                pe.wait_ge(loaded, 32 * b + 32)
                for t in range(NT):
                    last = nc.tensor.matmul(k.S[0][0:TP, t // 3, (t % 3) * 128:(t % 3 + 1) * 128],
                                            k.xT3[:, t * TP:(t + 1) * TP], k.R4[:, :], start=True, stop=True)
                last.then_inc(made, 1)
                wait_apart(pe, src_ready, 2 * b + 1)
                turn(nc, k, k.q1)
                k.turned_last.then_inc(turned, 1)
                pe.wait_ge(turned_kept, 2 * b + 1)
                for t in range(NT):
                    last = nc.tensor.matmul(k.MI[0:TP, t * 64:(t + 1) * 64], k.xT[:, t * TP:(t + 1) * TP],
                                            k.NW[:, 64:128], start=True, stop=True)
                last.then_inc(z1_made, 1)
                wait_apart(pe, src_ready, 2 * b + 2)
                turn(nc, k, k.xn)
                k.turned_last.then_inc(turned, 1)

        @block.scalar
        def _(act):
            with act.Fori(0, B) as b:
                act.wait_ge(made, b + 1)
                for c in range(2):
                    src = k.S[0][0:TP, c, 0:384].rearrange("p (a w) -> p a w", a=3)
                    nc.scalar.activation(k.G[:, 3 * c:3 * c + 3, 0:128], src, ACT.Copy)
                    last = nc.scalar.activation(k.E0[:, 3 * c:3 * c + 3, 0:64], src[:, :, 64:128], ACT.Exp, scale=-1.0)
                last.then_inc(g_ready, 1)
                act.wait_ge(turned, 2 * b + 1)
                nc.scalar.activation(halves(k.xT[0:64, :]), k.T[0:64, :, 0:HALF], ACT.Copy).then_inc(turned_kept, 1)
                act.wait_ge(z1_made, b + 1)
                nc.scalar.activation(k.E1[:, :], k.MI[0:TP, 0:384], ACT.Exp, scale=-1.0).then_inc(e1_ready, 1)
                act.wait_ge(turned, 2 * b + 2)
                act.wait_ge(xT4_stored, 16 * b)
                nc.scalar.activation(halves(k.xT2[0:64, :]), k.T[0:64, :, 0:HALF], ACT.Copy).then_inc(turned_kept, 1)

        @block.gpsimd
        def _(pool):
            with pool.Fori(0, B) as b:
                rsqrt(nc, pool, k, NT, b + 1)

        @block.vector
        def _(dve):
            with dve.Fori(0, B) as b:
                dve.wait_ge(g_ready, b + 1)
                s0 = k.E0[:, :, 0:64]
                sigmoid_of_exp(nc, dve, s0, s0)
                nc.vector.tensor_tensor(tiles(k.silu), k.G[:, :, 64:128], s0, ALU.mult)
                dve.drain()
                nc.vector.tensor_tensor(tiles(k.q1), k.G[:, :, 0:64], tiles(k.silu), ALU.add).then_inc(src_ready, 1)
                dve.wait_ge(e1_ready, b + 1)
                nc.vector.tensor_tensor(k.q1[:, :], k.q1[:, :], k.h3[:, :], ALU.add)
                sigmoid_of_exp(nc, dve, k.E1[:, :], k.E1[:, :])
                nc.vector.tensor_tensor(k.silu[:, :], k.MI[0:TP, 0:384], k.E1[:, :], ALU.mult)
                dve.drain()
                dve.wait_ge(h4_stored, 16 * b)
                nc.vector.tensor_tensor(k.h4[:, :], k.q1[:, :], k.silu[:, :], ALU.add).then_inc(h4_ready, 1)
                dve.drain()
                layernorm(nc, dve, k, tiles(k.h4), tiles(k.xn), NT, D, 1e-5,
                          lambda: dve.wait_ge(k.rstd_ready, b + 1), src_ready)



def product_key_attention(nc, k, out, sem):
    xk_loaded, sims_made, sims_ready = sem("xk_loaded"), sem("sims_made"), sem("sims_ready")
    top_exp_in, top_exp, chosen = sem("top_exp_in"), sem("top_exp"), sem("indices_chosen")
    xa_loaded, acc_loaded, acc_ready, acc_stored = sem("xa_loaded"), sem("acc_loaded"), sem("acc_ready"), sem("acc_stored")
    gathered = [sem(f"gathered_{t}") for t in range(NT)]
    taken = sem("gathered_rows_taken")
    kv_turned, kv_ready = sem("kv_turned"), sem("kT4_ready")
    G = B * PH
    units = [unit(t + 1, k.xT[:, t * TP:(t + 1) * TP], k.kT[:, :],
                  lambda b: k.kv[:, b * 128 + 64:(b + 1) * 128], k.PV[0:TP, t * 64:(t + 1) * 64], True)
             for t in range(NT)]
    att = Attention(nc, k, sem, "a4", units)

    with nc.Block() as block:
        @block.sync
        def _(sp):
            def load_xk(g, b):
                wait_apart(sp, sims_made, g)
                sp.dma_start(k.xT3[0:64, :], row(k.d_xT4, b)).then_inc(xk_loaded, 16)

            def attention_io(g, b, b_last):
                wait_apart(sp, att.out_ready, NT * g)
                sp.dma_start(k.xT[0:64, :], row(k.d_xT4, b)).then_inc(xa_loaded, 16)
                wait_apart(sp, acc_stored, 16 * g)
                sp.dma_start(tiles(k.h4), tokens(out, b)).then_inc(acc_loaded, 16)
                wait_apart(sp, acc_ready, g + 1)
                sp.dma_start(tokens(out, b), tiles(k.h4)).then_inc(acc_stored, 16)

            load_xk(0, 0)
            with sp.Fori(0, G - 1) as g:
                b_next, b_now = ((g + 1) >> 3) & (B - 1), (g >> 3) & (B - 1)
                load_xk(g + 1, b_next)
                attention_io(g, b_now, 0)
            attention_io(G - 1, B - 1, 0)
            sp.wait_ge(acc_stored, 16 * G)

        @block.gpsimd
        def _(pool):
            with pool.Fori(0, G) as g:
                for t in range(NT):
                    wait_apart(pool, chosen, NT * g + t + 1)
                    for j in range(TOPK):
                        pool.indirect_dma_start(
                            out=k.rows[t][:, j * 128:(j + 1) * 128], out_offset=None, in_=k.table,
                            in_offset=bass.IndirectOffsetOnAxis(ap=k.idx[:, t * TOPK + j:t * TOPK + j + 1], axis=0))\
                            .then_inc(gathered[t], 16)

        @block.tensor
        def _(pe):
            def scores_of(g, h):
                pe.wait_ge(xk_loaded, 16 * g + 16)
                pe.wait_ge(sims_ready, 2 * g)
                for t in range(NT):
                    last = nc.tensor.matmul(k.S2[0:TP, t // 3, (t % 3) * 128:(t % 3 + 1) * 128],
                                            k.xT3[:, t * TP:(t + 1) * TP], k.Mk[:, bass.ds(h * 128, 128)],
                                            start=True, stop=True)
                last.then_inc(sims_made, 1)

            def attention(g):
                pe.wait_ge(xa_loaded, 16 * g + 16)
                for m in range(NT + 2):
                    if m < NT:
                        pe.wait_ge(kv_ready, NT * g + m)
                        wait_apart(pe, taken, NT * g + m + 1)
                        nc.tensor.transpose(k.MI[0:64, 0:TP], k.kv[:, m * 128:m * 128 + 64], k.ident[0:TP, 0:TP])\
                            .then_inc(kv_turned, 1)
                        pe.wait_ge(kv_ready, NT * g + m + 1)
                    if m == 2:
                        pe.wait_ge(acc_ready, g)
                    att.tensor(pe, g, m)

            scores_of(0, 0)
            with pe.Fori(0, G - 1) as g:
                h_next = (g + 1) & 7
                scores_of(g + 1, h_next)
                attention(g)
            attention(G - 1)

        @block.scalar
        def _(act):
            def choose(g):
                act.wait_ge(sims_made, g + 1)
                act.wait_ge(top_exp_in, g)
                for c in range(2):
                    nc.scalar.activation(k.sims[:, 3 * c:3 * c + 3, :],
                                         k.S2[0:TP, c, 0:384].rearrange("p (a w) -> p a w", a=3), ACT.Copy)\
                        .then_inc(sims_ready, 1)
                act.wait_ge(top_exp_in, g + 1)
                nc.scalar.activation(k.top_e[:, :], k.top_v[:, :], ACT.Exp).then_inc(top_exp, 1)

            def attention(g):
                for m in range(NT + 2):
                    if m < NT:
                        act.wait_ge(kv_turned, NT * g + m + 1)
                        nc.scalar.activation(k.kT[0:64, m * TP:(m + 1) * TP], k.MI[0:64, 0:TP], ACT.Copy)\
                            .then_inc(kv_ready, 1)
                    att.scalar(act, g, m)

            choose(0)
            with act.Fori(0, G - 1) as g:
                choose(g + 1)
                attention(g)
            attention(G - 1)

        @block.vector
        def _(dve):
            sc = k.sc[:, :].rearrange("p (t a n) -> p t a n", t=NT, a=2)
            ix = k.ix[:, :].rearrange("p (t a n) -> p t a n", t=NT, a=2)
            ixf = k.ixf[:, :].rearrange("p (t a n) -> p t a n", t=NT, a=2)
            cand = k.cand[:, :].rearrange("p (t n) -> p t n", t=NT)
            cidx = k.cidx[:, :].rearrange("p (t n) -> p t n", t=NT)

            def pairs(dst, src):
                at = 0
                for i0, ni, nj in RUNS:
                    for t0 in range(0, NT, 1 if ni > 1 and nj > 1 else NT):
                        ts = slice(t0, t0 + 1) if ni > 1 and nj > 1 else slice(0, NT)
                        d = dst[:, ts, at:at + ni * nj]
                        a, b = src[:, ts, 0, i0:i0 + ni], src[:, ts, 1, 0:nj]
                        if ni > 1 and nj > 1:
                            d = dst[:, t0, at:at + ni * nj].rearrange("p (i j) -> p i j", j=nj)
                            a = src[:, t0, 0, i0:i0 + ni].unsqueeze(2).to_broadcast([TP, ni, nj])
                            b = src[:, t0, 1, 0:nj].unsqueeze(1).to_broadcast([TP, ni, nj])
                        elif ni == 1:
                            a = a.to_broadcast([TP, NT, nj])
                        else:
                            b = b.to_broadcast([TP, NT, ni])
                        nc.vector.tensor_tensor(d, a, b, ALU.add)
                    at += ni * nj

            def choose(g, h):
                nc.vector.tensor_copy(k.head[:, :], k.heads[:, bass.ds(h, 1)])
                dve.wait_ge(sims_ready, 2 * g + 2)
                nc.vector.tensor_copy(k.gate[:, :], k.ones[0:TP, 0:1])
                both = [(t, a) for t in range(NT) for a in range(2)]
                for t, a in both:
                    nc.vector.max(sc[:, t, a, 0:8], k.sims[:, t, a * 64:(a + 1) * 64])
                dve.drain()
                for t, a in both:
                    s = k.sims[:, t, a * 64:(a + 1) * 64]
                    nc.vector.max_index(ix[:, t, a, 0:8], sc[:, t, a, 0:8], s)
                    nc.vector.match_replace(k.sims2[:, t, a * 64:(a + 1) * 64], sc[:, t, a, 0:8], s, NEG)
                dve.drain()
                for t, a in both:
                    nc.vector.max(sc[:, t, a, 8:16], k.sims2[:, t, a * 64:(a + 1) * 64])
                dve.drain()
                for t, a in both:
                    nc.vector.max_index(ix[:, t, a, 8:16], sc[:, t, a, 8:16], k.sims2[:, t, a * 64:(a + 1) * 64])
                dve.drain()
                nc.vector.tensor_copy(k.ixf[:, :], k.ix[:, :])
                dve.drain()
                nc.vector.tensor_scalar(ixf[:, :, 1, :], ixf[:, :, 1, :], float(PKEYS), None, ALU.mult)
                nc.vector.tensor_scalar(ixf[:, :, 0, :], ixf[:, :, 0, :], k.head[:, 0:1], None, ALU.add)
                pairs(cand, sc)
                dve.drain()
                pairs(cidx, ixf)
                for t in range(NT):
                    nc.vector.max(k.top[:, t, 0:8], cand[:, t, :])
                dve.drain()
                for t in range(NT):
                    nc.vector.max_index(k.pos[:, t, 0:8], k.top[:, t, 0:8], cand[:, t, :])
                    nc.vector.match_replace(k.cand2[:, t, :], k.top[:, t, 0:8], cand[:, t, :], NEG)
                dve.drain()
                for t in range(NT):
                    nc.vector.max(k.top[:, t, 8:16], k.cand2[:, t, :])
                dve.drain()
                for t in range(NT):
                    nc.vector.max_index(k.pos[:, t, 8:16], k.top[:, t, 8:16], k.cand2[:, t, :])
                nc.vector.tensor_tensor(tiles(k.top_v, TOPK), k.top[:, :, :], k.top[:, :, 0:1].to_broadcast([TP, NT, TOPK]),
                                        ALU.subtract).then_inc(top_exp_in, 1)
                dve.drain()
                nc.vector.tensor_copy(k.posf[:, :], k.pos[:, :, :].rearrange("p t n -> p (t n)"))
                dve.drain()
                for t in range(NT):
                    hot = k.hot[:, t * TOPK * NC_:(t + 1) * TOPK * NC_].rearrange("p (j c) -> p j c", c=NC_)
                    nc.vector.tensor_tensor(hot, bcast(k.posf[:, t * TOPK:(t + 1) * TOPK], NC_),
                                            k.place[:, :].unsqueeze(1).to_broadcast([TP, TOPK, NC_]), ALU.is_equal)
                dve.drain()
                for t in range(NT):
                    hot = k.hot[:, t * TOPK * NC_:(t + 1) * TOPK * NC_].rearrange("p (j c) -> p j c", c=NC_)
                    nc.vector.tensor_tensor(hot, hot, cidx[:, t:t + 1, :].to_broadcast([TP, TOPK, NC_]), ALU.mult)
                dve.drain()
                nc.vector.reduce_sum(k.idxf[:, :], k.hot[:, :].rearrange("p (j c) -> p j c", c=NC_), AXX)
                dve.drain()
                dve.wait_ge(top_exp, g + 1)
                nc.vector.reduce_sum(k.wsum[:, :], tiles(k.top_e, TOPK), AXX)
                dve.drain()
                nc.vector.reciprocal(k.wsum[:, :], k.wsum[:, :])
                dve.drain()
                nc.vector.tensor_tensor(tiles(k.w_next, TOPK), tiles(k.top_e, TOPK), bcast(k.wsum[:, :], TOPK), ALU.mult)
                dve.drain()

            def take_over(t):
                s = slice(t * TOPK, (t + 1) * TOPK)
                nc.vector.tensor_copy(k.w[:, s], k.w_next[:, s])
                nc.vector.tensor_copy(k.idx[:, s], k.idxf[:, s]).then_inc(chosen, 1)

            def attention(g, more):
                for m in range(NT + 2):
                    if m < NT:
                        dve.wait_ge(gathered[m], 16 * TOPK * (g + 1))
                        prod = k.prod[:, :].rearrange("p (j c) -> p j c", c=128)
                        nc.vector.tensor_tensor(prod, k.rows[m][:, :].rearrange("p (j c) -> p j c", c=128),
                                                bcast(k.w[:, m * TOPK:(m + 1) * TOPK], 128), ALU.mult)
                        dve.drain()
                        if more:
                            take_over(m)
                        nc.vector.reduce_sum(k.kv[:, m * 128:(m + 1) * 128], prod.rearrange("p j c -> p c j"), AXX)\
                            .then_inc(taken, 1)
                        dve.drain()
                    att.vector(dve, g, m)
                inverse_sums(nc, dve, k, 0, NT, True)
                dve.wait_ge(att.out_ready, NT * g + NT)
                nc.vector.tensor_tensor(tiles(k.tmp), tiles(k.PV[0:TP, 0:384]), bcast(k.rinv[:, 0:NT], D), ALU.mult)
                dve.drain()
                dve.wait_ge(acc_loaded, 16 * g + 16)
                nc.vector.tensor_tensor(k.h4[:, :], k.h4[:, :], k.tmp[:, :], ALU.add).then_inc(acc_ready, 1)
                dve.drain()

            for h in range(PH):
                nc.vector.memset(k.heads[:, h:h + 1], float(h * PKEYS * PKEYS))
            dve.drain()
            choose(0, 0)
            for t in range(NT):
                take_over(t)
            dve.drain()
            with dve.Fori(0, G - 1) as g:
                choose(g + 1, (g + 1) & 7)
                attention(g, True)
            attention(G - 1, False)



class Shared:
    pass


def build(nc, A, out):
    ctx = ExitStack()
    with ctx:
        def sb(name, shape, dt=FP):
            return ctx.enter_context(nc.sbuf_tensor(name, shape, dt))

        def sem(name):
            return ctx.enter_context(nc.semaphore(name))

        def eb(name, shape, dt=FP):
            return early.enter_context(nc.sbuf_tensor(name, shape, dt))

        k = Shared()
        ps = [ctx.enter_context(nc.psum_tensor(f"bank_pair_{i}", [128, 2, 512], FP)) for i in range(3)]
        k.S, k.T = ps[0:2], ps[2]
        k.S2 = ps[1]
        k.PV = ctx.enter_context(nc.psum_tensor("PV", [128, 512], FP))
        k.MI = ctx.enter_context(nc.psum_tensor("MI", [128, 512], FP))
        k.ident = sb("ident", [128, 128])
        k.ident_bf = sb("ident_bf", [128, 128], BF)
        k.causal = sb("causal", [TP, TP], BF)
        k.ones = sb("ones", [128, 128])
        k.minus_half = sb("minus_half", [128, 1])
        k.plus_half = sb("plus_half", [128, 1])
        k.place_i = sb("place_i", [TP, NC_], mybir.dt.int32)
        k.place = sb("place", [TP, NC_])
        k.WX = sb("WX", [128, 128])
        k.R3 = sb("R3", [128, 64])
        k.W2BD = sb("W2BD", [128, 128])
        k.W4 = sb("W4", [128, 64])
        k.WqN = sb("WqN", [64, 64])
        k.WkN = sb("WkN", [64, 64])
        k.WvT = sb("WvT", [128, 64])
        k.ATT0 = sb("ATT0", [128, 64])
        k.HLP = sb("HLP", [128, 128])
        k.HLT = sb("HLT", [128, 64])
        k.WVB = sb("WVB", [128, 64])
        k.wqb = sb("wqb", [128, NE, 128])
        k.wkb = sb("wkb", [128, 128])
        k.LB = sb("LB", [128, NE, 128])
        k.GW = sb("GW", [128, 2, 16])
        k.GB = sb("GB", [1, 16])
        k.FG = sb("FG", [128, 4])
        k.LNG = sb("LNG", [TP, 16])
        k.LNB = sb("LNB", [TP, 16])
        k.FNG = sb("FNG", [TP, 16])
        k.FNB = sb("FNB", [TP, 16])
        k.FC1 = sb("FC1", [128, 64])
        k.FC2 = sb("FC2", [128, 64])
        k.R2 = sb("R2", [128, 194])
        k.WB = sb("WB", [128, 128])
        k.NW = sb("NW", [128, 128])
        k.W1Tr = sb("W1Tr", [128, 64])
        k.WkT1 = sb("WkT1", [64, 64])
        k.WqT1 = sb("WqT1", [64, 64])
        k.R4 = sb("R4", [128, 128])
        k.grads = sb("grads", [65, 128])
        k.gsq = sb("gsq", [65, 128])
        k.gabs = sb("gabs", [65, 128])
        k.WPK = sb("WPK", [32, 1024])
        k.KPK = sb("KPK", [32, 1024])
        k.Mk = sb("Mk", [128, 1024])
        k.BD = sb("BD", [128, PH, 128])
        k.xT = sb("xT", [128, L])
        k.xT2 = sb("xT2", [128, L])
        k.xT3 = sb("xT3", [128, L])
        k.kT = sb("kT", [128, L])
        k.h1 = sb("h1", [TP, NT * D])
        k.h2 = sb("h2", [TP, NT * D])
        k.h3 = sb("h3", [TP, NT * D])
        k.h4 = sb("h4", [TP, NT * D])
        k.xn = sb("xn", [TP, NT * D])
        k.tmp = sb("tmp", [TP, NT * D])
        k.V = sb("V", [TP, NT * D])
        k.mix = sb("mix", [TP, NT * D])
        k.fx = sb("fx", [TP, NT * D])
        k.hx = sb("hx", [TP, NT * D])
        k.fout = sb("fout", [TP, NT * D])
        k.live = sb("live", [TP, NT * D])
        k.resid = sb("resid", [TP, NT * D])
        k.silu = sb("silu", [TP, NT * D])
        k.d0 = sb("d0", [TP, NT * D])
        k.dx = sb("dx", [TP, NT * D])
        k.dz0 = sb("dz0", [TP, NT * D])
        k.dz1 = sb("dz1", [TP, NT * D])
        k.E1 = sb("E1", [TP, NT * D])
        k.q1 = sb("q1", [TP, NT * D])
        k.ln_dev = sb("ln_dev", [TP, NT * D])
        k.ln_sq = sb("ln_sq", [TP, NT * D])
        k.ln_mean = sb("ln_mean", [TP, 24])
        k.ln_var = sb("ln_var", [TP, 24])
        k.ln_rstd = sb("ln_rstd", [TP, 24])
        k.P0 = sb("P0", [TP, L])
        k.P1 = sb("P1", [TP, L])
        k.PT0 = sb("PT0", [TP, L])
        k.PT1 = sb("PT1", [TP, L])
        k.P, k.PT = [k.P0, k.P1], [k.PT0, k.PT1]
        k.nmax = sb("nmax", [TP, 96])
        k.mtmp = sb("mtmp", [TP, 192])
        k.rsum = sb("rsum", [TP, 96])
        k.rsum2 = sb("rsum2", [TP, 96])
        k.rinv = sb("rinv", [TP, 96])
        k.table = nc.dram_tensor("table", [ROWS, 128], FP).ap()
        k.d_h2 = nc.dram_tensor("d_h2", [B, TP, NT * D], FP).ap()
        k.d_h3 = nc.dram_tensor("d_h3", [B, TP, NT * D], FP).ap()
        k.d_xT2 = nc.dram_tensor("d_xT2", [B, D, L], FP).ap()
        k.d_xT3 = nc.dram_tensor("d_xT3", [B, D, L], FP).ap()
        k.d_xT4 = nc.dram_tensor("d_xT4", [B, D, L], FP).ap()

        early = ctx.enter_context(ExitStack())
        k.xs = eb("xs", [128, L])
        k.U0 = eb("U0", [128, L + 2])
        k.U1 = eb("U1", [128, L + 2])
        k.UR = eb("UR", [128, L + 2])
        k.U = [k.U0, k.U1]
        k.sxT = eb("sxT", [128, L])
        k.UT = eb("UT", [128, NE, L])
        k.sxn = eb("sxn", [128, NH, L])
        k.Vp = eb("Vp", [TP, NT, NH, 128])
        k.PG = [eb(f"PG{i}", [TP, NE * L]) for i in range(2)]
        k.PTG = [eb(f"PTG{i}", [TP, NE * TP]) for i in range(2)]
        k.outT = eb("outT", [128, NE * TP])
        k.att = eb("att", [TP, NT, 256])
        k.big = eb("big", [TP, 1536])
        k.soft = eb("soft", [TP, 96])
        k.soft_exp = eb("soft_exp", [TP, 96])
        k.soft_m = eb("soft_m", [TP, 24])
        k.G = eb("G", [TP, NT, 194])
        k.E0 = eb("E0", [TP, NT, 65])
        k.x1 = eb("x1", [TP, NT, 65])
        k.alr = eb("alr", [TP, NT])
        k.rows_in = eb("rows_in", [128, 8, 128])
        k.rows_turned = eb("rows_turned", [128, 1024])
        k.rows_out = eb("rows_out", [128, 1024])

        for e in (nc.tensor, nc.gpsimd, nc.sync):
            PASSED[e.engine] = sem("waits_passed_" + str(e.engine).split(".")[-1])
        clear(nc, k)
        load_weights(nc, k, A, sem)
        weight_products(nc, k, sem)
        build_table(nc, k, A, sem)
        tok_and_attention(nc, k, A, sem)
        residuals(nc, k, A, sem)
        ffn_and_gradients(nc, k, A, sem)
        adamw(nc, k, sem)
        retrieve(nc, k, A, out, sem)
        early.close()
        k.sims = sb("sims", [TP, NT, 128])
        k.sims2 = sb("sims2", [TP, NT, 128])
        k.sc = sb("sc", [TP, NT * 32])
        k.ix = sb("ix", [TP, NT * 32], U32)
        k.ixf = sb("ixf", [TP, NT * 32])
        k.cand = sb("cand", [TP, NT * NC_])
        k.cidx = sb("cidx", [TP, NT * NC_])
        k.cand2 = sb("cand2", [TP, NT, NC_])
        k.top = sb("top", [TP, NT, TOPK])
        k.pos = sb("pos", [TP, NT, TOPK], U32)
        k.posf = sb("posf", [TP, NT * TOPK])
        k.top_v = sb("top_v", [TP, NT * TOPK])
        k.top_e = sb("top_e", [TP, NT * TOPK])
        k.hot = sb("hot", [TP, NT * TOPK * NC_])
        k.idxf = sb("idxf", [TP, NT * TOPK])
        k.wsum = sb("wsum", [TP, NT])
        k.w_next = sb("w_next", [TP, NT * TOPK])
        k.w = sb("w", [TP, NT * TOPK])
        k.idx = sb("idx", [TP, NT * TOPK], U32)
        k.gate = sb("gate", [TP, 1])
        k.heads = sb("heads", [TP, PH])
        k.head = sb("head", [TP, 1])
        k.prod = sb("prod", [TP, TOPK * 128])
        k.kv = sb("kv", [TP, NT * 128])
        k.rows = [sb(f"rows_{t}", [TP, TOPK * 128]) for t in range(NT)]
        product_key_attention(nc, k, out, sem)


def host_arrays(i):
    import numpy as np
    c = np.ascontiguousarray
    i = {n: np.asarray(v) for n, v in i.items()}
    f = {
        "x": c(i["x"]), "xr": c(i["x"][:, :, ::-1]),
        "W1T": c(i["L0_tok_W1"].T), "W2T": c(i["L0_tok_W2"].T), "W3T": c(i["L0_tok_W3"].T), "W4T": c(i["L0_tok_W4"].T),
        "b1": i["L0_tok_b1"][None], "b2": i["L0_tok_b2"][None], "b3": i["L0_tok_b3"][None], "b4": i["L0_tok_b4"][None],
        "attn_Wq": c(i["L0_attn_Wq"]), "attn_Wk": c(i["L0_attn_Wk"]), "attn_WvT": c(i["L0_attn_Wv"].T),
        "hlT": c(i["L0_ffn_hl_w"].reshape(64, 64).T), "hl_b": c(i["L0_ffn_hl_b"].reshape(1, 64)),
        "gwT": c(i["L0_ffn_gate_w"].transpose(0, 2, 1)), "gb": c(i["L0_ffn_gate_b"].reshape(1, 16)),
        "fgT": c(i["L0_ffn_fgate_w"].T), "wvT": c(i["L0_ffn_wv"].transpose(0, 2, 1)),
        "wq": c(i["L0_ffn_wq"]), "wk": c(i["L0_ffn_wk"]),
        "fc1T": c(i["L0_ffn_fc1_w"].T), "fc2T": c(i["L0_ffn_fc2_w"].T),
        "fc1_b": i["L0_ffn_fc1_b"][None], "fc2_b": i["L0_ffn_fc2_b"][None],
        "ln_g": i["L0_ffn_ln_g"][None], "ln_b": i["L0_ffn_ln_b"][None],
        "fn_g": i["L0_ffn_fnorm_g"][None], "fn_b": i["L0_ffn_fnorm_b"][None],
        "Wk1": c(i["L1_attn_Wk"]), "Wv1": c(i["L1_attn_Wv"]), "Wlr": c(i["L1_attn_Wlr"]), "Wq1": c(i["L1_attn_Wq"]),
        "blr": i["L1_attn_blr"][None], "Ws": c(i["L1_attn_Ws"]), "bs": c(i["L1_attn_bs"].reshape(1, 128)),
        "Ws1T": c(i["L1_attn_Ws"][1].T), "WkT1": c(i["L1_attn_Wk"].T), "WqT1": c(i["L1_attn_Wq"].T),
        "wpk": c(i["L1_ffn_Wq_pk"].reshape(64, 2, 8, 32).transpose(3, 1, 2, 0).reshape(32, 1024)),
        "kpk": c(i["L1_ffn_pk_keys"].transpose(3, 0, 2, 1).reshape(32, 1024)),
        "WqpT": c(i["L1_ffn_Wq"].T), "Wo": c(i["L1_ffn_Wo"]),
        "keys": c(i["L1_ffn_keys_table"]), "values": c(i["L1_ffn_values_table"]),
    }
    return {n: c(v) for n, v in f.items()}


def kernel(**inputs):
    import numpy as np
    import concourse.bacc as bacc
    from concourse.bass_utils import run_bass_kernel_spmd

    nc = bacc.Bacc("TRN2", target_bir_lowering=False, num_devices=1)
    arrays = host_arrays(inputs)
    aps = {n: nc.dram_tensor(f"in_{n}", a.shape, mybir.dt.from_np(a.dtype), kind="ExternalInput").ap()
           for n, a in arrays.items()}
    out = nc.dram_tensor("out_dram", (B, L, D), FP, kind="ExternalOutput").ap()
    build(nc, aps, out)
    r = run_bass_kernel_spmd(nc, [{f"in_{n}": a for n, a in arrays.items()}], core_ids=[0])
    return r.results[0]["out_dram"]
```

```python
import concourse.bass as bass
from concourse import mybir
from contextlib import ExitStack

FP = mybir.dt.float32
BF = mybir.dt.bfloat16
U32 = mybir.dt.uint32
ALU = mybir.AluOpType
ACT = mybir.ActivationFunctionType
AXX = mybir.AxisListType.X

B, CH, L, D = 16, 4, 750, 64
TP, NT = 125, 6
HALF = L // 2
STEPS = 8
NH, NE, HD = 4, 4, 16
PH, PKEYS, PDK, TOPK = 8, 64, 32, 16
ROWS = PH * PKEYS * PKEYS
NEG = -3.0e38
RUNS = [(0, 1, 16), (1, 1, 8), (2, 1, 5), (3, 1, 4), (4, 1, 3), (5, 3, 2), (8, 8, 1)]
NC_ = sum(n * m for _, n, m in RUNS)


PASSED = {}


def wait_apart(eng, semaphore, value):
    eng.wait_ge(semaphore, value)
    eng.sem_inc(PASSED[eng.engine], 1)


def bcast(ap, n):
    return ap.unsqueeze(2).to_broadcast([ap.shape[0], ap.shape[1], n])


def row(ap, i):
    return ap[bass.ds(i, 1), :, :].rearrange("a p n -> (a p) n")


def tokens(ap, b):
    return ap.rearrange("b (t p) d -> b p t d", p=TP)[bass.ds(b, 1), :, :, :].rearrange("a p t d -> (a p) t d")



def layernorm(nc, dve, k, src, dst, groups, width, eps, wait_rstd, done, scale=None, shift=None):
    dev, sq = k.ln_dev[0:TP, 0:groups * width].rearrange("p (g w) -> p g w", w=width), \
        k.ln_sq[0:TP, 0:groups * width].rearrange("p (g w) -> p g w", w=width)
    mean, var, rstd = k.ln_mean[0:TP, 0:groups], k.ln_var[0:TP, 0:groups], k.ln_rstd[0:TP, 0:groups]
    nc.vector.reduce_sum(mean, src, AXX)
    dve.drain()
    nc.vector.tensor_scalar_mul(mean, mean, 1.0 / width)
    dve.drain()
    nc.vector.tensor_tensor(dev, src, bcast(mean, width), ALU.subtract)
    dve.drain()
    nc.vector.tensor_tensor(sq, dev, dev, ALU.mult)
    dve.drain()
    nc.vector.reduce_sum(var, sq, AXX)
    dve.drain()
    nc.vector.tensor_scalar(var, var, 1.0 / width, eps, ALU.mult, ALU.add).then_inc(k.var_ready, 1)
    if scale is not None:
        nc.vector.tensor_tensor(dev, dev, scale[0:TP, :].unsqueeze(1).to_broadcast([TP, groups, width]), ALU.mult)
        dve.drain()
    wait_rstd()
    if scale is None:
        nc.vector.tensor_tensor(dst, dev, bcast(rstd, width), ALU.mult).then_inc(done, 1)
    else:
        nc.vector.tensor_tensor(dev, dev, bcast(rstd, width), ALU.mult)
        dve.drain()
        nc.vector.tensor_tensor(dst, dev, shift[0:TP, :].unsqueeze(1).to_broadcast([TP, groups, width]), ALU.add)\
            .then_inc(done, 1)
    dve.drain()


def rsqrt(nc, pool, k, groups, n):
    pool.wait_ge(k.var_ready, n)
    nc.gpsimd.tensor_tensor(k.ln_rstd[0:TP, 0:groups], k.ln_var[0:TP, 0:groups],
                            k.minus_half[0:TP, 0:1].to_broadcast([TP, groups]), ALU.pow).then_inc(k.rstd_ready, 1)



class Attention:

    def __init__(self, nc, k, sem, name, units):
        self.nc, self.k, self.units = nc, k, units
        self.n = len(units)
        self.nb_second = [sum(u.nb > 3 for u in units[:m]) for m in range(len(units) + 1)]
        self.scores_ready = sem(name + "_scores_ready")
        self.max_ready = sem(name + "_max_ready")
        self.probs_ready = sem(name + "_probs_ready")
        self.first_turned = sem(name + "_first_turned")
        self.second_turned = sem(name + "_second_turned")
        self.first_copied = sem(name + "_first_copied")
        self.second_copied = sem(name + "_second_copied")
        self.out_ready = sem(name + "_out_ready")

    def tensor(self, pe, it, m):
        nc, k, N, units = self.nc, self.k, self.n, self.units
        base = it * N
        if m < N:
            u = units[m]
            if m >= 2:
                pe.wait_ge(self.probs_ready, base + m - 1)
            w = u.nb * TP
            parts = [(0, w)] if w <= 500 else [(0, 375), (375, w)]
            for h, (lo, hi) in enumerate(parts):
                diag = u.masked and hi == w
                last = nc.tensor.matmul(k.S[m % 2][0:TP, h, 0:hi - lo], u.q, u.keys[:, lo:hi],
                                        start=True, stop=not diag)
                if diag:
                    last = nc.tensor.matmul(k.S[m % 2][0:TP, h, hi - lo - TP:hi - lo], k.ident_bf[0:TP, 0:TP],
                                            k.causal[0:TP, :], start=False, stop=True)
            last.then_inc(self.scores_ready, 1)
        if 1 <= m <= N:
            n = m - 1
            u = units[n]
            pe.wait_ge(self.probs_ready, base + n + 1)
            if n >= 1:
                pe.wait_ge(self.first_copied, base + n)
            for b in range(min(3, u.nb)):
                last = nc.tensor.transpose(k.T[0:TP, 0, b * TP:(b + 1) * TP], k.P[n % 2][:, b * TP:(b + 1) * TP],
                                           k.ident[0:TP, 0:TP])
            last.then_inc(self.first_turned, 1)
            if u.nb > 3:
                if n >= 1:
                    pe.wait_ge(self.second_copied, it * self.nb_second[N] + self.nb_second[n])
                for b in range(3, u.nb):
                    last = nc.tensor.transpose(k.T[0:TP, 1, (b - 3) * TP:(b - 2) * TP],
                                               k.P[n % 2][:, b * TP:(b + 1) * TP], k.ident[0:TP, 0:TP])
                last.then_inc(self.second_turned, 1)
        if 2 <= m:
            n = m - 2
            u = units[n]
            pe.wait_ge(self.first_copied, base + n + 1)
            if u.nb > 3:
                pe.wait_ge(self.second_copied, it * self.nb_second[N] + self.nb_second[n + 1])
            for b in range(u.nb):
                last = nc.tensor.matmul(u.out, k.PT[n % 2][:, b * TP:(b + 1) * TP], u.value(b),
                                        start=b == 0, stop=b == u.nb - 1)
            last.then_inc(self.out_ready, 1)

    def vector(self, dve, it, m):
        nc, k, N = self.nc, self.k, self.n
        if m < N:
            u = self.units[m]
            dve.wait_ge(self.scores_ready, it * N + m + 1)
            minus_max(nc, dve, k, k.S[m % 2], m, u.nb * TP, self.max_ready)
        if 1 <= m <= N and self.units[m - 1].nb > 3:
            n = m - 1
            u = self.units[n]
            if n >= 2:
                dve.wait_ge(self.out_ready, it * N + n - 1)
            dve.wait_ge(self.second_turned, it * self.nb_second[N] + self.nb_second[m])
            w = (u.nb - 3) * TP
            nc.vector.tensor_copy(k.PT[n % 2][:, 375:375 + w], k.T[0:TP, 1, 0:w]).then_inc(self.second_copied, 1)

    def scalar(self, act, it, m):
        nc, k, N = self.nc, self.k, self.n
        if m < N:
            u = self.units[m]
            act.wait_ge(self.max_ready, it * N + m + 1)
            if m >= 2:
                act.wait_ge(self.first_turned, it * N + m - 1)
                if self.units[m - 2].nb > 3:
                    act.wait_ge(self.second_turned, it * self.nb_second[N] + self.nb_second[m - 1])
            exp_rows(nc, k, k.P[m % 2], 0, m, u.nb * TP, self.probs_ready)
        if 1 <= m <= N:
            n = m - 1
            u = self.units[n]
            if n >= 2:
                act.wait_ge(self.out_ready, it * N + n - 1)
            act.wait_ge(self.first_turned, it * N + m)
            w = min(3, u.nb) * TP
            nc.scalar.activation(k.PT[n % 2][:, 0:w], k.T[0:TP, 0, 0:w], ACT.Copy).then_inc(self.first_copied, 1)


class ExpertAttention:

    def __init__(self, nc, k, sem, grads_kept):
        self.nc, self.k, self.grads_kept = nc, k, grads_kept
        self.scores_ready, self.max_ready, self.probs_ready = \
            sem("a2_scores_ready"), sem("a2_max_ready"), sem("a2_probs_ready")
        self.turned, self.copied = sem("a2_turned"), [sem("a2_copied_by_act"), sem("a2_copied_by_dve")]
        self.used = sem("a2_probs_used")
        self.outT_ready, self.out_turned, self.kept = sem("a2_outT_ready"), sem("a2_out_turned"), sem("a2_kept")
        self.att_turned, self.attT_ready = sem("a2_att_turned"), sem("a2_attT_ready")
        self.gate_made, self.gate_kept = sem("a2_gate_made"), sem("a2_gate_kept")
        self.groups = [(i, n) for i in range(NT) for n in range(NH)]
        self.first_turn = [sum(i + 1 for i, _ in self.groups[:g]) for g in range(len(self.groups) + 1)]
        self.turns = self.first_turn[-1]

    def copies(self, b, t):
        return b * (self.turns // 2) + t // 2 + 1

    def scores(self, pe, b, g, e):
        nc, k = self.nc, self.k
        (i, n), u = self.groups[g], 4 * g + e
        if u >= 2:
            pe.wait_ge(self.probs_ready, 96 * b + u - 1)
        w = (i + 1) * TP
        for h, (lo, hi) in enumerate([(0, w)] if w <= 500 else [(0, 375), (375, w)]):
            last = nc.tensor.matmul(k.S[u % 2][0:TP, h, 0:hi - lo], k.UT[:, e, i * TP:(i + 1) * TP],
                                    k.sxn[:, n, lo:hi], start=True, stop=hi != w)
        last = nc.tensor.matmul(k.S[u % 2][0:TP, h, hi - lo - TP:hi - lo], k.ident_bf[0:TP, 0:TP],
                                k.causal[0:TP, :], start=False, stop=True)
        last.then_inc(self.scores_ready, 1)

    def turn(self, pe, b, g, j):
        nc, k, t = self.nc, self.k, self.first_turn[g] + j
        if t >= 2:
            pe.wait_ge(self.copied[t % 2], self.copies(b, t - 2))
        if j == 0:
            pe.wait_ge(self.probs_ready, 96 * b + 4 * g + 4)
        for e in range(NE):
            last = nc.tensor.transpose(k.T[0:TP, t % 2, e * TP:(e + 1) * TP],
                                       k.PG[g % 2][:, e * L + j * TP:e * L + (j + 1) * TP], k.ident[0:TP, 0:TP])
        last.then_inc(self.turned, 1)

    def product(self, pe, b, g, j):
        nc, k, t = self.nc, self.k, self.first_turn[g] + j
        i, n = self.groups[g]
        pe.wait_ge(self.copied[t % 2], self.copies(b, t))
        if n == 0 and j == 0 and i:
            pe.wait_ge(self.outT_ready, NT * b + i)
        if g == 0 and j == 0:
            pe.wait_ge(self.grads_kept, b)
        nc.tensor.matmul(k.PV[:, 0:NE * TP], k.Vp[:, j, n, :], k.PTG[t % 2][:, :], start=n == 0 and j == 0,
                         stop=n == NH - 1 and j == i).then_inc(self.used, 1)

    def turn_out(self, pe, b, i):
        nc, k = self.nc, self.k
        if i:
            pe.wait_ge(self.gate_kept, NT * b + i)
        pe.wait_ge(self.outT_ready, NT * b + i + 1)
        for e in range(NE):
            last = nc.tensor.transpose(k.MI[0:TP, e * 128:(e + 1) * 128], k.outT[:, e * TP:(e + 1) * TP],
                                       k.ident[:, :])
        last.then_inc(self.out_turned, 1)

    def turn_att(self, pe, b, i):
        nc, k = self.nc, self.k
        pe.wait_ge(self.kept, NT * b + i + 1)
        for c in range(2):
            last = nc.tensor.transpose(k.MI[:, c * 128:c * 128 + TP], k.att[:, i, c * 128:(c + 1) * 128],
                                       k.ident[0:TP, 0:TP])
        last.then_inc(self.att_turned, 1)

    def gate(self, pe, b, i):
        nc, k = self.nc, self.k
        out, cols = k.MI[0:TP, 256:272], slice(i * TP, (i + 1) * TP)
        pe.wait_ge(self.attT_ready, NT * b + i + 1)
        nc.tensor.matmul(out, k.ones[0:1, 0:TP], k.GB[:, :], start=True, stop=False)
        nc.tensor.matmul(out, k.UT[:, 0, cols], k.GW[:, 0, :], start=False, stop=False)
        nc.tensor.matmul(out, k.UT[:, 1, cols], k.GW[:, 1, :], start=False, stop=True).then_inc(self.gate_made, 1)

    def tensor(self, pe, b):
        N = len(self.groups)
        for g in range(N + 1):
            nb = self.groups[g - 1][0] + 1 if g else 0
            for j in range(max(NE if g < N else 0, nb + 1)):
                if 0 < g < N and j < NE:
                    self.scores(pe, b, g, j)
                if j < nb:
                    self.turn(pe, b, g - 1, j)
                if 1 <= j <= nb:
                    self.product(pe, b, g - 1, j - 1)
                if j == 2 and g % NH and g > NH:
                    (self.turn_out, self.turn_att, self.gate)[g % NH - 1](pe, b, g // NH - 1)
        for step in (self.turn_out, self.turn_att, self.gate):
            step(pe, b, NT - 1)

    def exponentials(self, act, b, g, e):
        u, w = 4 * g + e, (self.groups[g][0] + 1) * TP
        act.wait_ge(self.max_ready, 96 * b + u + 1)
        exp_rows(self.nc, self.k, self.k.PG[g % 2], e * L, u, w, self.probs_ready)

    def maxima(self, dve, b, g, e):
        u, w = 4 * g + e, (self.groups[g][0] + 1) * TP
        dve.wait_ge(self.scores_ready, 96 * b + u + 1)
        minus_max(self.nc, dve, self.k, self.k.S[u % 2], u, w, self.max_ready)

    def scalar(self, act, b):
        nc, k, N = self.nc, self.k, len(self.groups)
        for g in range(N + 1):
            nb = self.groups[g - 1][0] + 1 if g else 0
            for j in range(max(NE if g < N else 0, nb)):
                if 0 < g < N and j < NE:
                    if j == 0 and g >= 2:
                        act.wait_ge(self.turned, b * self.turns + self.first_turn[g - 1])
                    self.exponentials(act, b, g, j)
                if j < nb:
                    self.copy(act, b, g - 1, j, 0)
            if g % NH == 2 and g > NH:
                self.keep_att(act, b, g // NH - 1)
            if g % NH == 0 and g:
                i = g // NH - 1
                if i:
                    act.wait_ge(self.out_turned, NT * b + i)
                act.wait_ge(self.used, b * self.turns + self.first_turn[g])
                nc.scalar.activation(k.outT[:, :], k.PV[:, 0:NE * TP], ACT.Copy).then_inc(self.outT_ready, 1)
        self.keep_att(act, b, NT - 1)

    def keep_att(self, act, b, i):
        nc, k = self.nc, self.k
        act.wait_ge(self.att_turned, NT * b + i + 1)
        nc.scalar.activation(k.UT[:, 0:2, i * TP:(i + 1) * TP],
                             k.MI[:, 0:256].rearrange("p (c s) -> p c s", c=2)[:, :, 0:TP], ACT.Copy)\
            .then_inc(self.attT_ready, 1)

    def copy(self, eng, b, g, j, mine):
        nc, k, t = self.nc, self.k, self.first_turn[g] + j
        if t % 2 != mine:
            return
        if t >= 2:
            eng.wait_ge(self.used, b * self.turns + t - 1)
        eng.wait_ge(self.turned, b * self.turns + t + 1)
        dst, src = k.PTG[t % 2][:, :], k.T[0:TP, t % 2, 0:NE * TP]
        if mine:
            nc.vector.tensor_copy(dst, src).then_inc(self.copied[1], 1)
        else:
            nc.scalar.activation(dst, src, ACT.Copy).then_inc(self.copied[0], 1)

    def vector(self, dve, b):
        nc, k, N = self.nc, self.k, len(self.groups)
        for g in range(N + 1):
            nb = self.groups[g - 1][0] + 1 if g else 0
            for j in range(max(NE if g < N else 0, nb)):
                if 0 < g < N and j < NE:
                    self.maxima(dve, b, g, j)
                if j < nb:
                    self.copy(dve, b, g - 1, j, 1)
            if g % NH == 1 and g > NH:
                self.normalise(dve, b, g // NH - 1)
            if g % NH == 3 and g > NH:
                self.keep_gate(dve, b, g // NH - 1)
        self.normalise(dve, b, NT - 1)
        self.keep_gate(dve, b, NT - 1)

    def keep_gate(self, dve, b, i):
        dve.wait_ge(self.gate_made, NT * b + i + 1)
        self.nc.vector.tensor_copy(self.k.logits[:, i * 16:(i + 1) * 16], self.k.MI[0:TP, 256:272])\
            .then_inc(self.gate_kept, 1)

    def normalise(self, dve, b, i):
        nc, k = self.nc, self.k
        dve.wait_ge(self.out_turned, NT * b + i + 1)
        inverse_sums(nc, dve, k, 16 * i, 16 * i + 16, i == 4)
        a4 = k.att[:, i, :].rearrange("p (n e d) -> p n e d", n=NH, e=NE)
        nc.vector.tensor_tensor(a4, k.MI[0:TP, :].rearrange("p (e n d) -> p n e d", e=NE, n=NH)[:, :, :, 0:HD],
                                k.rinv[:, 16 * i:16 * i + 16].rearrange("p (n e) -> p n e", n=NH).unsqueeze(3)
                                .to_broadcast([TP, NH, NE, HD]), ALU.mult)
        dve.drain()
        live = k.live_sx[:, i * 64:(i + 1) * 64].rearrange("p (n d) -> p n d", n=NH).unsqueeze(2)\
            .to_broadcast([TP, NH, NE, HD])
        nc.vector.tensor_tensor(a4, a4, live, ALU.mult).then_inc(self.kept, 1)


def minus_max(nc, dve, k, scores, u, w, done):
    if w <= 500 or w == 750:
        src = scores[0:TP, 0, 0:w] if w <= 500 else scores[0:TP, :, 0:375]
        nc.vector.tensor_reduce(k.nmax[:, u:u + 1], src, AXX if w <= 500 else mybir.AxisListType.XY,
                                ALU.max, negate=True).then_inc(done, 1)
        return
    nc.vector.reduce_max(k.mtmp[:, 2 * u:2 * u + 1], scores[0:TP, 0, 0:375], AXX)
    nc.vector.reduce_max(k.mtmp[:, 2 * u + 1:2 * u + 2], scores[0:TP, 1, 0:w - 375], AXX)
    dve.drain()
    nc.vector.tensor_reduce(k.nmax[:, u:u + 1], k.mtmp[:, 2 * u:2 * u + 2], AXX, ALU.max, negate=True).then_inc(done, 1)


def exp_rows(nc, k, buf, at, u, w, done):
    bias, scores = k.nmax[:, u:u + 1], k.S[u % 2]
    if w <= 500 or w == 750:
        dst, src = buf[:, at:at + w], scores[0:TP, 0, 0:min(w, 500)]
        if w == 750:
            dst, src = dst.rearrange("p (h w) -> p h w", h=2), scores[0:TP, :, 0:375]
        nc.scalar.activation(dst, src, ACT.Exp, bias=bias, accum_out=k.rsum[:, u:u + 1]).then_inc(done, 1)
        return
    nc.scalar.activation(buf[:, at:at + 375], scores[0:TP, 0, 0:375], ACT.Exp, bias=bias, accum_out=k.rsum[:, u:u + 1])
    nc.scalar.activation(buf[:, at + 375:at + w], scores[0:TP, 1, 0:w - 375], ACT.Exp, bias=bias,
                         accum_out=k.rsum2[:, u:u + 1]).then_inc(done, 1)


class unit:

    def __init__(self, nb, q, keys, value, out, masked):
        self.nb, self.q, self.keys, self.value, self.out, self.masked = nb, q, keys, value, out, masked


def inverse_sums(nc, dve, k, lo, hi, split):
    if split:
        nc.vector.tensor_tensor(k.rinv[:, lo:hi], k.rsum[:, lo:hi], k.rsum2[:, lo:hi], ALU.add)
        dve.drain()
        nc.vector.reciprocal(k.rinv[:, lo:hi], k.rinv[:, lo:hi])
    else:
        nc.vector.reciprocal(k.rinv[:, lo:hi], k.rsum[:, lo:hi])
    dve.drain()



def clear(nc, k):
    with nc.Block() as block:
        @block.gpsimd
        def _(pool):
            nc.gpsimd.memset(k.minus_half[:, :], -0.5)
            nc.gpsimd.memset(k.plus_half[:, :], 0.5)
            nc.gpsimd.memset(k.ident[:, :], 0.0)
            nc.gpsimd.memset(k.ident_bf[:, :], 0.0)
            nc.gpsimd.memset(k.causal[:, :], 0.0)
            pool.drain()
            for m in (k.ident, k.ident_bf):
                nc.gpsimd.affine_select(out=m[:, :], in_=m[:, :], compare_op=ALU.not_equal, fill=1.0,
                                        base=0, pattern=[[-1, 128]], channel_multiplier=1)
            nc.gpsimd.affine_select(out=k.causal[:, :], in_=k.causal[:, :], compare_op=ALU.is_ge, fill=NEG,
                                    base=0, pattern=[[-1, TP]], channel_multiplier=1)
            nc.gpsimd.iota(k.place_i[:, :], pattern=[[1, NC_]], base=0, channel_multiplier=0)
            nc.gpsimd.memset(k.xs[:, :], 1.0)

        @block.vector
        def _(dve):
            for t in (k.W2BD, k.WX, k.R3, k.ATT0, k.WvT, k.HLP, k.HLT, k.WVB, k.GW, k.FC1, k.FC2, k.FG, k.R2, k.WB,
                      k.NW, k.W1Tr, k.R4, k.Mk, k.rsum2, k.wqb, k.wkb, k.BD, k.U[0], k.U[1], k.UR, k.grads, k.sxn,
                      k.Vp, k.kT):
                nc.vector.memset(t[:], 0.0)
            nc.vector.memset(k.ones[:, :], 1.0)
            for t in (k.xT, k.xT2, k.xT3):
                nc.vector.memset(t[64:128, :], 0.0)
            nc.vector.memset(k.x1[:, :, 64:65], 1.0)
            dve.drain()
            for t in (k.xT, k.xT2, k.xT3):
                nc.vector.memset(t[64:65, :], 1.0)
            nc.vector.memset(k.R2[64:65, 64:65], 1.0)


def load_weights(nc, k, A, sem):
    done = sem("weights_loaded")
    qkv = [
        (k.WX[0:4, 0:64], A["W1T"]), (k.WX[4:8, 64:128], A["W1T"]),
        (k.R3[0:4, :], A["W3T"]), (k.R3[8:9, :], A["b3"]), (k.R3[9:10, :], A["b4"]), (k.R3[10:11, :], A["b4"]),
        (k.W2BD[0:64, 0:64], A["W2T"]), (k.W2BD[64:128, 64:128], A["W2T"]),
        (k.W4[0:64, :], A["W4T"]), (k.W4[64:128, :], A["W4T"]),
        (k.WqN[:, :], A["attn_Wq"]), (k.WkN[:, :], A["attn_Wk"]), (k.WvT[0:64, :], A["attn_WvT"]),
        (k.HLT[0:64, :], A["hlT"]), (k.HLT[64:65, :], A["hl_b"]),
        (k.GW[0:64, 0, 0:4], A["gwT"][0]), (k.GW[64:128, 0, 4:8], A["gwT"][1]),
        (k.GW[0:64, 1, 8:12], A["gwT"][2]), (k.GW[64:128, 1, 12:16], A["gwT"][3]),
        (k.GB[:, :], A["gb"]), (k.FG[0:64, :], A["fgT"]),
        (k.R2[0:64, 0:64], A["Wk1"]), (k.R2[0:64, 129:193], A["Wv1"]), (k.R2[0:64, 193:194], A["Wlr"]),
        (k.R2[64:65, 193:194], A["blr"]),
        (k.WB[0:64, 0:64], A["Ws"][0]), (k.WB[0:64, 64:128], A["Ws"][1]),
        (k.WB[64:65, :], A["bs"]), (k.W1Tr[0:64, :], A["Ws1T"]), (k.WkT1[:, :], A["WkT1"]), (k.WqT1[:, :], A["WqT1"]),
        (k.R4[0:64, 0:64], A["Wq1"]), (k.WPK[:, :], A["wpk"]), (k.KPK[:, :], A["kpk"]),
    ]
    for j in range(2):
        for r, n in ((8, "b1"), (9, "b2")):
            qkv.append((k.WX[r:r + 1, 64 * j:64 * j + 64], A[n]))
    for n in range(NH):
        s = slice(16 * n, 16 * n + 16)
        p = slice(32 * n, 32 * n + 16)
        qkv += [(k.HLP[0:64, p], A["hlT"][:, s]), (k.HLP[64:65, p], A["hl_b"][:, s]),
                (k.WVB[p, s], A["wvT"][n]), (k.wkb[p, p], A["wk"][n]),
                (k.FC1[s, s], A["fc1T"]), (k.FC1[64:65, s], A["fc1_b"]),
                (k.FC2[s, s], A["fc2T"]), (k.FC2[64:65, s], A["fc2_b"])]
        qkv += [(k.wqb[p, e, p], A["wq"][n, e]) for e in range(NE)]
    for t, n in ((k.LNG, "ln_g"), (k.LNB, "ln_b"), (k.FNG, "fn_g"), (k.FNB, "fn_b")):
        qkv.append((t[:, :], A[n].to_broadcast([TP, 16])))
    for h in range(PH):
        qkv += [(k.BD[0:64, h, 0:64], A["WqpT"][64 * h:64 * h + 64, :]),
                (k.BD[64:128, h, 64:128], A["Wo"][64 * h:64 * h + 64, :])]
    with nc.Block() as block:
        @block.sync
        def _(sp):
            for dst, src in qkv[0::2]:
                sp.dma_start(dst, src).then_inc(done, 16)
            sp.wait_ge(done, 16 * len(qkv))

        @block.scalar
        def _(act):
            for dst, src in qkv[1::2]:
                act.dma_start(dst, src).then_inc(done, 16)


def weight_products(nc, k, sem):
    made, kept = sem("weight_products_made"), sem("weight_products_kept")
    with nc.Block() as block:
        @block.tensor
        def _(pe):
            nc.tensor.matmul(k.PV[0:64, 0:64], k.WkN[:, :], k.WqN[:, :], start=True, stop=True)
            nc.tensor.matmul(k.PV[0:64, 64:128], k.WkT1[:, :], k.WB[0:64, 0:64], start=True, stop=True).then_inc(made, 1)
            for e in range(NE):
                last = nc.tensor.matmul(k.MI[:, e * 128:(e + 1) * 128], k.wqb[:, e, :], k.wkb[:, :],
                                        start=True, stop=True)
            last.then_inc(made, 1)
            for h in range(PH):
                for p in range(2):
                    c = (h * 2 + p) * 64
                    last = nc.tensor.matmul(k.S[0][0:64, c // 512, c % 512:c % 512 + 64],
                                            k.WPK[:, (p * PH + h) * 64:(p * PH + h + 1) * 64],
                                            k.KPK[:, (p * PH + h) * 64:(p * PH + h + 1) * 64], start=True, stop=True)
            last.then_inc(made, 1)

        @block.vector
        def _(dve):
            dve.wait_ge(made, 1)
            nc.vector.tensor_copy(k.ATT0[0:64, :], k.PV[0:64, 0:64])
            nc.vector.tensor_copy(k.R2[0:64, 65:129], k.PV[0:64, 64:128])
            nc.vector.tensor_copy(k.R2[64:65, 65:129], k.WB[64:65, 0:64])
            dve.wait_ge(made, 2)
            nc.vector.tensor_scalar_mul(k.LB[:, :, :], k.MI[:, :].rearrange("p (e c) -> p e c", e=NE), HD ** 0.5)
            dve.wait_ge(made, 3)
            nc.vector.tensor_copy(k.Mk[0:64, :].rearrange("p (a c) -> p a c", a=2), k.S[0][0:64, :, :])
            nc.vector.tensor_copy(k.place[:, :], k.place_i[:, :])
            nc.vector.tensor_scalar_mul(k.BD[0:64, :, :], k.BD[0:64, :, :], D ** -0.5)


def build_table(nc, k, A, sem):
    loaded, stored = [sem("even_rows_loaded"), sem("odd_rows_loaded")], [sem("even_rows_stored"), sem("odd_rows_stored")]
    turned, turned_kept = sem("rows_turned"), sem("turned_rows_kept")
    mapped, mapped_kept = sem("rows_mapped"), sem("mapped_rows_kept")
    N = ROWS // 1024

    def in_pairs(eng, step):
        step(0, 0)
        step(1, 1)
        with eng.Fori(1, N // 2 - 1) as pair:
            step(2 * pair, 0)
            step(2 * pair + 1, 1)
        step(N - 2, 0)
        step(N - 1, 1)

    def is_first(i):
        return isinstance(i, int) and i < 2

    def is_last(i):
        return isinstance(i, int) and i == N - 1

    with nc.Block() as block:
        @block.sync
        def _(sp):
            def load(i, q):
                for c, n in ((0, "keys"), (64, "values")):
                    src = A[n].rearrange("(i p j) d -> i p j d", p=128, j=8)[bass.ds(i, 1), :, :, :]
                    sp.dma_start(k.rows_in[q][:, :, c:c + 64], src.rearrange("a p j d -> (a p) j d"))\
                        .then_inc(loaded[q], 16)

            def step(i, q):
                if not is_last(i):
                    sp.wait_ge(turned, i)
                    load(i + 1, 1 - q)
                sp.wait_ge(mapped_kept, 2 * i + 2)
                dst = k.table.rearrange("(i p j) d -> i p (j d)", p=128, j=8)
                sp.dma_start(row(dst, i), k.rows_out[q][:, :]).then_inc(stored[q], 16)

            load(0, 0)
            in_pairs(sp, step)
            for q in range(2):
                sp.wait_ge(stored[q], 8 * N)

        @block.tensor
        def _(pe):
            def turn_rows(i, q):
                pe.wait_ge(loaded[q], 32 * (i >> 1) + 32)
                pe.wait_ge(turned_kept, 2 * i)
                for j in range(8):
                    last = nc.tensor.transpose(k.S[0][:, j // 4, (j % 4) * 128:(j % 4 + 1) * 128],
                                               k.rows_in[q][:, j, :], k.ident[:, :])
                last.then_inc(turned, 1)

            def step(i, q):
                if not is_last(i):
                    turn_rows(i + 1, 1 - q)
                pe.wait_ge(turned_kept, 2 * i + 2)
                pe.wait_ge(mapped_kept, 2 * i)
                for j in range(8):
                    last = nc.tensor.matmul(k.S[1][:, j // 4, (j % 4) * 128:(j % 4 + 1) * 128],
                                            k.rows_turned[q][:, j * 128:(j + 1) * 128],
                                            k.BD[:, :, :].rearrange("p h c -> p (h c)")[:, bass.ds(((i >> 2) & (PH - 1)) * 128, 128)],
                                            start=True, stop=True)
                last.then_inc(mapped, 1)

            turn_rows(0, 0)
            in_pairs(pe, step)

        def copies(eng, copy, bank):
            cols = slice(512 * bank, 512 * bank + 512)

            def keep_turned(i, q):
                eng.wait_ge(turned, i + 1)
                copy(k.rows_turned[q][:, cols], k.S[0][:, bank, :]).then_inc(turned_kept, 1)

            def step(i, q):
                if not is_last(i):
                    eng.wait_ge(mapped, i)
                    keep_turned(i + 1, 1 - q)
                eng.wait_ge(mapped, i + 1)
                if not is_first(i):
                    eng.wait_ge(stored[q], 16 * (i >> 1))
                copy(k.rows_out[q][:, cols], k.S[1][:, bank, :]).then_inc(mapped_kept, 1)

            keep_turned(0, 0)
            in_pairs(eng, step)

        @block.scalar
        def _(act):
            copies(act, lambda dst, src: nc.scalar.activation(dst, src, ACT.Copy), 0)

        @block.vector
        def _(dve):
            copies(dve, lambda dst, src: nc.vector.tensor_copy(dst, src), 1)



def tok_and_attention(nc, k, A, sem):
    xs_loaded, tok_products, tok_done = sem("xs_loaded"), sem("tok_products"), sem("tok_steps_done")
    tok_out, h1_ready, xn_ready = sem("tok_out"), sem("h1_ready"), sem("xn1_ready")
    xn_turned, xT_ready, kT_made, kT_ready = sem("xn1_turned"), sem("xT1_ready"), sem("kT1_made"), sem("kT1_ready")
    v_made, v_ready, h2_ready = sem("v1_made"), sem("v1_ready"), sem("h2_ready")
    xn2_ready, xn2_turned, xT2_ready = sem("xn2_ready"), sem("xn2_turned"), sem("xT2_ready")
    h2_stored, xT2_stored = sem("h2_stored"), sem("xT2_stored")
    k.var_ready, k.rstd_ready = sem("p1_var_ready"), sem("p1_rstd_ready")
    INCS = 2 * (STEPS - 1) + 4
    units = [unit(NT, k.xT[:, t * TP:(t + 1) * TP], k.kT[:, :],
                  lambda b: k.V[:, b * 64:(b + 1) * 64], k.PV[0:TP, t * 64:(t + 1) * 64], False) for t in range(NT)]
    att = Attention(nc, k, sem, "a1", units)
    with nc.Block() as block:
        @block.sync
        def _(sp):
            def load(b):
                sp.dma_start(k.xs[0:4, :], row(A["x"], b)).then_inc(xs_loaded, 16)
                sp.dma_start(k.xs[4:8, :], row(A["xr"], b)).then_inc(xs_loaded, 16)

            def store(b):
                sp.wait_ge(h2_ready, b + 1)
                sp.dma_start(row(k.d_h2, b), k.h2[:, :]).then_inc(h2_stored, 16)
                sp.wait_ge(xT2_ready, b + 1)
                sp.dma_start(row(k.d_xT2, b), k.xT2[0:64, :]).then_inc(xT2_stored, 16)

            load(0)
            with sp.Fori(0, B - 1) as b:
                sp.wait_ge(tok_out, b + 1)
                load(b + 1)
                store(b)
            store(B - 1)
            sp.wait_ge(h2_stored, 16 * B)
            sp.wait_ge(xT2_stored, 16 * B)

        @block.tensor
        def _(pe):
            def turn_xn2(b):
                wait_apart(pe, xn2_ready, b + 1)
                turn(nc, k, k.xn)
                k.turned_last.then_inc(xn2_turned, 1)

            def tok(b, after):
                pe.wait_ge(xs_loaded, 32 * b + 32)
                for s in range(STEPS):
                    if s == STEPS - 2 and after:
                        turn_xn2(b - 1)
                    for h in range(2):
                        out = k.S[s % 2][:, h, 0:HALF]
                        last = nc.tensor.matmul(out, k.WX[:, :], k.xs[:, h * HALF:(h + 1) * HALF],
                                                start=True, stop=s == 0)
                        if s:
                            pe.wait_ge(tok_done, b * INCS + 2 * s - 1 + h)
                            last = nc.tensor.matmul(out, k.W2BD[:, :], k.U[(s - 1) % 2][:, h * HALF:(h + 1) * HALF],
                                                    start=False, stop=True)
                        last.then_inc(tok_products, 1)
                pe.wait_ge(tok_done, b * INCS + INCS)
                if after:
                    pe.wait_ge(h2_ready, b)
                for t in range(NT):
                    out, cols = k.PV[0:TP, t * 64:(t + 1) * 64], slice(t * TP, (t + 1) * TP)
                    nc.tensor.matmul(out, k.xs[:, cols], k.R3[:, :], start=True, stop=False)
                    last = nc.tensor.matmul(out, k.UR[:, cols], k.W4[:, :], start=False, stop=True)
                last.then_inc(tok_out, 1)

            def attention(b):
                pe.wait_ge(xT2_ready, b)
                wait_apart(pe, xn_ready, b + 1)
                turn(nc, k, k.xn)
                k.turned_last.then_inc(xn_turned, 1)
                wait_apart(pe, xT_ready, b + 1)
                for h in range(2):
                    last = nc.tensor.matmul(k.S[1][0:64, h, 0:HALF], k.ATT0[:, :], k.xT[:, h * HALF:(h + 1) * HALF],
                                            start=True, stop=True)
                last.then_inc(kT_made, 1)
                for t in range(NT):
                    last = nc.tensor.matmul(k.MI[0:TP, t * 64:(t + 1) * 64], k.xT[:, t * TP:(t + 1) * TP],
                                            k.WvT[:, :], start=True, stop=True)
                last.then_inc(v_made, 1)
                pe.wait_ge(kT_ready, b + 1)
                pe.wait_ge(v_ready, b + 1)
                for m in range(NT + 2):
                    att.tensor(pe, b, m)

            tok(0, False)
            with pe.Fori(0, B - 1) as b:
                attention(b)
                tok(b + 1, True)
            attention(B - 1)
            turn_xn2(B - 1)

        @block.scalar
        def _(act):
            def keep_xn2(b):
                act.wait_ge(xn2_turned, b + 1)
                act.wait_ge(xT2_stored, 16 * b)
                nc.scalar.activation(halves(k.xT2[0:64, :]), k.T[0:64, :, 0:HALF], ACT.Copy).then_inc(xT2_ready, 1)

            def tok(b, after):
                for s in range(STEPS - 1):
                    if s == STEPS - 2 and after:
                        keep_xn2(b - 1)
                    for h in range(2):
                        act.wait_ge(tok_products, b * 2 * STEPS + 2 * s + h + 1)
                        nc.scalar.activation(k.U[s % 2][:, 1 + h * HALF:1 + (h + 1) * HALF],
                                             k.S[s % 2][:, h, 0:HALF], ACT.Relu).then_inc(tok_done, 1)
                s = STEPS - 1
                act.wait_ge(tok_products, b * 2 * STEPS + 2 * s + 2)
                for h in range(2):
                    nc.scalar.activation(k.UR[0:64, 1 + h * HALF:1 + (h + 1) * HALF],
                                         k.S[1][0:64, h, 0:HALF], ACT.Relu).then_inc(tok_done, 1)
                nc.scalar.activation(k.UR[64:128, 0:HALF - 1], k.S[1][64:128, 1, HALF - 2::-1], ACT.Relu)\
                    .then_inc(tok_done, 1)
                nc.scalar.activation(k.UR[64:128, HALF - 1:L - 1], k.S[1][64:128, 0, HALF - 1::-1], ACT.Relu)\
                    .then_inc(tok_done, 1)
                act.wait_ge(tok_out, b + 1)
                nc.scalar.activation(k.h1[:, :], k.PV[0:TP, 0:384], ACT.Relu).then_inc(h1_ready, 1)

            def attention(b):
                act.wait_ge(xn_turned, b + 1)
                nc.scalar.activation(halves(k.xT[0:64, :]), k.T[0:64, :, 0:HALF], ACT.Copy).then_inc(xT_ready, 1)
                act.wait_ge(kT_made, b + 1)
                nc.scalar.activation(halves(k.kT[0:64, :]), k.S[1][0:64, :, 0:HALF], ACT.Copy).then_inc(kT_ready, 1)
                for m in range(NT + 2):
                    att.scalar(act, b, m)

            tok(0, False)
            with act.Fori(0, B - 1) as b:
                attention(b)
                tok(b + 1, True)
            attention(B - 1)
            keep_xn2(B - 1)

        @block.gpsimd
        def _(pool):
            with pool.Fori(0, B) as b:
                for n in range(2):
                    rsqrt(nc, pool, k, NT, b * 2 + n + 1)

        @block.vector
        def _(dve):
            with dve.Fori(0, B) as b:
                dve.wait_ge(h1_ready, b + 1)
                dve.wait_ge(xn2_turned, b)
                layernorm(nc, dve, k, tiles(k.h1), tiles(k.xn), NT, D, 1e-5,
                          lambda: dve.wait_ge(k.rstd_ready, 2 * b + 1), xn_ready)
                dve.wait_ge(v_made, b + 1)
                nc.vector.tensor_copy(k.V[:, :], k.MI[0:TP, 0:384]).then_inc(v_ready, 1)
                for m in range(NT + 2):
                    att.vector(dve, b, m)
                inverse_sums(nc, dve, k, 0, NT, False)
                dve.wait_ge(att.out_ready, NT * b + NT)
                nc.vector.tensor_tensor(tiles(k.tmp), tiles(k.PV[0:TP, 0:384]), bcast(k.rinv[:, 0:NT], D), ALU.mult)
                dve.drain()
                dve.wait_ge(h2_stored, 16 * b)
                nc.vector.scalar_tensor_tensor(k.h2[:, :], k.tmp[:, :], D ** -0.5, k.h1[:, :], ALU.mult, ALU.add)\
                    .then_inc(h2_ready, 1)
                dve.drain()
                layernorm(nc, dve, k, tiles(k.h2), tiles(k.xn), NT, D, 1e-5,
                          lambda: dve.wait_ge(k.rstd_ready, 2 * b + 2), xn2_ready)


def tiles(ap, w=D):
    ap = ap if isinstance(ap, bass.AP) else ap[:, :]
    return ap.rearrange("p (t w) -> p t w", w=w)


def halves(ap):
    return ap.rearrange("p (h w) -> p h w", h=2)


def turn(nc, k, src):
    for t in range(NT):
        k.turned_last = nc.tensor.transpose(k.T[0:64, t // 3, (t % 3) * TP:(t % 3 + 1) * TP],
                                            src[:, t * 64:(t + 1) * 64], k.ident[0:TP, 0:TP])



def residuals(nc, k, A, sem):
    loaded, made, kept = sem("resid_x_loaded"), sem("resid_made"), sem("resid_kept")
    with nc.Block() as block:
        @block.sync
        def _(sp):
            for n in range(NH):
                sp.wait_ge(made, n)
                sp.dma_start(k.xT2[0:64, :], k.d_xT2[n]).then_inc(loaded, 16)

        @block.tensor
        def _(pe):
            for n in range(NH):
                pe.wait_ge(loaded, 16 * n + 16)
                pe.wait_ge(kept, n)
                for t in range(NT):
                    last = nc.tensor.matmul(k.MI[0:TP, t * 16:(t + 1) * 16], k.xT2[:, t * TP:(t + 1) * TP],
                                            k.HLT[:, n * 16:(n + 1) * 16], start=True, stop=True)
                last.then_inc(made, 1)

        @block.vector
        def _(dve):
            for n in range(NH):
                dve.wait_ge(made, n + 1)
                nc.vector.tensor_copy(tiles(k.resid)[:, :, n * 16:(n + 1) * 16], tiles(k.MI[0:TP, 0:96], 16))\
                    .then_inc(kept, 1)


def softmax4(nc, dve, k, logits, groups, exp_in, exp_done, n):
    g, e = k.soft[:, 0:groups * 4].rearrange("p (g e) -> p g e", e=4), \
        k.soft_exp[:, 0:groups * 4].rearrange("p (g e) -> p g e", e=4)
    nc.vector.reduce_max(k.soft_m[:, 0:groups], logits, AXX)
    dve.drain()
    nc.vector.tensor_tensor(g, logits, bcast(k.soft_m[:, 0:groups], 4), ALU.subtract).then_inc(exp_in, 1)
    dve.wait_ge(exp_done, n)
    nc.vector.reduce_sum(k.soft_m[:, 0:groups], e, AXX)
    dve.drain()
    nc.vector.reciprocal(k.soft_m[:, 0:groups], k.soft_m[:, 0:groups])
    dve.drain()
    nc.vector.tensor_tensor(g, e, bcast(k.soft_m[:, 0:groups], 4), ALU.mult)
    dve.drain()


def sigmoid_of_exp(nc, dve, dst, e):
    nc.vector.tensor_scalar_add(dst, e, 1.0)
    dve.drain()
    nc.vector.reciprocal(dst, dst)
    dve.drain()


def r2_place(k, t):
    bank = (k.S[0][:, 0, :], k.S[0][:, 1, :], k.S[1][:, 0, :])[t // 2]
    return bank[0:TP, (t % 2) * 194:(t % 2 + 1) * 194]


def ffn_and_gradients(nc, k, A, sem):
    h2_loaded, x_loaded, sxT_made, sxT_ready = sem("h2_loaded"), sem("xT2_loaded"), sem("sxT_made"), sem("sxT_ready")
    sx_made, sx_ready, u_made, u_ready = sem("sx_made"), sem("sx_ready"), sem("u_made"), sem("u_ready")
    v_made, v_ready, sxn_ready = sem("v2_made"), sem("v2_ready"), sem("sx_by_head_ready")
    soft_in, soft_exp = sem("soft_in"), sem("soft_exp")
    src_ready, turned, turned_kept = sem("p2_turn_source"), sem("p2_turned"), sem("p2_turned_kept")
    fc1_made, fc2_made, fg_made, r2_made = sem("fc1_made"), sem("fc2_made"), sem("fgate_made"), sem("r2_made")
    g_ready, z1_made, e1_ready, dx_made = sem("x0_ready"), sem("z1_made"), sem("e1_ready"), sem("dx_made")
    dz0_ready, grads_made, grads_kept = sem("dz0_ready"), sem("grads_made"), sem("grads_kept")
    h3_ready, h3_stored, xT3_stored = sem("h3_ready"), sem("h3_stored"), sem("xT3_stored")
    k.var_ready, k.rstd_ready = sem("p2_var_ready"), sem("p2_rstd_ready")
    att = ExpertAttention(nc, k, sem, grads_kept)
    TURNS = 6
    with nc.Block() as block:
        @block.sync
        def _(sp):
            def load_x(b):
                sp.dma_start(k.xT2[0:64, :], row(k.d_xT2, b)).then_inc(x_loaded, 16)

            def store(b):
                sp.wait_ge(h3_ready, b + 1)
                sp.dma_start(row(k.d_h3, b), k.h3[:, :]).then_inc(h3_stored, 16)
                sp.wait_ge(turned_kept, TURNS * b + 4)
                sp.dma_start(row(k.d_xT3, b), k.xT3[0:64, :]).then_inc(xT3_stored, 16)

            def load_h2(b):
                sp.dma_start(k.h2[:, :], row(k.d_h2, b)).then_inc(h2_loaded, 16)

            load_x(0)
            load_h2(0)
            with sp.Fori(0, B - 1) as b:
                sp.wait_ge(sx_made, b + 1)
                load_x(b + 1)
                store(b)
                load_h2(b + 1)
            store(B - 1)
            sp.wait_ge(h3_stored, 16 * B)
            sp.wait_ge(xT3_stored, 16 * B)

        @block.tensor
        def _(pe):
            def turned_of(b, n, src):
                wait_apart(pe, src_ready, TURNS * b + n)
                turn(nc, k, src)
                k.turned_last.then_inc(turned, 1)
                pe.wait_ge(turned_kept, TURNS * b + n)

            def per_tile(weights, width, x, done, bank=k.MI):
                for t in range(NT):
                    last = nc.tensor.matmul(bank[0:TP, t * width:(t + 1) * width], x[:, t * TP:(t + 1) * TP],
                                            weights, start=True, stop=True)
                last.then_inc(done, 1)

            def prepare(b):
                pe.wait_ge(x_loaded, 16 * b + 16)
                for h in range(2):
                    last = nc.tensor.matmul(k.S[0][:, h, 0:HALF], k.HLP[:, :], k.xT2[:, h * HALF:(h + 1) * HALF],
                                            start=True, stop=True)
                last.then_inc(sxT_made, 1)
                per_tile(k.HLT[:, :], 64, k.xT2, sx_made, k.PV)
                pe.wait_ge(sxT_ready, b + 1)
                for e in range(NE):
                    if e >= 2:
                        pe.wait_ge(u_ready, 4 * b + e - 1)
                    for h in range(2):
                        last = nc.tensor.matmul(k.S[(e + 1) % 2][:, h, 0:HALF], k.LB[:, e, :],
                                                k.sxT[:, h * HALF:(h + 1) * HALF], start=True, stop=True)
                    last.then_inc(u_made, 1)

            def values(b):
                pe.wait_ge(sx_ready, b + 1)
                per_tile(k.WVB[:, :], 64, k.sxT, v_made, k.PV)

            def batch(b, more):
                pe.wait_ge(v_ready, b + 1)
                att.tensor(pe, b)
                if more:
                    prepare(b + 1)
                turned_of(b, 1, k.fx)
                per_tile(k.FC1[:, :], 64, k.xT, fc1_made)
                if more:
                    values(b + 1)
                turned_of(b, 2, k.hx)
                per_tile(k.FC2[:, :], 64, k.xT, fc2_made)
                turned_of(b, 3, k.fout)
                per_tile(k.FG[:, :], 4, k.xT, fg_made)
                if more:
                    pe.wait_ge(u_ready, 4 * b + 8)
                turned_of(b, 4, k.xn)
                for t in range(NT):
                    last = nc.tensor.matmul(r2_place(k, t), k.xT3[:, t * TP:(t + 1) * TP], k.R2[:, :],
                                            start=True, stop=True)
                last.then_inc(r2_made, 1)
                wait_apart(pe, src_ready, TURNS * b + 5)
                for t in range(NT):
                    last = nc.tensor.transpose(k.T[0:64, t // 3, (t % 3) * TP:(t % 3 + 1) * TP],
                                               k.x1[:, t, 0:64], k.ident[0:TP, 0:TP])
                last.then_inc(turned, 1)
                pe.wait_ge(turned_kept, TURNS * b + 5)
                per_tile(k.WB[:, 64:128], 64, k.xT, z1_made)
                if more:
                    pe.wait_ge(sxn_ready, b + 2)
                    for e in range(2):
                        att.scores(pe, b + 1, 0, e)
                turned_of(b, 6, k.dz1)
                per_tile(k.W1Tr[:, :], 64, k.xT, dx_made)
                if more:
                    for e in range(2, NE):
                        att.scores(pe, b + 1, 0, e)
                if more:
                    pe.wait_ge(v_ready, b + 2)
                pe.wait_ge(dz0_ready, b + 1)
                for t in range(NT):
                    nc.tensor.matmul(k.PV[0:65, 0:64], k.G[:, t, 0:65], k.dz0[:, t * 64:(t + 1) * 64],
                                     start=t == 0, stop=t == NT - 1)
                for t in range(NT):
                    last = nc.tensor.matmul(k.PV[0:65, 64:128], k.x1[:, t, :], k.dz1[:, t * 64:(t + 1) * 64],
                                            start=t == 0, stop=t == NT - 1)
                last.then_inc(grads_made, 1)

            prepare(0)
            values(0)
            pe.wait_ge(u_ready, 4)
            pe.wait_ge(sxn_ready, 1)
            for e in range(NE):
                att.scores(pe, 0, 0, e)
            with pe.Fori(0, B - 1) as b:
                batch(b, True)
            batch(B - 1, False)

        @block.scalar
        def _(act):
            def keep_turned(b, n, dst):
                act.wait_ge(turned, TURNS * b + n)
                nc.scalar.activation(halves(dst[0:64, :]), k.T[0:64, :, 0:HALF], ACT.Copy).then_inc(turned_kept, 1)

            def prepare(b):
                act.wait_ge(sxT_made, b + 1)
                nc.scalar.activation(halves(k.sxT[:, :]), k.S[0][:, :, 0:HALF], ACT.Copy).then_inc(sxT_ready, 1)
                for e in range(NE):
                    act.wait_ge(u_made, 4 * b + e + 1)
                    nc.scalar.activation(halves(k.UT[:, e, :]), k.S[(e + 1) % 2][:, :, 0:HALF], ACT.Copy)\
                        .then_inc(u_ready, 1)

            def batch(b, more):
                att.scalar(act, b)
                act.wait_ge(soft_in, 2 * b + 1)
                nc.scalar.activation(k.soft_exp[:, 0:96], k.soft[:, 0:96], ACT.Exp).then_inc(soft_exp, 1)
                if more:
                    act.wait_ge(att.gate_made, NT * b + NT)
                    prepare(b + 1)
                for n in (1, 2, 3):
                    keep_turned(b, n, k.xT)
                act.wait_ge(soft_in, 2 * b + 2)
                nc.scalar.activation(k.soft_exp[:, 0:24], k.soft[:, 0:24], ACT.Exp).then_inc(soft_exp, 1)
                act.wait_ge(xT3_stored, 16 * b)
                keep_turned(b, 4, k.xT3)
                act.wait_ge(r2_made, b + 1)
                for c in range(3):
                    src = (k.S[0][0:TP, 0, :], k.S[0][0:TP, 1, :], k.S[1][0:TP, 0, :])[c][:, 0:388]\
                        .rearrange("p (a w) -> p a w", a=2)
                    nc.scalar.activation(k.G[:, 2 * c:2 * c + 2, :], src, ACT.Copy)
                    last = nc.scalar.activation(k.E0[:, 2 * c:2 * c + 2, 0:64], src[:, :, 65:129], ACT.Exp, scale=-1.0)
                    last = nc.scalar.activation(k.E0[:, 2 * c:2 * c + 2, 64:65], src[:, :, 193:194], ACT.Exp, scale=-1.0)
                last.then_inc(g_ready, 1)
                keep_turned(b, 5, k.xT)
                act.wait_ge(z1_made, b + 1)
                nc.scalar.activation(k.E1[:, :], k.MI[0:TP, 0:384], ACT.Exp, scale=-1.0).then_inc(e1_ready, 1)
                keep_turned(b, 6, k.xT)
                if more:
                    for e in range(NE):
                        att.exponentials(act, b + 1, 0, e)

            prepare(0)
            for e in range(NE):
                att.exponentials(act, 0, 0, e)
            with act.Fori(0, B - 1) as b:
                batch(b, True)
            batch(B - 1, False)

        @block.gpsimd
        def _(pool):
            def keys_by_head(b):
                wait_apart(pool, sxT_ready, b + 1)
                for n in range(NH):
                    p = slice(32 * n, 32 * n + 16)
                    last = nc.gpsimd.tensor_copy(k.sxn[p, n, :], k.sxT[p, :])
                last.then_inc(sxn_ready, 1)

            def batch(b, more):
                rsqrt(nc, pool, k, NT * NH, 3 * b + 1)
                if more:
                    pool.drain()
                    keys_by_head(b + 1)
                    pool.drain()
                rsqrt(nc, pool, k, NT * NH, 3 * b + 2)
                rsqrt(nc, pool, k, NT, 3 * b + 3)

            keys_by_head(0)
            with pool.Fori(0, B - 1) as b:
                batch(b, True)
            batch(B - 1, False)

        @block.vector
        def _(dve):
            def keep_live(b):
                dve.wait_ge(sx_made, b + 1)
                nc.vector.tensor_scalar(k.live_sx[:, :], k.PV[0:TP, 0:384], 0.0, None, ALU.not_equal).then_inc(sx_ready, 1)

            def keep_values(b):
                dve.wait_ge(v_made, b + 1)
                for n in range(NH):
                    last = nc.vector.tensor_copy(k.Vp[:, :, n, 32 * n:32 * n + 16],
                                                 tiles(k.PV[0:TP, 0:384])[:, :, 16 * n:16 * n + 16])
                last.then_inc(v_ready, 1)

            def batch(b, more):
                att.vector(dve, b)
                dve.drain()
                softmax4(nc, dve, k, k.logits[:, :].rearrange("p (g e) -> p g e", e=4), 24, soft_in, soft_exp, 2 * b + 1)
                nc.vector.tensor_tensor(k.big[:, :].rearrange("p (a d) -> p a d", d=16),
                                        k.att[:, :, :].rearrange("p t (a d) -> p (t a) d", d=16),
                                        bcast(k.soft[:, 0:96], 16), ALU.mult)
                dve.drain()
                nc.vector.reduce_sum(tiles(k.mix, 16), k.big[:, :].rearrange("p (g e d) -> p g d e", e=NE, d=HD), AXX)
                dve.drain()
                nc.vector.tensor_tensor(k.mix[:, :], k.mix[:, :], k.resid[:, :], ALU.add)
                dve.drain()
                layernorm(nc, dve, k, tiles(k.mix, 16), tiles(k.fx, 16), 24, 16, 1e-8,
                          lambda: dve.wait_ge(k.rstd_ready, 3 * b + 1), src_ready, k.LNG, k.LNB)
                nc.vector.tensor_scalar(k.live[:, :], k.fx[:, :], 0.0, None, ALU.not_equal)
                dve.drain()
                if more:
                    keep_live(b + 1)
                dve.wait_ge(fc1_made, b + 1)
                nc.vector.scalar_tensor_tensor(k.hx[:, :], k.MI[0:TP, 0:384], 0.0, k.live[:, :], ALU.max, ALU.mult)\
                    .then_inc(src_ready, 1)
                if more:
                    keep_values(b + 1)
                dve.wait_ge(fc2_made, b + 1)
                nc.vector.tensor_tensor(k.mix[:, :], k.MI[0:TP, 0:384], k.live[:, :], ALU.mult)
                dve.drain()
                nc.vector.tensor_tensor(k.mix[:, :], k.mix[:, :], k.fx[:, :], ALU.add)
                dve.drain()
                layernorm(nc, dve, k, tiles(k.mix, 16), tiles(k.fout, 16), 24, 16, 1e-8,
                          lambda: dve.wait_ge(k.rstd_ready, 3 * b + 2), src_ready, k.FNG, k.FNB)
                dve.wait_ge(fg_made, b + 1)
                softmax4(nc, dve, k, k.MI[0:TP, 0:24].rearrange("p (g e) -> p g e", e=4), NT, soft_in, soft_exp, 2 * b + 2)
                nc.vector.tensor_tensor(tiles(k.mix, 16), tiles(k.fout, 16), bcast(k.soft[:, 0:24], 16), ALU.mult)
                dve.drain()
                dve.wait_ge(h3_stored, 16 * b)
                dve.wait_ge(h2_loaded, 16 * b + 16)
                nc.vector.tensor_tensor(k.h3[:, :], k.mix[:, :], k.h2[:, :], ALU.add).then_inc(h3_ready, 1)
                dve.drain()
                layernorm(nc, dve, k, tiles(k.h3), tiles(k.xn), NT, D, 1e-5,
                          lambda: dve.wait_ge(k.rstd_ready, 3 * b + 3), src_ready)
                dve.wait_ge(g_ready, b + 1)
                x0, z0, tgt = k.G[:, :, 0:64], k.G[:, :, 65:129], k.G[:, :, 129:193]
                sigmoid_of_exp(nc, dve, k.E0[:, :, :], k.E0[:, :, :])
                s0 = k.E0[:, :, 0:64]
                nc.vector.tensor_scalar_mul(k.alr[:, :].unsqueeze(2), k.E0[:, :, 64:65], 0.1 * 2.0 / D)
                nc.vector.tensor_tensor(tiles(k.silu), z0, s0, ALU.mult)
                dve.drain()
                nc.vector.tensor_tensor(k.x1[:, :, 0:64], x0, tiles(k.silu), ALU.add).then_inc(src_ready, 1)
                slope(nc, dve, tiles(k.d0), s0, tiles(k.silu), tiles(k.tmp))
                dve.wait_ge(e1_ready, b + 1)
                sigmoid_of_exp(nc, dve, k.E1[:, :], k.E1[:, :])
                nc.vector.tensor_tensor(k.silu[:, :], k.MI[0:TP, 0:384], k.E1[:, :], ALU.mult)
                dve.drain()
                nc.vector.tensor_tensor(tiles(k.dx), k.x1[:, :, 0:64], tiles(k.silu), ALU.add)
                dve.drain()
                nc.vector.tensor_tensor(tiles(k.dx), tiles(k.dx), tgt, ALU.subtract)
                dve.drain()
                nc.vector.tensor_tensor(tiles(k.dx), tiles(k.dx), bcast(k.alr[:, :], D), ALU.mult)
                slope(nc, dve, k.dz1[:, :], k.E1[:, :], k.silu[:, :], k.tmp[:, :])
                nc.vector.tensor_tensor(k.dz1[:, :], k.dz1[:, :], k.dx[:, :], ALU.mult).then_inc(src_ready, 1)
                if more:
                    for e in range(2):
                        att.maxima(dve, b + 1, 0, e)
                dve.wait_ge(dx_made, b + 1)
                nc.vector.tensor_tensor(k.dx[:, :], k.MI[0:TP, 0:384], k.dx[:, :], ALU.add)
                dve.drain()
                nc.vector.tensor_tensor(k.dz0[:, :], k.dx[:, :], k.d0[:, :], ALU.mult).then_inc(dz0_ready, 1)
                if more:
                    for e in range(2, NE):
                        att.maxima(dve, b + 1, 0, e)
                dve.wait_ge(grads_made, b + 1)
                nc.vector.tensor_tensor(k.grads[:, :], k.grads[:, :], k.PV[0:65, 0:128], ALU.add).then_inc(grads_kept, 1)
                dve.drain()

            keep_live(0)
            keep_values(0)
            for e in range(NE):
                att.maxima(dve, 0, 0, e)
            with dve.Fori(0, B - 1) as b:
                batch(b, True)
            batch(B - 1, False)


def slope(nc, dve, dst, s, silu, tmp):
    nc.vector.tensor_tensor(tmp, silu, s, ALU.mult)
    nc.vector.tensor_tensor(dst, silu, s, ALU.add)
    dve.drain()
    nc.vector.tensor_tensor(dst, dst, tmp, ALU.subtract)
    dve.drain()


def adamw(nc, k, sem):
    squared, rooted, stepped, made = sem("grads_squared"), sem("grads_rooted"), sem("stepped"), sem("wq_w0_made")
    with nc.Block() as block:
        @block.gpsimd
        def _(pool):
            pool.wait_ge(squared, 1)
            nc.gpsimd.tensor_tensor(k.gabs[:, :], k.gsq[:, :], k.plus_half[0:65, 0:1].to_broadcast([65, 128]), ALU.pow)\
                .then_inc(rooted, 1)

        @block.vector
        def _(dve):
            nc.vector.tensor_tensor(k.gsq[:, :], k.grads[:, :], k.grads[:, :], ALU.mult).then_inc(squared, 1)
            dve.wait_ge(rooted, 1)
            nc.vector.tensor_scalar_add(k.gabs[:, :], k.gabs[:, :], 1e-8)
            dve.drain()
            nc.vector.reciprocal(k.gabs[:, :], k.gabs[:, :])
            dve.drain()
            nc.vector.tensor_tensor(k.gabs[:, :], k.gabs[:, :], k.grads[:, :], ALU.mult)
            nc.vector.tensor_scalar_mul(k.NW[0:65, :], k.WB[0:65, :], 1.0 - 0.001 * 0.01)
            dve.drain()
            nc.vector.scalar_tensor_tensor(k.NW[0:65, :], k.gabs[:, :], -0.001, k.NW[0:65, :], ALU.mult, ALU.add)\
                .then_inc(stepped, 1)
            dve.drain()
            dve.wait_ge(made, 1)
            nc.vector.memset(k.R4[64:65, 0:64], 0.0)
            nc.vector.tensor_copy(k.R4[0:64, 64:128], k.MI[0:64, 0:64])
            nc.vector.tensor_copy(k.R4[64:65, 64:128], k.NW[64:65, 0:64])

        @block.tensor
        def _(pe):
            pe.wait_ge(stepped, 1)
            nc.tensor.matmul(k.MI[0:64, 0:64], k.WqT1[:, :], k.NW[0:64, 0:64], start=True, stop=True).then_inc(made, 1)



def retrieve(nc, k, A, out, sem):
    h_loaded, x_loaded, made, g_ready = sem("h3_loaded"), sem("xT3_loaded"), sem("q_made"), sem("q_ready")
    src_ready, turned, turned_kept = sem("p3_turn_source"), sem("p3_turned"), sem("p3_turned_kept")
    z1_made, e1_ready, h4_ready = sem("rz1_made"), sem("re1_ready"), sem("h4_ready")
    h4_stored, xT4_stored = sem("h4_stored"), sem("xT4_stored")
    k.var_ready, k.rstd_ready = sem("p3_var_ready"), sem("p3_rstd_ready")
    with nc.Block() as block:
        @block.sync
        def _(sp):
            def load_xT3(b):
                sp.dma_start(k.xT3[0:64, :], row(k.d_xT3, b)).then_inc(x_loaded, 16)

            def load_h3(b):
                sp.dma_start(k.h3[:, :], row(k.d_h3, b)).then_inc(h_loaded, 16)

            def store(b, more):
                sp.wait_ge(h4_ready, b + 1)
                sp.dma_start(tokens(out, b), tiles(k.h4)).then_inc(h4_stored, 16)
                if more:
                    load_h3(b + 1)
                sp.wait_ge(turned_kept, 2 * b + 2)
                sp.dma_start(row(k.d_xT4, b), k.xT2[0:64, :]).then_inc(xT4_stored, 16)

            load_xT3(0)
            load_h3(0)
            with sp.Fori(0, B - 1) as b:
                sp.wait_ge(made, b + 1)
                load_xT3(b + 1)
                store(b, True)
            store(B - 1, False)
            sp.wait_ge(h4_stored, 16 * B)
            sp.wait_ge(xT4_stored, 16 * B)

        @block.tensor
        def _(pe):
            def queries(b):
                pe.wait_ge(x_loaded, 16 * b + 16)
                for t in range(NT):
                    last = nc.tensor.matmul(k.S[0][0:TP, t // 3, (t % 3) * 128:(t % 3 + 1) * 128],
                                            k.xT3[:, t * TP:(t + 1) * TP], k.R4[:, :], start=True, stop=True)
                last.then_inc(made, 1)

            def rest(b, more):
                pe.wait_ge(turned_kept, 2 * b)
                wait_apart(pe, src_ready, 2 * b + 1)
                turn(nc, k, k.q1)
                k.turned_last.then_inc(turned, 1)
                pe.wait_ge(turned_kept, 2 * b + 1)
                for t in range(NT):
                    last = nc.tensor.matmul(k.MI[0:TP, t * 64:(t + 1) * 64], k.xT[:, t * TP:(t + 1) * TP],
                                            k.NW[:, 64:128], start=True, stop=True)
                last.then_inc(z1_made, 1)
                if more:
                    pe.wait_ge(g_ready, b + 1)
                    queries(b + 1)
                wait_apart(pe, src_ready, 2 * b + 2)
                turn(nc, k, k.xn)
                k.turned_last.then_inc(turned, 1)

            queries(0)
            with pe.Fori(0, B - 1) as b:
                rest(b, True)
            rest(B - 1, False)

        @block.scalar
        def _(act):
            def keep_queries(b):
                act.wait_ge(made, b + 1)
                for c in range(2):
                    src = k.S[0][0:TP, c, 0:384].rearrange("p (a w) -> p a w", a=3)
                    nc.scalar.activation(k.G[:, 3 * c:3 * c + 3, 0:128], src, ACT.Copy)
                    last = nc.scalar.activation(k.E0[:, 3 * c:3 * c + 3, 0:64], src[:, :, 64:128], ACT.Exp, scale=-1.0)
                last.then_inc(g_ready, 1)

            def rest(b, more):
                act.wait_ge(turned, 2 * b + 1)
                nc.scalar.activation(halves(k.xT[0:64, :]), k.T[0:64, :, 0:HALF], ACT.Copy).then_inc(turned_kept, 1)
                act.wait_ge(z1_made, b + 1)
                nc.scalar.activation(k.E1[:, :], k.MI[0:TP, 0:384], ACT.Exp, scale=-1.0).then_inc(e1_ready, 1)
                if more:
                    act.wait_ge(src_ready, 2 * b + 1)
                    keep_queries(b + 1)
                act.wait_ge(turned, 2 * b + 2)
                act.wait_ge(xT4_stored, 16 * b)
                nc.scalar.activation(halves(k.xT2[0:64, :]), k.T[0:64, :, 0:HALF], ACT.Copy).then_inc(turned_kept, 1)

            keep_queries(0)
            with act.Fori(0, B - 1) as b:
                rest(b, True)
            rest(B - 1, False)

        @block.gpsimd
        def _(pool):
            with pool.Fori(0, B) as b:
                rsqrt(nc, pool, k, NT, b + 1)

        @block.vector
        def _(dve):
            with dve.Fori(0, B) as b:
                dve.wait_ge(g_ready, b + 1)
                s0 = k.E0[:, :, 0:64]
                sigmoid_of_exp(nc, dve, s0, s0)
                nc.vector.tensor_tensor(tiles(k.silu), k.G[:, :, 64:128], s0, ALU.mult)
                dve.drain()
                nc.vector.tensor_tensor(tiles(k.q1), k.G[:, :, 0:64], tiles(k.silu), ALU.add).then_inc(src_ready, 1)
                dve.wait_ge(e1_ready, b + 1)
                dve.wait_ge(h_loaded, 16 * b + 16)
                nc.vector.tensor_tensor(k.q1[:, :], k.q1[:, :], k.h3[:, :], ALU.add)
                sigmoid_of_exp(nc, dve, k.E1[:, :], k.E1[:, :])
                nc.vector.tensor_tensor(k.silu[:, :], k.MI[0:TP, 0:384], k.E1[:, :], ALU.mult)
                dve.drain()
                dve.wait_ge(h4_stored, 16 * b)
                nc.vector.tensor_tensor(k.h4[:, :], k.q1[:, :], k.silu[:, :], ALU.add).then_inc(h4_ready, 1)
                dve.drain()
                layernorm(nc, dve, k, tiles(k.h4), tiles(k.xn), NT, D, 1e-5,
                          lambda: dve.wait_ge(k.rstd_ready, b + 1), src_ready)



def product_key_attention(nc, k, out, sem):
    xk_loaded, sims_made, sims_ready = sem("xk_loaded"), sem("sims_made"), sem("sims_ready")
    top_exp_in, top_exp, chosen = sem("top_exp_in"), sem("top_exp"), sem("indices_chosen")
    xa_loaded, acc_loaded, acc_ready, acc_stored = sem("xa_loaded"), sem("acc_loaded"), sem("acc_ready"), sem("acc_stored")
    gathered = [sem(f"gathered_{t}") for t in range(NT)]
    taken = sem("gathered_rows_taken")
    kv_turned, kv_ready = sem("kv_turned"), sem("kT4_ready")
    G = B * PH
    units = [unit(t + 1, k.xT[:, t * TP:(t + 1) * TP], k.kT[:, :],
                  lambda b: k.kv[:, b * 128 + 64:(b + 1) * 128], k.PV[0:TP, t * 64:(t + 1) * 64], True)
             for t in range(NT)]
    att = Attention(nc, k, sem, "a4", units)

    with nc.Block() as block:
        @block.sync
        def _(sp):
            def load_xk(g, b):
                wait_apart(sp, sims_made, g)
                sp.dma_start(k.xT3[0:64, :], row(k.d_xT4, b)).then_inc(xk_loaded, 16)

            def attention_io(g, b, b_last):
                wait_apart(sp, att.out_ready, NT * g)
                sp.dma_start(k.xT[0:64, :], row(k.d_xT4, b)).then_inc(xa_loaded, 16)
                wait_apart(sp, acc_stored, 16 * g)
                sp.dma_start(tiles(k.h4), tokens(out, b)).then_inc(acc_loaded, 16)
                wait_apart(sp, acc_ready, g + 1)
                sp.dma_start(tokens(out, b), tiles(k.h4)).then_inc(acc_stored, 16)

            load_xk(0, 0)
            with sp.Fori(0, G - 1) as g:
                b_next, b_now = ((g + 1) >> 3) & (B - 1), (g >> 3) & (B - 1)
                load_xk(g + 1, b_next)
                attention_io(g, b_now, 0)
            attention_io(G - 1, B - 1, 0)
            sp.wait_ge(acc_stored, 16 * G)

        @block.gpsimd
        def _(pool):
            with pool.Fori(0, G) as g:
                for t in range(NT):
                    wait_apart(pool, chosen, NT * g + t + 1)
                    for j in range(TOPK):
                        pool.indirect_dma_start(
                            out=k.rows[t][:, j * 128:(j + 1) * 128], out_offset=None, in_=k.table,
                            in_offset=bass.IndirectOffsetOnAxis(ap=k.idx[:, t * TOPK + j:t * TOPK + j + 1], axis=0))\
                            .then_inc(gathered[t], 16)

        @block.tensor
        def _(pe):
            def scores_of(g, h):
                pe.wait_ge(xk_loaded, 16 * g + 16)
                pe.wait_ge(sims_ready, 2 * g)
                for t in range(NT):
                    last = nc.tensor.matmul(k.S2[0:TP, t // 3, (t % 3) * 128:(t % 3 + 1) * 128],
                                            k.xT3[:, t * TP:(t + 1) * TP], k.Mk[:, bass.ds(h * 128, 128)],
                                            start=True, stop=True)
                last.then_inc(sims_made, 1)

            def attention(g):
                pe.wait_ge(xa_loaded, 16 * g + 16)
                for m in range(NT + 2):
                    if m < NT:
                        pe.wait_ge(kv_ready, NT * g + m)
                        wait_apart(pe, taken, NT * g + m + 1)
                        nc.tensor.transpose(k.MI[0:64, 0:TP], k.kv[:, m * 128:m * 128 + 64], k.ident[0:TP, 0:TP])\
                            .then_inc(kv_turned, 1)
                        pe.wait_ge(kv_ready, NT * g + m + 1)
                    if m == 2:
                        pe.wait_ge(acc_ready, g)
                    att.tensor(pe, g, m)

            scores_of(0, 0)
            with pe.Fori(0, G - 1) as g:
                h_next = (g + 1) & 7
                scores_of(g + 1, h_next)
                attention(g)
            attention(G - 1)

        @block.scalar
        def _(act):
            def choose(g):
                act.wait_ge(sims_made, g + 1)
                act.wait_ge(top_exp_in, g)
                for c in range(2):
                    nc.scalar.activation(k.sims[:, 3 * c:3 * c + 3, :],
                                         k.S2[0:TP, c, 0:384].rearrange("p (a w) -> p a w", a=3), ACT.Copy)\
                        .then_inc(sims_ready, 1)
                act.wait_ge(top_exp_in, g + 1)
                nc.scalar.activation(k.top_e[:, :], k.top_v[:, :], ACT.Exp).then_inc(top_exp, 1)

            def attention(g):
                for m in range(NT + 2):
                    if m < NT:
                        act.wait_ge(kv_turned, NT * g + m + 1)
                        nc.scalar.activation(k.kT[0:64, m * TP:(m + 1) * TP], k.MI[0:64, 0:TP], ACT.Copy)\
                            .then_inc(kv_ready, 1)
                    att.scalar(act, g, m)

            choose(0)
            with act.Fori(0, G - 1) as g:
                choose(g + 1)
                attention(g)
            attention(G - 1)

        @block.vector
        def _(dve):
            sc = k.sc[:, :].rearrange("p (t a n) -> p t a n", t=NT, a=2)
            ix = k.ix[:, :].rearrange("p (t a n) -> p t a n", t=NT, a=2)
            ixf = k.ixf[:, :].rearrange("p (t a n) -> p t a n", t=NT, a=2)
            cand = k.cand[:, :].rearrange("p (t n) -> p t n", t=NT)
            cidx = k.cidx[:, :].rearrange("p (t n) -> p t n", t=NT)

            def pairs(dst, src):
                at = 0
                for i0, ni, nj in RUNS:
                    for t0 in range(0, NT, 1 if ni > 1 and nj > 1 else NT):
                        ts = slice(t0, t0 + 1) if ni > 1 and nj > 1 else slice(0, NT)
                        d = dst[:, ts, at:at + ni * nj]
                        a, b = src[:, ts, 0, i0:i0 + ni], src[:, ts, 1, 0:nj]
                        if ni > 1 and nj > 1:
                            d = dst[:, t0, at:at + ni * nj].rearrange("p (i j) -> p i j", j=nj)
                            a = src[:, t0, 0, i0:i0 + ni].unsqueeze(2).to_broadcast([TP, ni, nj])
                            b = src[:, t0, 1, 0:nj].unsqueeze(1).to_broadcast([TP, ni, nj])
                        elif ni == 1:
                            a = a.to_broadcast([TP, NT, nj])
                        else:
                            b = b.to_broadcast([TP, NT, ni])
                        nc.vector.tensor_tensor(d, a, b, ALU.add)
                    at += ni * nj

            def choose(g, h):
                nc.vector.tensor_copy(k.head[:, :], k.heads[:, bass.ds(h, 1)])
                dve.wait_ge(sims_ready, 2 * g + 2)
                nc.vector.tensor_copy(k.gate[:, :], k.ones[0:TP, 0:1])
                both = [(t, a) for t in range(NT) for a in range(2)]
                for t, a in both:
                    nc.vector.max(sc[:, t, a, 0:8], k.sims[:, t, a * 64:(a + 1) * 64])
                dve.drain()
                for t, a in both:
                    s = k.sims[:, t, a * 64:(a + 1) * 64]
                    nc.vector.max_index(ix[:, t, a, 0:8], sc[:, t, a, 0:8], s)
                    nc.vector.match_replace(k.sims2[:, t, a * 64:(a + 1) * 64], sc[:, t, a, 0:8], s, NEG)
                dve.drain()
                for t, a in both:
                    nc.vector.max(sc[:, t, a, 8:16], k.sims2[:, t, a * 64:(a + 1) * 64])
                dve.drain()
                for t, a in both:
                    nc.vector.max_index(ix[:, t, a, 8:16], sc[:, t, a, 8:16], k.sims2[:, t, a * 64:(a + 1) * 64])
                dve.drain()
                nc.vector.tensor_copy(k.ixf[:, :], k.ix[:, :])
                dve.drain()
                nc.vector.tensor_scalar(ixf[:, :, 1, :], ixf[:, :, 1, :], float(PKEYS), None, ALU.mult)
                nc.vector.tensor_scalar(ixf[:, :, 0, :], ixf[:, :, 0, :], k.head[:, 0:1], None, ALU.add)
                pairs(cand, sc)
                dve.drain()
                pairs(cidx, ixf)
                for t in range(NT):
                    nc.vector.max(k.top[:, t, 0:8], cand[:, t, :])
                dve.drain()
                for t in range(NT):
                    nc.vector.max_index(k.pos[:, t, 0:8], k.top[:, t, 0:8], cand[:, t, :])
                    nc.vector.match_replace(k.cand2[:, t, :], k.top[:, t, 0:8], cand[:, t, :], NEG)
                dve.drain()
                for t in range(NT):
                    nc.vector.max(k.top[:, t, 8:16], k.cand2[:, t, :])
                dve.drain()
                for t in range(NT):
                    nc.vector.max_index(k.pos[:, t, 8:16], k.top[:, t, 8:16], k.cand2[:, t, :])
                nc.vector.tensor_tensor(tiles(k.top_v, TOPK), k.top[:, :, :], k.top[:, :, 0:1].to_broadcast([TP, NT, TOPK]),
                                        ALU.subtract).then_inc(top_exp_in, 1)
                dve.drain()
                nc.vector.tensor_copy(k.posf[:, :], k.pos[:, :, :].rearrange("p t n -> p (t n)"))
                dve.drain()
                for t in range(NT):
                    hot = k.hot[:, t * TOPK * NC_:(t + 1) * TOPK * NC_].rearrange("p (j c) -> p j c", c=NC_)
                    nc.vector.tensor_tensor(hot, bcast(k.posf[:, t * TOPK:(t + 1) * TOPK], NC_),
                                            k.place[:, :].unsqueeze(1).to_broadcast([TP, TOPK, NC_]), ALU.is_equal)
                dve.drain()
                for t in range(NT):
                    hot = k.hot[:, t * TOPK * NC_:(t + 1) * TOPK * NC_].rearrange("p (j c) -> p j c", c=NC_)
                    nc.vector.tensor_tensor(hot, hot, cidx[:, t:t + 1, :].to_broadcast([TP, TOPK, NC_]), ALU.mult)
                dve.drain()
                nc.vector.reduce_sum(k.idxf[:, :], k.hot[:, :].rearrange("p (j c) -> p j c", c=NC_), AXX)
                dve.drain()
                dve.wait_ge(top_exp, g + 1)
                nc.vector.reduce_sum(k.wsum[:, :], tiles(k.top_e, TOPK), AXX)
                dve.drain()
                nc.vector.reciprocal(k.wsum[:, :], k.wsum[:, :])
                dve.drain()
                nc.vector.tensor_tensor(tiles(k.w_next, TOPK), tiles(k.top_e, TOPK), bcast(k.wsum[:, :], TOPK), ALU.mult)
                dve.drain()

            def take_over(t):
                s = slice(t * TOPK, (t + 1) * TOPK)
                nc.vector.tensor_copy(k.w[:, s], k.w_next[:, s])
                nc.vector.tensor_copy(k.idx[:, s], k.idxf[:, s]).then_inc(chosen, 1)

            def attention(g, more):
                for m in range(NT + 2):
                    if m < NT:
                        dve.wait_ge(gathered[m], 16 * TOPK * (g + 1))
                        prod = k.prod[:, :].rearrange("p (j c) -> p j c", c=128)
                        nc.vector.tensor_tensor(prod, k.rows[m][:, :].rearrange("p (j c) -> p j c", c=128),
                                                bcast(k.w[:, m * TOPK:(m + 1) * TOPK], 128), ALU.mult)
                        dve.drain()
                        if more:
                            take_over(m)
                        nc.vector.reduce_sum(k.kv[:, m * 128:(m + 1) * 128], prod.rearrange("p j c -> p c j"), AXX)\
                            .then_inc(taken, 1)
                        dve.drain()
                    att.vector(dve, g, m)
                inverse_sums(nc, dve, k, 0, NT, True)
                dve.wait_ge(att.out_ready, NT * g + NT)
                nc.vector.tensor_tensor(tiles(k.tmp), tiles(k.PV[0:TP, 0:384]), bcast(k.rinv[:, 0:NT], D), ALU.mult)
                dve.drain()
                dve.wait_ge(acc_loaded, 16 * g + 16)
                nc.vector.tensor_tensor(k.h4[:, :], k.h4[:, :], k.tmp[:, :], ALU.add).then_inc(acc_ready, 1)
                dve.drain()

            for h in range(PH):
                nc.vector.memset(k.heads[:, h:h + 1], float(h * PKEYS * PKEYS))
            dve.drain()
            choose(0, 0)
            for t in range(NT):
                take_over(t)
            dve.drain()
            with dve.Fori(0, G - 1) as g:
                choose(g + 1, (g + 1) & 7)
                attention(g, True)
            attention(G - 1, False)



class Shared:
    pass


def build(nc, A, out):
    ctx = ExitStack()
    with ctx:
        def sb(name, shape, dt=FP):
            return ctx.enter_context(nc.sbuf_tensor(name, shape, dt))

        def sem(name):
            return ctx.enter_context(nc.semaphore(name))

        def eb(name, shape, dt=FP):
            return early.enter_context(nc.sbuf_tensor(name, shape, dt))

        k = Shared()
        ps = [ctx.enter_context(nc.psum_tensor(f"bank_pair_{i}", [128, 2, 512], FP)) for i in range(3)]
        k.S, k.T = ps[0:2], ps[2]
        k.S2 = ps[1]
        k.PV = ctx.enter_context(nc.psum_tensor("PV", [128, 512], FP))
        k.MI = ctx.enter_context(nc.psum_tensor("MI", [128, 512], FP))
        k.ident = sb("ident", [128, 128])
        k.ident_bf = sb("ident_bf", [128, 128], BF)
        k.causal = sb("causal", [TP, TP], BF)
        k.ones = sb("ones", [128, 128])
        k.minus_half = sb("minus_half", [128, 1])
        k.plus_half = sb("plus_half", [128, 1])
        k.place_i = sb("place_i", [TP, NC_], mybir.dt.int32)
        k.place = sb("place", [TP, NC_])
        k.WX = sb("WX", [128, 128])
        k.R3 = sb("R3", [128, 64])
        k.W2BD = sb("W2BD", [128, 128])
        k.W4 = sb("W4", [128, 64])
        k.WqN = sb("WqN", [64, 64])
        k.WkN = sb("WkN", [64, 64])
        k.WvT = sb("WvT", [128, 64])
        k.ATT0 = sb("ATT0", [128, 64])
        k.HLP = sb("HLP", [128, 128])
        k.HLT = sb("HLT", [128, 64])
        k.WVB = sb("WVB", [128, 64])
        k.wqb = sb("wqb", [128, NE, 128])
        k.wkb = sb("wkb", [128, 128])
        k.LB = sb("LB", [128, NE, 128])
        k.GW = sb("GW", [128, 2, 16])
        k.GB = sb("GB", [1, 16])
        k.FG = sb("FG", [128, 4])
        k.LNG = sb("LNG", [TP, 16])
        k.LNB = sb("LNB", [TP, 16])
        k.FNG = sb("FNG", [TP, 16])
        k.FNB = sb("FNB", [TP, 16])
        k.FC1 = sb("FC1", [128, 64])
        k.FC2 = sb("FC2", [128, 64])
        k.R2 = sb("R2", [128, 194])
        k.WB = sb("WB", [128, 128])
        k.NW = sb("NW", [128, 128])
        k.W1Tr = sb("W1Tr", [128, 64])
        k.WkT1 = sb("WkT1", [64, 64])
        k.WqT1 = sb("WqT1", [64, 64])
        k.R4 = sb("R4", [128, 128])
        k.grads = sb("grads", [65, 128])
        k.gsq = sb("gsq", [65, 128])
        k.gabs = sb("gabs", [65, 128])
        k.WPK = sb("WPK", [32, 1024])
        k.KPK = sb("KPK", [32, 1024])
        k.Mk = sb("Mk", [128, 1024])
        k.BD = sb("BD", [128, PH, 128])
        k.xT = sb("xT", [128, L])
        k.xT2 = sb("xT2", [128, L])
        k.xT3 = sb("xT3", [128, L])
        k.kT = sb("kT", [128, L])
        k.h1 = sb("h1", [TP, NT * D])
        k.h2 = sb("h2", [TP, NT * D])
        k.h3 = sb("h3", [TP, NT * D])
        k.h4 = sb("h4", [TP, NT * D])
        k.xn = sb("xn", [TP, NT * D])
        k.tmp = sb("tmp", [TP, NT * D])
        k.V = sb("V", [TP, NT * D])
        k.mix = sb("mix", [TP, NT * D])
        k.fx = sb("fx", [TP, NT * D])
        k.hx = sb("hx", [TP, NT * D])
        k.fout = sb("fout", [TP, NT * D])
        k.live = sb("live", [TP, NT * D])
        k.resid = sb("resid", [TP, NT * D])
        k.silu = sb("silu", [TP, NT * D])
        k.d0 = sb("d0", [TP, NT * D])
        k.dx = sb("dx", [TP, NT * D])
        k.dz0 = sb("dz0", [TP, NT * D])
        k.dz1 = sb("dz1", [TP, NT * D])
        k.E1 = sb("E1", [TP, NT * D])
        k.q1 = sb("q1", [TP, NT * D])
        k.ln_dev = sb("ln_dev", [TP, NT * D])
        k.ln_sq = sb("ln_sq", [TP, NT * D])
        k.ln_mean = sb("ln_mean", [TP, 24])
        k.ln_var = sb("ln_var", [TP, 24])
        k.ln_rstd = sb("ln_rstd", [TP, 24])
        k.P0 = sb("P0", [TP, L])
        k.P1 = sb("P1", [TP, L])
        k.PT0 = sb("PT0", [TP, L])
        k.PT1 = sb("PT1", [TP, L])
        k.P, k.PT = [k.P0, k.P1], [k.PT0, k.PT1]
        k.nmax = sb("nmax", [TP, 96])
        k.mtmp = sb("mtmp", [TP, 192])
        k.rsum = sb("rsum", [TP, 96])
        k.rsum2 = sb("rsum2", [TP, 96])
        k.rinv = sb("rinv", [TP, 96])
        k.table = nc.dram_tensor("table", [ROWS, 128], FP).ap()
        k.d_h2 = nc.dram_tensor("d_h2", [B, TP, NT * D], FP).ap()
        k.d_h3 = nc.dram_tensor("d_h3", [B, TP, NT * D], FP).ap()
        k.d_xT2 = nc.dram_tensor("d_xT2", [B, D, L], FP).ap()
        k.d_xT3 = nc.dram_tensor("d_xT3", [B, D, L], FP).ap()
        k.d_xT4 = nc.dram_tensor("d_xT4", [B, D, L], FP).ap()

        early = ctx.enter_context(ExitStack())
        k.xs = eb("xs", [128, L])
        k.U0 = eb("U0", [128, L + 2])
        k.U1 = eb("U1", [128, L + 2])
        k.UR = eb("UR", [128, L + 2])
        k.U = [k.U0, k.U1]
        k.live_sx = eb("live_sx", [TP, NT * D])
        k.sxT = eb("sxT", [128, L])
        k.UT = eb("UT", [128, NE, L])
        k.sxn = eb("sxn", [128, NH, L])
        k.Vp = eb("Vp", [TP, NT, NH, 128])
        room = [eb(f"rows_or_probabilities_{i}", [128, 3 * 1024]) for i in range(2)]
        k.rows_in = [r[:, 0:1024].rearrange("p (j d) -> p j d", j=8) for r in room]
        k.rows_turned, k.rows_out = [r[:, 1024:2048] for r in room], [r[:, 2048:3072] for r in room]
        k.PG = [r[0:TP, 0:NE * L] for r in room]
        k.PTG = [eb(f"PTG{i}", [TP, NE * TP]) for i in range(2)]
        k.outT = eb("outT", [128, NE * TP])
        k.att = eb("att", [TP, NT, 256])
        k.big = eb("big", [TP, 1536])
        k.logits = eb("logits", [TP, 96])
        k.soft = eb("soft", [TP, 96])
        k.soft_exp = eb("soft_exp", [TP, 96])
        k.soft_m = eb("soft_m", [TP, 24])
        k.G = eb("G", [TP, NT, 194])
        k.E0 = eb("E0", [TP, NT, 65])
        k.x1 = eb("x1", [TP, NT, 65])
        k.alr = eb("alr", [TP, NT])

        for e in (nc.tensor, nc.gpsimd, nc.sync):
            PASSED[e.engine] = sem("waits_passed_" + str(e.engine).split(".")[-1])
        clear(nc, k)
        load_weights(nc, k, A, sem)
        weight_products(nc, k, sem)
        build_table(nc, k, A, sem)
        tok_and_attention(nc, k, A, sem)
        residuals(nc, k, A, sem)
        ffn_and_gradients(nc, k, A, sem)
        adamw(nc, k, sem)
        retrieve(nc, k, A, out, sem)
        early.close()
        k.sims = sb("sims", [TP, NT, 128])
        k.sims2 = sb("sims2", [TP, NT, 128])
        k.sc = sb("sc", [TP, NT * 32])
        k.ix = sb("ix", [TP, NT * 32], U32)
        k.ixf = sb("ixf", [TP, NT * 32])
        k.cand = sb("cand", [TP, NT * NC_])
        k.cidx = sb("cidx", [TP, NT * NC_])
        k.cand2 = sb("cand2", [TP, NT, NC_])
        k.top = sb("top", [TP, NT, TOPK])
        k.pos = sb("pos", [TP, NT, TOPK], U32)
        k.posf = sb("posf", [TP, NT * TOPK])
        k.top_v = sb("top_v", [TP, NT * TOPK])
        k.top_e = sb("top_e", [TP, NT * TOPK])
        k.hot = sb("hot", [TP, NT * TOPK * NC_])
        k.idxf = sb("idxf", [TP, NT * TOPK])
        k.wsum = sb("wsum", [TP, NT])
        k.w_next = sb("w_next", [TP, NT * TOPK])
        k.w = sb("w", [TP, NT * TOPK])
        k.idx = sb("idx", [TP, NT * TOPK], U32)
        k.gate = sb("gate", [TP, 1])
        k.heads = sb("heads", [TP, PH])
        k.head = sb("head", [TP, 1])
        k.prod = sb("prod", [TP, TOPK * 128])
        k.kv = sb("kv", [TP, NT * 128])
        k.rows = [sb(f"rows_{t}", [TP, TOPK * 128]) for t in range(NT)]
        product_key_attention(nc, k, out, sem)


def host_arrays(i):
    import numpy as np
    c = np.ascontiguousarray
    i = {n: np.asarray(v) for n, v in i.items()}
    f = {
        "x": c(i["x"]), "xr": c(i["x"][:, :, ::-1]),
        "W1T": c(i["L0_tok_W1"].T), "W2T": c(i["L0_tok_W2"].T), "W3T": c(i["L0_tok_W3"].T), "W4T": c(i["L0_tok_W4"].T),
        "b1": i["L0_tok_b1"][None], "b2": i["L0_tok_b2"][None], "b3": i["L0_tok_b3"][None], "b4": i["L0_tok_b4"][None],
        "attn_Wq": c(i["L0_attn_Wq"]), "attn_Wk": c(i["L0_attn_Wk"]), "attn_WvT": c(i["L0_attn_Wv"].T),
        "hlT": c(i["L0_ffn_hl_w"].reshape(64, 64).T), "hl_b": c(i["L0_ffn_hl_b"].reshape(1, 64)),
        "gwT": c(i["L0_ffn_gate_w"].transpose(0, 2, 1)), "gb": c(i["L0_ffn_gate_b"].reshape(1, 16)),
        "fgT": c(i["L0_ffn_fgate_w"].T), "wvT": c(i["L0_ffn_wv"].transpose(0, 2, 1)),
        "wq": c(i["L0_ffn_wq"]), "wk": c(i["L0_ffn_wk"]),
        "fc1T": c(i["L0_ffn_fc1_w"].T), "fc2T": c(i["L0_ffn_fc2_w"].T),
        "fc1_b": i["L0_ffn_fc1_b"][None], "fc2_b": i["L0_ffn_fc2_b"][None],
        "ln_g": i["L0_ffn_ln_g"][None], "ln_b": i["L0_ffn_ln_b"][None],
        "fn_g": i["L0_ffn_fnorm_g"][None], "fn_b": i["L0_ffn_fnorm_b"][None],
        "Wk1": c(i["L1_attn_Wk"]), "Wv1": c(i["L1_attn_Wv"]), "Wlr": c(i["L1_attn_Wlr"]), "Wq1": c(i["L1_attn_Wq"]),
        "blr": i["L1_attn_blr"][None], "Ws": c(i["L1_attn_Ws"]), "bs": c(i["L1_attn_bs"].reshape(1, 128)),
        "Ws1T": c(i["L1_attn_Ws"][1].T), "WkT1": c(i["L1_attn_Wk"].T), "WqT1": c(i["L1_attn_Wq"].T),
        "wpk": c(i["L1_ffn_Wq_pk"].reshape(64, 2, 8, 32).transpose(3, 1, 2, 0).reshape(32, 1024)),
        "kpk": c(i["L1_ffn_pk_keys"].transpose(3, 0, 2, 1).reshape(32, 1024)),
        "WqpT": c(i["L1_ffn_Wq"].T), "Wo": c(i["L1_ffn_Wo"]),
        "keys": c(i["L1_ffn_keys_table"]), "values": c(i["L1_ffn_values_table"]),
    }
    return {n: c(v) for n, v in f.items()}


def kernel(**inputs):
    import numpy as np
    import concourse.bacc as bacc
    from concourse.bass_utils import run_bass_kernel_spmd

    nc = bacc.Bacc("TRN2", target_bir_lowering=False, num_devices=1)
    arrays = host_arrays(inputs)
    aps = {n: nc.dram_tensor(f"in_{n}", a.shape, mybir.dt.from_np(a.dtype), kind="ExternalInput").ap()
           for n, a in arrays.items()}
    out = nc.dram_tensor("out_dram", (B, L, D), FP, kind="ExternalOutput").ap()
    build(nc, aps, out)
    r = run_bass_kernel_spmd(nc, [{f"in_{n}": a for n, a in arrays.items()}], core_ids=[0])
    return r.results[0]["out_dram"]
```
